# Optimizing a Trainium2 kernel written in Bass

```python
import numpy as np
import jax
import jax.numpy as jnp

def _softmax(x, axis=-1):
    return jax.nn.softmax(x, axis=axis)

def _gelu(x):
    return jax.nn.gelu(x, approximate=True)

def _silu(x):
    return jax.nn.silu(x)

def _sigmoid(x):
    return jax.nn.sigmoid(x)

def _layernorm(x, axis=-1, eps=1e-05):
    m = jnp.mean(x, axis=axis, keepdims=True)
    v = jnp.var(x, axis=axis, keepdims=True)
    return (x - m) / jnp.sqrt(v + eps)

def _scatter_add(tgt, idx, src, axis=0):
    return tgt.at[idx].add(src)

def _segment_sum(src, seg, n):
    return jax.ops.segment_sum(src, seg, n)
kernel_name = 'mk_seq_postln_d1_jaxref_r4_83cfb6'

def setup_inputs(seed: int=0):
    np.random.seed(seed)
    _w = jnp.asarray

    def _L0_attn_setup():
        import jax, jax.numpy as jnp
        import numpy as np
        B, S, D, N = (16, 512, 256, 16)
        key = jax.random.key(seed)
        ks = jax.random.split(key, 8)
        sc = lambda d: 1.0 / np.sqrt(d)
        return {'x': jax.random.normal(ks[0], (B, S, D), jnp.float32), 'WA': jax.random.normal(ks[1], (N, D), jnp.float32) * sc(D), 'WB': jax.random.normal(ks[2], (N, D), jnp.float32) * sc(D), 'WC': jax.random.normal(ks[3], (D, N), jnp.float32) * sc(N), 'WD': jax.random.normal(ks[4], (D, D), jnp.float32) * sc(D), 'bD': jax.random.normal(ks[5], (D,), jnp.float32) * 0.01, 'Wg': jax.random.normal(ks[6], (D, D), jnp.float32) * sc(D), 'bg': jax.random.normal(ks[7], (D,), jnp.float32) * 0.01}
    _L0_attn_in = _L0_attn_setup()

    def _L0_ffn_setup():
        import jax, jax.numpy as jnp
        import numpy as np
        B, S, D, H, F = (4, 1024, 256, 16, 1024)
        CAP = 0.125
        ROPE_BASE = 10000.0

        def rmsnorm(x, g):
            return x * jax.lax.rsqrt(jnp.mean(x * x, -1, keepdims=True) + 1e-06) * g

        def rope(t, pos):
            hd = t.shape[-1]
            inv = 1.0 / ROPE_BASE ** (jnp.arange(0, hd, 2, dtype=jnp.float32) / hd)
            f = pos[:, None, :, None].astype(jnp.float32) * inv
            emb = jnp.concatenate([f, f], axis=-1)
            cos, sin = (jnp.cos(emb), jnp.sin(emb))
            rot = jnp.concatenate([-t[..., hd // 2:], t[..., :hd // 2]], axis=-1)
            return t * cos + rot * sin
        key = jax.random.key(seed)
        ks = jax.random.split(key, 9)
        scale = 0.02
        x = jax.random.normal(ks[0], (B, S, D), jnp.float32)
        causal = jnp.where(jnp.tril(jnp.ones((S, S), bool)), 0.0, -1000000000.0).astype(jnp.float32)
        attention_mask = jnp.broadcast_to(causal[None, None], (B, 1, S, S))
        position_ids = jnp.broadcast_to(jnp.arange(S, dtype=jnp.int32), (B, S))
        return {'x': x, 'attention_mask': attention_mask, 'position_ids': position_ids, 'router_w': jax.random.normal(ks[1], (D, 1), jnp.float32) * scale, 'router_b': jnp.zeros((1,), jnp.float32), 'wq': jax.random.normal(ks[2], (D, D), jnp.float32) * scale, 'wk': jax.random.normal(ks[3], (D, D), jnp.float32) * scale, 'wv': jax.random.normal(ks[4], (D, D), jnp.float32) * scale, 'wo': jax.random.normal(ks[5], (D, D), jnp.float32) * scale, 'w1': jax.random.normal(ks[6], (D, F), jnp.float32) * scale, 'w2': jax.random.normal(ks[7], (F, D), jnp.float32) * scale, 'ln1': jnp.ones((D,), jnp.float32), 'ln2': jnp.ones((D,), jnp.float32)}
    _L0_ffn_in = _L0_ffn_setup()
    _d = {'L0_attn_x': _L0_attn_in['x'], 'L0_attn_WA': _L0_attn_in['WA'], 'L0_attn_WB': _L0_attn_in['WB'], 'L0_attn_WC': _L0_attn_in['WC'], 'L0_attn_WD': _L0_attn_in['WD'], 'L0_attn_bD': _L0_attn_in['bD'], 'L0_attn_Wg': _L0_attn_in['Wg'], 'L0_attn_bg': _L0_attn_in['bg'], 'L0_ffn_attention_mask': _L0_ffn_in['attention_mask'], 'L0_ffn_position_ids': _L0_ffn_in['position_ids'], 'L0_ffn_router_w': _L0_ffn_in['router_w'], 'L0_ffn_router_b': _L0_ffn_in['router_b'], 'L0_ffn_wq': _L0_ffn_in['wq'], 'L0_ffn_wk': _L0_ffn_in['wk'], 'L0_ffn_wv': _L0_ffn_in['wv'], 'L0_ffn_wo': _L0_ffn_in['wo'], 'L0_ffn_w1': _L0_ffn_in['w1'], 'L0_ffn_w2': _L0_ffn_in['w2'], 'L0_ffn_ln1': _L0_ffn_in['ln1'], 'L0_ffn_ln2': _L0_ffn_in['ln2']}
    _x0 = _d['L0_attn_x']
    _d['L0_attn_x'] = jax.random.normal(jax.random.fold_in(jax.random.key(seed), 1), (2, 4096, 256), dtype=_x0.dtype)
    del _x0
    return _d

def reference(L0_attn_x, L0_attn_WA, L0_attn_WB, L0_attn_WC, L0_attn_WD, L0_attn_bD, L0_attn_Wg, L0_attn_bg, L0_ffn_attention_mask, L0_ffn_position_ids, L0_ffn_router_w, L0_ffn_router_b, L0_ffn_wq, L0_ffn_wk, L0_ffn_wv, L0_ffn_wo, L0_ffn_w1, L0_ffn_w2, L0_ffn_ln1, L0_ffn_ln2):

    def _L0_attn_ref(x, WA, WB, WC, WD, bD, Wg, bg):
        import jax, jax.numpy as jnp
        import numpy as np
        B, S, D, N = (16, 512, 256, 16)
        a = jnp.tanh(jnp.einsum('bsd,nd->bsn', x, WA))
        b = jnp.einsum('bsd,nd->bsn', x, WB)
        g = jax.nn.sigmoid(jnp.einsum('bsd,ed->bse', x, Wg) + bg)
        dx = jnp.einsum('bsd,ed->bse', x, WD) + bD

        def step(h, ab):
            a_t, b_t = ab
            h = a_t * h + b_t
            return (h, h)
        h0 = jnp.zeros((x.shape[0], WA.shape[0]), x.dtype)
        _, hs = jax.lax.scan(step, h0, (jnp.swapaxes(a, 0, 1), jnp.swapaxes(b, 0, 1)))
        hs = jnp.swapaxes(hs, 0, 1)
        y = jnp.einsum('bsn,en->bse', hs, WC) * g + dx * (1.0 - g)
        return y

    def _L0_ffn_ref(x, attention_mask, position_ids, router_w, router_b, wq, wk, wv, wo, w1, w2, ln1, ln2):
        import jax, jax.numpy as jnp
        import numpy as np
        B, S, D, H, F = (4, 1024, 256, 16, 1024)
        CAP = 0.125
        ROPE_BASE = 10000.0

        def rmsnorm(x, g):
            return x * jax.lax.rsqrt(jnp.mean(x * x, -1, keepdims=True) + 1e-06) * g

        def rope(t, pos):
            hd = t.shape[-1]
            inv = 1.0 / ROPE_BASE ** (jnp.arange(0, hd, 2, dtype=jnp.float32) / hd)
            f = pos[:, None, :, None].astype(jnp.float32) * inv
            emb = jnp.concatenate([f, f], axis=-1)
            cos, sin = (jnp.cos(emb), jnp.sin(emb))
            rot = jnp.concatenate([-t[..., hd // 2:], t[..., :hd // 2]], axis=-1)
            return t * cos + rot * sin
        b, s, d = x.shape
        hd = d // H
        weights = (x @ router_w)[..., 0] + router_b[0]
        k = int(CAP * s)
        topv, topi = jax.lax.top_k(weights, k)
        thr = topv[:, -1]
        sel_mask = (weights > thr[:, None]).astype(x.dtype)
        kc = k - 1
        sel_idx = jnp.sort(topi[:, :kc], axis=1)
        bidx = jnp.arange(b)[:, None]
        x_sel = x[bidx, sel_idx]
        pos_sel = position_ids[bidx, sel_idx]
        w_sel = weights[bidx, sel_idx]
        m = attention_mask[:, 0]
        m_sel = m[bidx[:, :, None], sel_idx[:, :, None], sel_idx[:, None, :]]
        hn = rmsnorm(x_sel, ln1)

        def heads(t):
            return t.reshape(b, kc, H, hd).transpose(0, 2, 1, 3)
        q = rope(heads(hn @ wq), pos_sel)
        kk = rope(heads(hn @ wk), pos_sel)
        v = heads(hn @ wv)
        sc = jnp.einsum('bhqd,bhkd->bhqk', q, kk) / np.sqrt(hd).astype(np.float32)
        sc = sc + m_sel[:, None]
        a = jax.nn.softmax(sc, axis=-1)
        o = jnp.einsum('bhqk,bhkd->bhqd', a, v).transpose(0, 2, 1, 3).reshape(b, kc, d) @ wo
        x1 = x_sel + o
        x2 = x1 + jax.nn.gelu(rmsnorm(x1, ln2) @ w1) @ w2
        proc = x2 * w_sel[..., None]
        out = jnp.zeros_like(x).at[bidx, sel_idx].set(proc)
        return out + x * (1.0 - sel_mask)[..., None]
    x = L0_attn_x
    x = _layernorm(x + _L0_attn_ref(x, L0_attn_WA, L0_attn_WB, L0_attn_WC, L0_attn_WD, L0_attn_bD, L0_attn_Wg, L0_attn_bg), axis=-1)
    x = _layernorm(x + _L0_ffn_ref(x, L0_ffn_attention_mask, L0_ffn_position_ids, L0_ffn_router_w, L0_ffn_router_b, L0_ffn_wq, L0_ffn_wk, L0_ffn_wv, L0_ffn_wo, L0_ffn_w1, L0_ffn_w2, L0_ffn_ln1, L0_ffn_ln2), axis=-1)
    return x

_drawn_inputs = setup_inputs


def setup_inputs(seed=0):
    import zlib

    import numpy as np

    out = dict(_drawn_inputs(seed))
    spreads = {'L0_ffn_ln1': (1.0, 0.6), 'L0_ffn_ln2': (1.0, 0.6)}
    factors = {'L0_attn_bD': 8.0,
     'L0_attn_bg': 8.0,
     'L0_ffn_router_w': 4.21,
     'L0_ffn_wq': 8.0,
     'L0_ffn_wk': 8.0,
     'L0_ffn_wv': 8.0,
     'L0_ffn_wo': 8.0,
     'L0_ffn_w1': 4.054,
     'L0_ffn_w2': 3.944}
    for name, (base, spread) in spreads.items():
        noise = np.random.default_rng([zlib.crc32(name.encode()), seed]).standard_normal(out[name].shape)
        drawn = base * np.exp(spread * noise) if base else spread * noise
        out[name] = jnp.asarray(drawn.astype(out[name].dtype))
    for name, factor in factors.items():
        out[name] = (out[name] * factor).astype(out[name].dtype)
    return out
```

```python
from contextlib import ExitStack

import numpy as np

import concourse.bass as bass
from concourse import mybir

ALU = mybir.AluOpType
ACT = mybir.ActivationFunctionType
F32 = mybir.dt.float32
BF16 = mybir.dt.bfloat16
I32 = mybir.dt.int32
X = mybir.AxisListType.X

P = 128
B, S, D = 2, 4096, 256
N = 16
F = 1024
H, HD = 16, 16
KD = D // P
T = 4
GT = T * P
NG = S // GT
U = 4
LOOPS = NG // U
BROW = 32
K = S // 8
MS = 1024
C = K // P
LN_EPS = 1e-5
RMS_EPS = 1e-6
ROPE_BASE = 10000.0
DIGIT = 4
CAND = 2 ** DIGIT - 1
ROUNDS = 32 // DIGIT
VALS = 6
SLOTS = 6
ER = SLOTS * HD
HG = 4
HP = 32
FB = F // P
SIGN = -2 ** 31
MAGIC = 1.5 * 2.0 ** 23
PI2_A = 6.28125
PI2_B = float(np.float32(2 * np.pi - PI2_A).view(np.uint32).__and__(np.uint32(0xFFFFF000)).view(np.float32))
PI2_C = float(2 * np.pi - PI2_A - PI2_B)
PI_MAX = float(np.nextafter(np.float32(np.pi), np.float32(0)))
INV_FREQ = [float(v) for v in np.float32(1.0) / np.power(np.float32(ROPE_BASE), np.arange(0, HD, 2, dtype=np.float32) / np.float32(HD))]


def before(turn, u, j):
    return turn * (U // 2) + (u + 1 - j) // 2


class Steps:

    def __init__(self, eng, sem):
        self.eng, self.sem, self.base, self.k, self.reg, self.per = eng, sem, 0, 0, None, 0

    def value(self):
        at = self.base + self.k
        return at if self.reg is None else self.reg * self.per + at

    def done(self, ins):
        self.k += 1
        ins.then_inc(self.sem, 1)
        return self.value()

    def link(self, ins):
        self.eng.wait_ge(self.sem, self.done(ins))

    def enter(self, reg, per):
        self.base, self.k, self.reg, self.per = self.base + self.k, 0, reg, per

    def leave(self, trips):
        assert self.k == self.per, (self.k, self.per)
        self.base, self.k, self.reg = self.base + trips * self.per, 0, None


def build(nc, x_in, WA, WB, WC, WD, bD, Wg, bg, mask_in, pos_in, router_w, router_b,
          wq, wk, wv, wo, w1, w2, ln1, ln2, out):
    with ExitStack() as ctx:
        def sb(name, shape, dt=F32):
            return ctx.enter_context(nc.sbuf_tensor(name, shape, dt))

        def sem(name):
            return ctx.enter_context(nc.semaphore(name))

        def sems(name, n=2):
            return [sem(f"{name}{i}") for i in range(n)]

        mt_dram = [nc.dram_tensor(f"mt_scratch{b}", (MS, K), F32, kind="Internal").ap() for b in range(B)]
        x1_dram = nc.dram_tensor("x1_scratch", (B * S, D), F32, kind="Internal").ap()

        ps = ctx.enter_context(nc.psum_tensor("ps", [P, 8, 512], F32))

        ident = sb("ident", [P, P])
        nmask = [sb(f"nmask{b}", [P, C, K]) for b in range(B)]
        early = [m[:, :, :].rearrange("p c k -> p (c k)") for m in nmask]
        wraw = early[1][:, 0:4 * D].rearrange("p (m h d) -> p m h d", m=2, h=2)
        wab_raw = early[1][0:N, 4 * D:6 * D].rearrange("p (m d) -> p m d", m=2)
        wc_raw = early[1][:, 6 * D:6 * D + 2 * N].rearrange("p (h n) -> p h n", h=2)
        wgdT = sb("wgdT", [P, KD, 2 * D])
        wabT = sb("wabT", [P, KD, BROW + N])
        wcT = sb("wcT", [N, D])
        bias_row = early[0][0:3, 0:2 * D]
        bias_rest = early[0][0:3, 2 * D:4 * D]
        bias_h, bias_m, bias_l = (early[0][0:3, 4 * D + n * D:5 * D + n * D].bitcast(BF16) for n in range(3))
        bias3 = sb("bias3", [3, 2 * D], BF16)
        ones3 = sb("ones3", [3, P], BF16)
        rw_row = sb("rw_row", [P, D])
        rb_col = sb("rb_col", [P, 1])
        minus_half = sb("minus_half", [P, T])

        arena = sb("arena", [P, (U + 4) * T * D])
        x_sb = [arena[:, u * T * D:(u + 1) * T * D].rearrange("p (t d) -> p t d", t=T) for u in range(U)]
        xT = [arena[:, (U + j) * T * D:(U + j + 1) * T * D].rearrange("p (k n) -> p k n", k=KD) for j in range(2)]
        s_sb = [arena[:, (U + 2 + j) * T * D:(U + 3 + j) * T * D].rearrange("p (t d) -> p t d", t=T) for j in range(2)]
        arena2 = sb("arena2", [P, 9216])
        a_sb, b_sb, h_sb = ([arena2[0:N, 4096 + (2 * n + j) * GT:4096 + (2 * n + j + 1) * GT] for j in range(2)]
                            for n in range(3))
        g_sb, rec_g, dx_g, mix = ([arena2[:, (2 * n + q) * 2 * D:(2 * n + q + 1) * 2 * D].rearrange(
            "p (t d) -> p t d", t=2) for q in range(2)] for n in range(4))
        x1_sb = [sb(f"x1_sb{j}", [P, T, D]) for j in range(2)]
        ob_sb = [sb(f"ob_sb{j}", [P, T, D]) for j in range(2)]
        stats = [sb(f"stats{j}", [P, T, 6]) for j in range(2)]
        mv = [sb(f"mv{j}", [P, T, 2]) for j in range(2)]
        small = [sb(f"small{j}", [P, 8, T]) for j in range(2)]
        junk = arena2[:, 7168:9216].rearrange("p (j t d) -> p j t d", j=2, t=T)
        logit = [sb(f"logit{j}", [P, T]) for j in range(2)]
        W = sb("W", [P, B, NG, T])

        ident_b = sb("ident_b", [P, P], BF16)
        ones_b = sb("ones_b", [P, P], BF16)
        below_b = sb("below_b", [P, P], BF16)
        digit_i = sb("digit_i", [P, CAND], I32)
        digits = sb("digits", [P, ROUNDS, CAND], I32)
        hi_i = sb("hi_i", [P, P], I32)
        hi_row = sb("hi_row", [P, P], BF16)
        lo_i = sb("lo_i", [P, C], I32)
        lo_row = sb("lo_row", [P, C])
        pgt = sb("pgt", [P, 3, NG, T], I32)
        vals = sb("vals", [P, B, NG * T, VALS], BF16)
        prefix = sb("prefix", [P, B, 1], I32)
        cand = sb("cand", [P, B, CAND], I32)
        cand_m = sb("cand_m", [P, B, CAND], I32)
        cand_f = sb("cand_f", [P, B, CAND], I32)
        geq = sb("geq", [P, B, CAND, NG * T], BF16)
        cnt = sb("cnt", [P, B * CAND], BF16)
        enough = sb("enough", [P, B, CAND])
        found = sb("found", [P, B], I32)
        thr = sb("thr", [P, B, 1], I32)
        flags = sb("flags", [P, 2, B, NG, T])
        fcnt = sb("fcnt", [P, 2, B, NG], BF16)
        ftot = sb("ftot", [P, 2, B, NG])
        fscan = sb("fscan", [P, 2, B, NG])
        zeros = sb("zeros", [P, NG])
        rank = sb("rank", [P, 2, B, NG, T])
        room = sb("room", [P, B, 1])
        sel = sb("sel", [P, 4, B, NG * T])
        slot_i = sb("slot_i", [P, 3, B, NG * T], I32)
        slot_f = sb("slot_f", [P, 2, B, NG * T])
        w_rest = sb("w_rest", [P, 2, B, NG * T])
        at_lo = sb("at_lo", [P, B, NG * T, C])
        lo_vals = sb("lo_vals", [P, B, NG * T, C, VALS], BF16)
        picked = sb("picked", [P, B, C, VALS])
        pick_f = sb("pick_f", [P, 4, B, C])
        w_sel = sb("w_sel", [P, B, C])
        not_m = sb("not_m", [P, B, C])
        row_x = sb("row_x", [P, B, C], I32)
        row_m = sb("row_m", [P, B, C], I32)
        row_t = sb("row_t", [P, B, C], I32)

        wqk = sb("wqk", [P, KD, 2 * D])
        wv_sb = sb("wv_sb", [P, KD, D])
        wo_pad = sb("wo_pad", [P, H // HG, D])
        w1_sb = sb("w1_sb", [P, KD, F])
        w2_sb = sb("w2_sb", [P, FB, D])
        ln_col = sb("ln_col", [P, 2, KD])
        inv_f = sb("inv_f", [P, HD // 2])
        x_sel, keep = x1_sb, ob_sb
        pos_i = sb("pos_i", [P, B, C], I32)
        pos_f = sb("pos_f", [P, B, C])
        trig = [sb(f"trig{b}", [P, 8, C, HD // 2]) for b in range(B)]
        big = sb("big", [P, C * MS])
        at_hi = big[:, :].bitcast(BF16).rearrange("p (b n h) -> p b n h", b=B, h=P)
        m_rows = big[:, :].rearrange("p (c s) -> p c s", c=C)
        m_k = big[:, 0:C * K].rearrange("p (c k) -> p c k", c=C)
        prT = [big[:, n * 2048:(n + 1) * 2048].rearrange("p (h c n) -> p h c n", h=HG, c=C) for n in range(2)]
        hidden_sb = big[:, :].rearrange("p (f n) -> p f n", f=FB)
        big2 = sb("big2", [P, MS // P // 2, K])
        ms = [sb(f"ms{b}", [P, 6, C]) for b in range(B)]
        hn = wgdT[:, :, :].rearrange("p k (h d) -> p (k h) d", h=2)
        hnT = sb("hnT", [P, KD, K])
        qk = sb("qk", [P, C, 2 * D])
        onT = sb("onT", [P, H // HG, K])
        rope_a = onT[:, 0:2, :]
        rope_b = arena2[:, 1024:2048].rearrange("p (c n) -> p c n", c=2)
        v_sb = [sb(f"v_sb{b}", [P, C, D]) for b in range(B)]
        e_rest = arena2[:, 4096:5120].rearrange("p (e n) -> p e n", e=2)
        e_sb = [arena2[:, 5120 + e * 1536:6656 + e * 1536].bitcast(BF16).rearrange(
            "p (m h s k) -> p m h s k", m=2, h=H, s=SLOTS) for e in range(2)]
        qkT = [arena[:, 4096 * m:4096 * (m + 1)].bitcast(BF16)[0:ER, 0:H * K].rearrange("r (h n) -> r h n", h=H)
               for m in range(2)]
        v_cur = arena2[:, 8704:9216].rearrange("p (c h w) -> p c h w", c=C, h=HG)
        sm = [arena2[:, n * K:(n + 1) * K] for n in range(2)]
        pr = [arena2[:, 2048 + n * K:2048 + (n + 1) * K] for n in range(4)]
        nmax = sb("nmax", [P, C, HG])
        rsum = sb("rsum", [P, C, HG])
        rinv = sb("rinv", [P, C, HG])
        rinv_w = sb("rinv_w", [P, C, HG, HP])
        oT = arena2[:, 8192:8704]
        stat2 = sb("stat2", [P, C, 6])
        mv2 = sb("mv2", [P, C, 2])

        w_loaded = sem("w_loaded")
        w2_loaded = sem("w2_loaded")
        zeroed = sem("zeroed")
        pool_const = sem("pool_const")
        cnt_ready = sem("cnt_ready")
        cnt_sum = sem("cnt_sum")
        fcnt_ready = sem("fcnt_ready")
        fcnt_sum = sem("fcnt_sum")
        at_ready = sems("at_ready")
        lo_ready = sem("lo_ready")
        picked_done = sem("picked_done")
        rows_ready = sem("rows_ready")
        x_sel_in = sems("x_sel_in")
        pos_in_s = sems("pos_in_s")
        m_rows_in = sems("m_rows_in")
        mT_done = sems("mT_done")
        mT_ready = sems("mT_ready")
        mT_stored = sems("mT_stored")
        m_k_in = sems("m_k_in")
        nm_done = sems("nm_done")
        nm_ready = sems("nm_ready")
        ms_ready = sems("ms_ready")
        rms_ready = sems("rms_ready")
        hn_ready = sems("hn_ready")
        hnT_done = sems("hnT_done")
        hnT_ready = sems("hnT_ready")
        qk_done = sems("qk_done")
        v_done = sems("v_done")
        qk_ready = sems("qk_ready")
        v_ready = sems("v_ready")
        angle_ready = sems("angle_ready")
        sin_ready = sems("sin_ready")
        trig_ready = sems("trig_ready")
        rope_ready = sems("rope_ready")
        e_parts = sem("e_parts")
        e_ready = sem("e_ready")
        eT_done = [sem(f"eT_done{n}") for n in range(4)]
        qT_ready = sem("qT_ready")
        kT_ready = sem("kT_ready")
        v_cur_ready = sem("v_cur_ready")
        s_done = sem("s_done")
        sm_ready = sems("sm_ready")
        pr_ready = sems("pr_ready", 4)
        prT_done = sems("prT_done", 4)
        prT_copied = sems("prT_copied")
        pv_done = sems("pv_done")
        rinv_ready = sem("rinv_ready")
        rT_done = sem("rT_done")
        oT_ready = sem("oT_ready")
        onT_ready = sem("onT_ready")
        wo_done = sems("wo_done")
        h1_done = sems("h1_done")
        gelu_ready = sems("gelu_ready")
        w2_done = sems("w2_done")
        ve2_ready = sems("ve2_ready")
        pow3_ready = sems("pow3_ready")
        fin_ready = sems("fin_ready")
        scattered = sem("scattered")
        ident_ready = sem("ident_ready")
        wt_done = sem("wt_done")
        wt_copied = sem("wt_copied")
        const_ready = sem("const_ready")
        x_loaded = sems("x_loaded", U)
        xT_done = sems("xT_done")
        xT_copied = sems("xT_copied")
        ab_done = sem("ab_done")
        a_ready = sems("a_ready")
        b_ready = sems("b_ready")
        h_ready = sems("h_ready")
        gd_done = sem("gd_done")
        rec_done = sem("rec_done")
        g_ready = sem("g_ready")
        rec_g_done = sem("rec_g_done")
        dx_g_done = sem("dx_g_done")
        mixed = sem("mixed")
        s_ready = sem("s_ready")
        ve_ready = sem("ve_ready")
        pow_ready = sem("pow_ready")
        v2_ready = sem("v2_ready")
        pow2_ready = sem("pow2_ready")
        W_ready = sem("W_ready")
        x1_ready = sem("x1_ready")
        ob_ready = sem("ob_ready")
        dve_step = sem("dve_step")
        x1_stored = [sems(f"x1_stored{b}_") for b in range(B)]
        ob_stored = [sems(f"ob_stored{b}_") for b in range(B)]

        x1_rows = x1_dram.rearrange("(n p t) d -> n p (t d)", p=P, t=T)
        out_rows = out.rearrange("b (g p t) d -> (b g) p (t d)", p=P, t=T)
        xin_rows = x_in.rearrange("b (g p t) d -> (b g) p (t d)", p=P, t=T)

        block = ctx.enter_context(nc.Block())

        @block.sync
        def _(sp):
            sp.dma_start(wraw[:, 0, :, :], Wg.rearrange("(h e) d -> e h d", e=P)).then_inc(w_loaded, 16)
            sp.dma_start(wraw[:, 1, :, :], WD.rearrange("(h e) d -> e h d", e=P)).then_inc(w_loaded, 16)
            sp.dma_start(wab_raw[:, 0, :], WA).then_inc(w_loaded, 16)
            sp.dma_start(wab_raw[:, 1, :], WB).then_inc(w_loaded, 16)
            sp.dma_start(wc_raw[:, :, :], WC.rearrange("(h e) n -> e h n", e=P)).then_inc(w_loaded, 16)
            for u in range(U):
                sp.dma_start(x_sb[u][:, :, :], xin_rows[u]).then_inc(x_loaded[u], 16)
            bgr, bDr = (v.rearrange("(a d) -> a d", a=1).broadcast_to((3, D)) for v in (bg, bD))
            sp.dma_start(bias_row[:, 0:D], bgr).then_inc(w_loaded, 16)
            sp.dma_start(bias_row[:, D:2 * D], bDr).then_inc(w_loaded, 16)
            sp.dma_start(rw_row[:, :], router_w.rearrange("d a -> a d").broadcast_to((P, D))).then_inc(w_loaded, 16)
            sp.dma_start(rb_col[:, :], router_b.rearrange("(a d) -> a d", a=1).broadcast_to((P, 1))).then_inc(w_loaded, 16)

            sp.dma_start(wqk[:, :, 0:D], wq.rearrange("(k p) n -> p k n", p=P)).then_inc(w2_loaded, 16)
            sp.dma_start(wqk[:, :, D:2 * D], wk.rearrange("(k p) n -> p k n", p=P)).then_inc(w2_loaded, 16)
            sp.dma_start(wv_sb[:, :, :], wv.rearrange("(k p) n -> p k n", p=P)).then_inc(w2_loaded, 16)
            sp.dma_start(w1_sb[:, :, :], w1.rearrange("(k p) f -> p k f", p=P)).then_inc(w2_loaded, 16)
            sp.dma_start(w2_sb[:, :, :], w2.rearrange("(f p) n -> p f n", p=P)).then_inc(w2_loaded, 16)
            with nc.allow_non_contiguous_dma("two short columns"):
                sp.dma_start(ln_col[:, 0, :], ln1.rearrange("(k p) -> p k", p=P)).then_inc(w2_loaded, 16)
                sp.dma_start(ln_col[:, 1, :], ln2.rearrange("(k p) -> p k", p=P)).then_inc(w2_loaded, 16)
            sp.wait_ge(zeroed, 1)
            wo_v = wo.rearrange("(g h e) n -> h e g n", h=HG, e=HD)
            for h in range(HG):
                sp.dma_start(wo_pad[h * HP:h * HP + HD, :, :], wo_v[h]).then_inc(w2_loaded, 16)

            for b in range(B):
                def body(i, more, b=b):
                    turn = i + b * LOOPS
                    for u in range(U):
                        j, G = u % 2, U * turn + u
                        if more:
                            sp.wait_ge(s_ready, (G + 1) * 2)
                            sp.wait_ge(xT_done[1], G + 1)
                            sp.dma_start(x_sb[u][:, :, :], xin_rows[G + U]).then_inc(x_loaded[u], 16)
                        sp.wait_ge(x1_ready, (G + 1) * T)
                        sp.dma_start(x1_rows[G], x1_sb[j][:, :, :]).then_inc(x1_stored[b][j], 16)
                        sp.wait_ge(ob_ready, (G + 1) * T)
                        sp.dma_start(out_rows[G], ob_sb[j][:, :, :]).then_inc(ob_stored[b][j], 16)
                if b < B - 1:
                    with sp.Fori(0, LOOPS) as i:
                        body(i, True)
                else:
                    with sp.Fori(0, LOOPS - 1) as i:
                        body(i, True)
                    body(LOOPS - 1, False)
            for b in range(B):
                for h in range(2):
                    sp.wait_ge(mT_ready[b], (h + 1) * MS // P // 2)
                    sp.dma_start(mt_dram[b].rearrange("(h n p) q -> h p n q", p=P, h=2)[h],
                                 big2[:, :, :]).then_inc(mT_stored[b], 16)
            for b in range(B):
                for j in range(2):
                    sp.wait_ge(ob_stored[b][j], 16 * NG // 2)
            sp.wait_ge(scattered, 16 * B * C)

        @block.gpsimd
        def _(pool):
            pool.memset(ident[:, :], 0.0).then_inc(ident_ready, 1)
            pool.wait_ge(ident_ready, 1)
            pool.affine_select(out=ident[:, :], in_=ident[:, :], compare_op=ALU.not_equal, fill=1.0, base=0,
                               pattern=[[-1, P]], channel_multiplier=1).then_inc(ident_ready, 1)
            pool.memset(minus_half[:, :], -0.5).then_inc(ident_ready, 1)
            pool.memset(ones3[:, :], 1.0).then_inc(ident_ready, 1)
            pool.wait_ge(ident_ready, 3)
            pool.memset(wo_pad[:, :, :], 0.0).then_inc(zeroed, 1)
            pool.memset(zeros[:, :], 0.0).then_inc(pool_const, 1)
            pool.memset(ones_b[:, :], 1.0).then_inc(pool_const, 1)
            pool.wait_ge(pool_const, 2)
            pool.affine_select(out=below_b[:, :], in_=ones_b[:, :], compare_op=ALU.is_gt, fill=0.0, base=0,
                               pattern=[[1, P]], channel_multiplier=-1).then_inc(pool_const, 1)
            pool.iota(digit_i[:, :], [[1, CAND]], base=1, channel_multiplier=0).then_inc(pool_const, 1)
            pool.iota(hi_i[:, :], [[1, P]], base=0, channel_multiplier=0).then_inc(pool_const, 1)
            pool.iota(lo_i[:, :], [[1, C]], base=0, channel_multiplier=0).then_inc(pool_const, 1)
            pool.iota(pgt[:, 0, :, :], [[0, NG], [0, T]], base=0, channel_multiplier=1).then_inc(pool_const, 1)
            pool.iota(pgt[:, 1, :, :], [[1, NG], [0, T]], base=0, channel_multiplier=0).then_inc(pool_const, 1)
            pool.iota(pgt[:, 2, :, :], [[0, NG], [1, T]], base=0, channel_multiplier=0).then_inc(pool_const, 1)
            for k in range(HD // 2):
                pool.memset(inv_f[:, k:k + 1], INV_FREQ[k]).then_inc(pool_const, 1)

            for b in range(B):
                with pool.Fori(0, LOOPS) as i:
                    turn = i + b * LOOPS

                    def combine(u, q):
                        j, G = u % 2, U * turn + u
                        n = 2 * G + q
                        pool.wait_ge(rec_g_done, n + 1)
                        pool.wait_ge(dx_g_done, n + 1)
                        pool.tensor_tensor(mix[q][:, :, :], rec_g[q][:, :, :], dx_g[q][:, :, :],
                                           ALU.subtract).then_inc(mixed, 1)
                        pool.wait_ge(x1_ready, before(turn, u, j) * 2 * T - T * (1 if j and u > 1 else 0))
                        pool.wait_ge(mixed, n + 1)
                        pool.tensor_tensor(s_sb[j][:, 2 * q:2 * q + 2, :], mix[q][:, :, :],
                                           x_sb[u][:, 2 * q:2 * q + 2, :], ALU.add).then_inc(s_ready, 1)

                    def rstd(u):
                        pool.wait_ge(ve_ready, U * turn + u + 1)
                        pool.tensor_tensor(small[u % 2][:, 1, :], small[u % 2][:, 0, :], minus_half[:, :],
                                           ALU.pow).then_inc(pow_ready, 1)

                    def rstd2(u):
                        pool.wait_ge(v2_ready, U * turn + u + 1)
                        pool.tensor_tensor(small[u % 2][:, 5, :], small[u % 2][:, 4, :], minus_half[:, :],
                                           ALU.pow).then_inc(pow2_ready, 1)

                    combine(0, 0)
                    for u in range(U):
                        combine(u, 1)
                        rstd(u)
                        if u + 1 < U:
                            combine(u + 1, 0)
                        rstd2(u)

            def gather(dst, table, index, signal):
                pool.indirect_dma_start(out=dst, out_offset=None, in_=table,
                                        in_offset=bass.IndirectOffsetOnAxis(ap=index, axis=0)).then_inc(signal, 16)

            def rsqrt(dst, src, ready, n, signal):
                pool.wait_ge(ready, n)
                pool.tensor_tensor(dst, src, minus_half[:, 0:C], ALU.pow).then_inc(signal, 1)

            mask_rows = mask_in.rearrange("a o s t -> (a o s) t")
            pos_rows = pos_in.rearrange("a (s o) -> (a s) o", o=1)
            pool.wait_ge(rows_ready, 4)
            for b in range(B):
                for j in range(2):
                    pool.wait_ge(x1_stored[b][j], 16 * NG // 2)
            for b in range(B):
                for c in range(C):
                    gather(x_sel[b][:, c, :], x1_dram, row_x[:, b, c:c + 1], x_sel_in[b])
                if b > 0:
                    pool.wait_ge(nm_done[b - 1], C)
                for c in range(C):
                    gather(m_rows[:, c, :], mask_rows, row_m[:, b, c:c + 1], m_rows_in[b])
                rsqrt(ms[b][:, 2, :], ms[b][:, 1, :], ms_ready[b], 1, rms_ready[b])
                for c in range(C):
                    gather(pos_i[:, b, c:c + 1], pos_rows, row_m[:, b, c:c + 1], pos_in_s[b])
                pool.wait_ge(mT_stored[b], 32)
                pool.wait_ge(mT_done[b], MS // P)
                for c in range(C):
                    gather(m_k[:, c, :], mt_dram[b], row_t[:, b, c:c + 1], m_k_in[b])
            for b in range(B):
                if b == 0:
                    pool.memset(v_cur[:, :, :, :], 0.0).then_inc(zeroed, 1)
                    for n in range(4):
                        pool.memset(pr[n][:, K - 1:K], 0.0).then_inc(zeroed, 1)
                    pool.wait_ge(zeroed, 2)
                with pool.Fori(0, H // HG) as hg:
                    turn = hg + b * (H // HG)
                    pool.wait_ge(pv_done[1], turn * (C // 2))
                    pool.wait_ge(v_ready[b], C)
                    for c in range(C):
                        ins = pool.tensor_copy(v_cur[:, c, :, 0:HD],
                                               v_sb[b][:, c, bass.ts(hg, HG * HD)].rearrange("p (h w) -> p h w", h=HG))
                    ins.then_inc(v_cur_ready, 1)
                rsqrt(ms[b][:, 5, :], ms[b][:, 4, :], ms_ready[b], 2, rms_ready[b])
                rsqrt(ms[b][:, 2, :], ms[b][:, 1, :], ve2_ready[b], 1, pow3_ready[b])
                for j in range(2):
                    pool.wait_ge(ob_stored[b][j], 16 * NG // 2)
                for c in range(C):
                    n = P - (c == C - 1)
                    pool.wait_ge(fin_ready[b], c + 1)
                    pool.indirect_dma_start(out=out.rearrange("b s d -> (b s) d"),
                                            out_offset=bass.IndirectOffsetOnAxis(ap=row_x[0:n, b, c:c + 1], axis=0),
                                            in_=hn[0:n, c, :], in_offset=None).then_inc(scattered, 16)

        @block.tensor
        def _(pe):
            pe.wait_ge(ident_ready, 4)
            pe.wait_ge(w_loaded, 16 * 9)
            for c in range(KD):
                for m in range(2):
                    for h in range(2):
                        pe.transpose(ps[:, c, m * D + h * P:m * D + (h + 1) * P],
                                     wraw[:, m, h, c * P:(c + 1) * P], ident[:, :])
                for m in range(2):
                    pe.transpose(ps[:, 2, c * 64 + m * BROW:c * 64 + m * BROW + N],
                                 wab_raw[:, m, c * P:(c + 1) * P], ident[0:N, 0:N])
            for h in range(2):
                mm = pe.transpose(ps[0:N, 3, h * P:(h + 1) * P], wc_raw[:, h, :], ident[:, :])
            mm.then_inc(wt_done, 1)
            pe.wait_ge(wt_copied, 5)
            pe.wait_ge(const_ready, 1)
            for b in range(B):
                with pe.Fori(0, LOOPS) as i:
                    turn = i + b * LOOPS

                    def transposes(u):
                        j, G = u % 2, U * turn + u
                        pe.wait_ge(x_loaded[u], (turn + 1) * 16)
                        for c in range(KD):
                            if u == 0:
                                pe.wait_ge(xT_copied[1], before(turn, u, 1) * KD)
                            else:
                                pe.wait_ge(xT_copied[1 - j], (before(turn, u, 1 - j) - 1) * KD + c + 1)
                            for t in range(T):
                                mm = pe.transpose(ps[:, c, t * P:(t + 1) * P],
                                                  x_sb[u][:, t, c * P:(c + 1) * P], ident[:, :])
                            mm.then_inc(xT_done[c], 1)

                    def recurrence_inputs(u):
                        j = u % 2
                        pe.wait_ge(xT_copied[j], (before(turn, u, j) + 1) * KD)
                        pe.wait_ge(a_ready[1 - j], before(turn, u, 1 - j))
                        pe.wait_ge(b_ready[1 - j], before(turn, u, 1 - j))
                        for c in range(KD):
                            mm = pe.matmul(ps[0:BROW + N, 2, :], wabT[:, c, :], xT[j][:, c, :],
                                           start=(c == 0), stop=(c == KD - 1))
                        mm.then_inc(ab_done, 1)

                    def gates(u, q):
                        j, n = u % 2, 2 * (U * turn + u) + q
                        pe.wait_ge(dx_g_done, n - 1 if u else n - q)
                        for t in range(2):
                            o = ps[:, 3 + 2 * q + t, :]
                            tt = 2 * q + t
                            pe.matmul(o, ones3[:, :], bias3[:, :], start=True, stop=False)
                            for c in range(KD):
                                mm = pe.matmul(o, xT[j][:, c, tt * P:(tt + 1) * P], wgdT[:, c, :],
                                               start=False, stop=(c == KD - 1))
                        mm.then_inc(gd_done, 1)

                    def recurrence_out(u, q):
                        j, n = u % 2, 2 * (U * turn + u) + q
                        pe.wait_ge(h_ready[j], before(turn, u, j) + 1)
                        pe.wait_ge(rec_g_done, n)
                        for t in range(2):
                            tt = 2 * q + t
                            mm = pe.matmul(ps[:, 7, t * D:(t + 1) * D],
                                           h_sb[j][:, :].rearrange("n (p t) -> n t p", t=T)[:, tt, :],
                                           wcT[:, :], start=True, stop=True)
                        mm.then_inc(rec_done, 1)

                    transposes(0)
                    transposes(1)
                    recurrence_inputs(0)
                    for u in range(U):
                        gates(u, 0)
                        recurrence_out(u, 0)
                        if u + 1 < U:
                            recurrence_inputs(u + 1)
                        gates(u, 1)
                        if u + 2 < U:
                            transposes(u + 2)
                        recurrence_out(u, 1)

            for r in range(ROUNDS):
                pe.wait_ge(cnt_ready, r + 1)
                pe.matmul(ps[:, 0, 0:B * CAND], ones_b[:, :], cnt[:, :], start=True, stop=True).then_inc(cnt_sum, 1)
            pe.wait_ge(fcnt_ready, 1)
            pe.matmul(ps[:, 1, 0:32], below_b[:, :], fcnt[:, :, :, :], start=True, stop=True)
            pe.matmul(ps[:, 2, 0:32], ones_b[:, :], fcnt[:, :, :, :], start=True, stop=True).then_inc(fcnt_sum, 1)
            pe.wait_ge(lo_ready, 1)
            for b in range(B):
                pe.wait_ge(at_ready[b], 1)
                for n in range(NG * T):
                    mm = pe.matmul(ps[:, 3 + b, 0:C * VALS], at_hi[:, b, n, :], lo_vals[:, b, n, :, :],
                                   start=(n == 0), stop=(n == NG * T - 1))
                mm.then_inc(picked_done, 1)

            def turn_mask_rows(b):
                pe.wait_ge(m_rows_in[b], 16 * C)
                for n in range(MS // P):
                    if n >= 2:
                        pe.wait_ge(mT_ready[b], n - 1)
                    for c in range(C):
                        mm = pe.transpose(ps[:, n % 2, c * P:(c + 1) * P], m_rows[:, c, n * P:(n + 1) * P], ident[:, :])
                    mm.then_inc(mT_done[b], 1)

            def turn_mask_columns(b):
                pe.wait_ge(m_k_in[b], 16 * C)
                pe.wait_ge(mT_ready[b], MS // P)
                for c in range(C):
                    if c >= 2:
                        pe.wait_ge(nm_ready[b], c - 1)
                    for k in range(C):
                        mm = pe.transpose(ps[:, c % 2, k * P:(k + 1) * P], m_k[:, k, c * P:(c + 1) * P], ident[:, :])
                    mm.then_inc(nm_done[b], 1)

            def turn_hn(b, first):
                for k in range(KD):
                    for c in range(C):
                        pe.wait_ge(hn_ready[b], first + c + 1)
                        mm = pe.transpose(ps[:, 2 + k, c * P:(c + 1) * P], hn[:, c, k * P:(k + 1) * P], ident[:, :])
                    mm.then_inc(hnT_done[b], 1)

            def project(b):
                pe.wait_ge(hnT_ready[b], KD)
                for c in range(C):
                    if c >= 2:
                        pe.wait_ge(qk_ready[b], c - 1)
                        pe.wait_ge(v_ready[b], c - 1)
                    for k in range(KD):
                        mm = pe.matmul(ps[:, 4 + c % 2, :], hnT[:, k, c * P:(c + 1) * P], wqk[:, k, :],
                                       start=(k == 0), stop=(k == KD - 1))
                    mm.then_inc(qk_done[b], 1)
                    for k in range(KD):
                        mm = pe.matmul(ps[:, 6 + c % 2, 0:D], hnT[:, k, c * P:(c + 1) * P], wv_sb[:, k, :],
                                       start=(k == 0), stop=(k == KD - 1))
                    mm.then_inc(v_done[b], 1)

            psb = ps[:, :, :].bitcast(BF16)

            def turn_split(b):
                with pe.Fori(0, C // 2) as i:
                    for e in range(2):
                        done = 2 * i + e + b * C
                        pe.wait_ge(e_ready, (done + 1) * 2)
                        for m in range(2):
                            for half in range(2):
                                pe.wait_ge((qT_ready, kT_ready)[m], done * 2)
                                for h in range(8):
                                    mm = pe.transpose(psb[0:ER, 2 * m + half, h * P:(h + 1) * P],
                                                      e_sb[e][:, m, 8 * half + h, :, :], ident_b[:, :])
                                mm.then_inc(eT_done[2 * m + half], 1)

            def attention(b):
                pe.wait_ge(nm_ready[B - 1], C)
                pe.wait_ge(qT_ready, (b + 1) * C * 2)
                pe.wait_ge(kT_ready, (b + 1) * C * 2)
                pe.wait_ge(zeroed, 6)
                with pe.Fori(0, H // HG) as hg:
                    turn = hg + b * (H // HG)
                    units = [(c, h) for c in range(C) for h in range(HG)]
                    base = turn * len(units)

                    def scores(u):
                        c, h = units[u]
                        pe.wait_ge(sm_ready[u % 2], turn * 8 + u // 2)
                        pe.matmul(ps[:, u % 2, :], qkT[0][:, bass.ds(hg * HG + h, 1), c * P:(c + 1) * P],
                                  qkT[1][:, bass.ds(hg * HG + h, 1), :], start=True, stop=True).then_inc(s_done, 1)

                    def turn_probs(u):
                        pe.wait_ge(pr_ready[u % 4], turn * 4 + u // 4 + 1)
                        half = len(units) // 2
                        pe.wait_ge(prT_copied[u % 2], turn * half + u // 2)
                        for k in range(C):
                            mm = pe.transpose(ps[:, 2 + u % 2, k * P:(k + 1) * P], pr[u % 4][:, k * P:(k + 1) * P],
                                              ident[:, :])
                        mm.then_inc(prT_done[u % 4], 1)

                    def values(c):
                        if c == 0:
                            pe.wait_ge(v_cur_ready, turn + 1)
                            pe.wait_ge(oT_ready, turn)
                        half = len(units) // 2
                        for par in range(2):
                            pe.wait_ge(prT_copied[par], turn * half + 2 * (c + 1))
                        for k in range(C):
                            for h in range(HG):
                                mm = pe.matmul(ps[h * HP:(h + 1) * HP, 4, c * P:(c + 1) * P],
                                               v_cur[:, k, h, :], prT[c % 2][:, h, k, :],
                                               start=(k == 0), stop=(k == C - 1))
                        mm.then_inc(pv_done[c % 2], 1)

                    scores(0)
                    scores(1)
                    for u in range(len(units)):
                        turn_probs(u)
                        if u + 2 < len(units):
                            scores(u + 2)
                        if u % HG == 0 and u:
                            values(u // HG - 1)
                    values(C - 1)
                    pe.wait_ge(rinv_ready, 2 * turn + 2)
                    pe.wait_ge(onT_ready, turn)
                    for c in range(C):
                        mm = pe.transpose(ps[:, 5, c * P:(c + 1) * P], rinv_w[:, c, :, :], ident[:, :])
                    mm.then_inc(rT_done, 1)

            def project_out(b):
                pe.wait_ge(onT_ready, (b + 1) * (H // HG))
                for c in range(C):
                    for g in range(H // HG):
                        mm = pe.matmul(ps[:, 6 + c // 2, (c % 2) * D:(c % 2 + 1) * D], onT[:, g, c * P:(c + 1) * P],
                                       wo_pad[:, g, :], start=(g == 0), stop=(g == H // HG - 1))
                    mm.then_inc(wo_done[b], 1)

            def feed_forward(b):
                pe.wait_ge(hnT_ready[b], 2 * KD)
                for f in range(FB):
                    if f >= 2:
                        pe.wait_ge(gelu_ready[b], f - 1)
                    for k in range(KD):
                        mm = pe.matmul(ps[:, 4 + f % 2, :], w1_sb[:, k, f * P:(f + 1) * P], hnT[:, k, :],
                                       start=(k == 0), stop=(k == KD - 1))
                    mm.then_inc(h1_done[b], 1)
                pe.wait_ge(gelu_ready[b], FB)
                for c in range(C):
                    for f in range(FB):
                        mm = pe.matmul(ps[:, 0 + c // 2, (c % 2) * D:(c % 2 + 1) * D], hidden_sb[:, f, c * P:(c + 1) * P],
                                       w2_sb[:, f, :], start=(f == 0), stop=(f == FB - 1))
                    mm.then_inc(w2_done[b], 1)

            for b in range(B):
                turn_hn(b, 0)
                project(b)
                turn_mask_rows(b)
                turn_mask_columns(b)
                if b == 0:
                    turn_split(b)
            for b in range(B):
                if b > 0:
                    turn_split(b)
                attention(b)
                project_out(b)
                turn_hn(b, C)
                feed_forward(b)

        @block.scalar
        def _(act):
            act.wait_ge(wt_done, 1)
            for c in range(KD):
                act.copy(wgdT[:, c, :], ps[:, c, :]).then_inc(wt_copied, 1)
            act.copy(wcT[:, :], ps[0:N, 3, 0:D]).then_inc(wt_copied, 1)
            for b in range(B):
                with act.Fori(0, LOOPS) as i:
                    turn = i + b * LOOPS

                    def copy_xT(u):
                        j, G = u % 2, U * turn + u
                        for c in range(KD):
                            act.wait_ge(xT_done[c], G + 1)
                            if c == 0:
                                act.wait_ge(gd_done, 2 * G - 2 if u else 2 * G)
                            act.copy(xT[j][:, c, :], ps[:, c, :]).then_inc(xT_copied[j], 1)

                    def recurrence(u):
                        j = u % 2
                        act.wait_ge(ab_done, U * turn + u + 1)
                        act.wait_ge(h_ready[j], before(turn, u, j))
                        act.activation(a_sb[j][:, :].rearrange("n (p t) -> n t p", t=T),
                                       ps[0:N, 2, :].rearrange("n (t p) -> n t p", t=T),
                                       ACT.Tanh).then_inc(a_ready[j], 1)
                        act.copy(b_sb[j][:, :].rearrange("n (p t) -> n t p", t=T),
                                 ps[BROW:BROW + N, 2, :].rearrange("n (t p) -> n t p", t=T)).then_inc(b_ready[j], 1)

                    def gate(u, q):
                        n = 2 * (U * turn + u) + q
                        act.wait_ge(gd_done, n + 1)
                        act.wait_ge(dx_g_done, n - 1 if u else n - q)
                        act.wait_ge(rec_g_done, n - 1 if u else n - q)
                        act.activation(g_sb[q][:, :, :], ps[:, 3 + 2 * q:5 + 2 * q, 0:D],
                                       ACT.Sigmoid).then_inc(g_ready, 1)

                    copy_xT(0)
                    copy_xT(1)
                    recurrence(0)
                    for u in range(U):
                        gate(u, 0)
                        if u + 1 < U:
                            recurrence(u + 1)
                        gate(u, 1)
                        if u + 2 < U:
                            copy_xT(u + 2)

            def copy_hnT(b, first):
                for k in range(KD):
                    act.wait_ge(hnT_done[b], first + k + 1)
                    act.copy(hnT[:, k, :], ps[:, 2 + k, :]).then_inc(hnT_ready[b], 1)

            def copy_qk(b):
                for c in range(C):
                    act.wait_ge(qk_done[b], c + 1)
                    if b > 0:
                        act.wait_ge(e_ready, 2 * C * b)
                    act.copy(qk[:, c, :], ps[:, 4 + c % 2, :]).then_inc(qk_ready[b], 1)

            def sines(b):
                act.wait_ge(angle_ready[b], 1)
                act.activation(trig[b][:, 4, :, :], trig[b][:, 3, :, :], ACT.Sin)
                act.activation(trig[b][:, 5, :, :], trig[b][:, 3, :, :], ACT.Sin, scale=0.5).then_inc(sin_ready[b], 1)

            def copy_mask_rows(b):
                for n in range(MS // P):
                    act.wait_ge(mT_done[b], n + 1)
                    if n == MS // P // 2:
                        act.wait_ge(mT_stored[b], 16)
                    elif b > 0 and n == 0:
                        act.wait_ge(mT_stored[b - 1], 32)
                    act.mul(big2[:, n % (MS // P // 2), :], ps[:, n % 2, :], -1.0).then_inc(mT_ready[b], 1)

            def split(b):
                with act.Fori(0, C // 2) as i:
                    for e in range(2):
                        done = 2 * i + e + b * C
                        q, k = e_sb[e][:, 0, :, :, :], e_sb[e][:, 1, :, :, :]
                        h2 = e_sb[e][:, :, :, 0:1, :].broadcast_to((P, 2, H, 2, HD))
                        act.wait_ge(e_parts, 2 * done + 1)
                        act.copy(q[:, :, 2:5:2, :], h2[:, 0])
                        act.copy(k[:, :, 1:6:4, :], h2[:, 1])
                        act.wait_ge(e_parts, 2 * done + 2)
                        act.copy(q[:, :, 1, :], q[:, :, 3, :])
                        act.copy(k[:, :, 2, :], k[:, :, 3, :]).then_inc(e_ready, 1)
                        for half in range(2):
                            act.wait_ge(eT_done[half], done + 1)
                            act.copy(qkT[0][:, 8 * half:8 * half + 8, bass.ds((2 * i + e) * P, P)],
                                     ps[:, :, :].bitcast(BF16)[0:ER, half, :].rearrange("r (h n) -> r h n", h=8)
                                     ).then_inc(qT_ready, 1)

            def attention(b):
                with act.Fori(0, H // HG) as hg:
                    turn = hg + b * (H // HG)

                    def exponentials(u):
                        c, h = u // HG, u % HG
                        act.wait_ge(sm_ready[u % 2], turn * 8 + u // 2 + 1)
                        act.wait_ge(prT_done[u % 4], turn * 4 + u // 4)
                        act.activation(pr[u % 4][:, 0:K - 1], sm[u % 2][:, 0:K - 1], ACT.Exp,
                                       bias=nmax[:, c, h:h + 1], scale=-1.0,
                                       accum_out=rsum[:, c, h:h + 1]).then_inc(pr_ready[u % 4], 1)

                    def copy_probs(u):
                        c, h = u // HG, u % HG
                        act.wait_ge(prT_done[u % 4], turn * 4 + u // 4 + 1)
                        act.wait_ge(pv_done[c % 2], turn * 2 + c // 2)
                        act.copy(prT[c % 2][:, h, :, :], ps[:, 2 + u % 2, :].rearrange("p (k n) -> p k n", k=C)
                                 ).then_inc(prT_copied[u % 2], 1)

                    act.wait_ge(rinv_ready, 2 * turn)
                    for u in range(0, C * HG, 2):
                        exponentials(u)
                        exponentials(u + 1)
                        copy_probs(u)
                    act.wait_ge(pv_done[1], turn * 2 + 2)
                    act.wait_ge(onT_ready, turn)
                    act.copy(oT[:, :], ps[:, 4, :]).then_inc(oT_ready, 1)

            def hidden(b):
                for f in range(FB):
                    act.wait_ge(h1_done[b], f + 1)
                    if b > 0 and f == 0:
                        act.wait_ge(w2_done[b - 1], C)
                    act.activation(hidden_sb[:, f, :], ps[:, 4 + f % 2, :], ACT.Gelu_apprx_tanh).then_inc(gelu_ready[b], 1)

            for b in range(B):
                copy_hnT(b, 0)
                copy_qk(b)
                sines(b)
                copy_mask_rows(b)
                if b == 0:
                    split(b)
            for b in range(B):
                if b > 0:
                    split(b)
                attention(b)
                copy_hnT(b, KD)
                hidden(b)

        @block.vector
        def _(dve):
            step = Steps(dve, dve_step)
            step.link(dve.memset(wabT[:, :, :], 0.0))
            dve.wait_ge(wt_done, 1)
            for m in range(2):
                dve.tensor_copy(wabT[:, :, m * BROW:m * BROW + N],
                                ps[:, 2, 0:128].rearrange("p (c w) -> p c w", c=2)[:, :, m * BROW:m * BROW + N]
                                ).then_inc(wt_copied, 1)
            dve.wait_ge(w_loaded, 16 * 9)
            dve.wait_ge(ident_ready, 2)
            step.link(dve.tensor_copy(bias_h[:, :], bias_row[:, :]))
            step.link(dve.tensor_tensor(bias_rest[:, :], bias_row[:, :], bias_h[:, :], ALU.subtract))
            step.link(dve.tensor_copy(bias_m[:, :], bias_rest[:, :]))
            step.link(dve.tensor_tensor(bias_row[:, :], bias_rest[:, :], bias_m[:, :], ALU.subtract))
            step.link(dve.tensor_copy(bias_l[:, :], bias_row[:, :]))
            step.link(dve.tensor_scalar(bias_rest[:, :], bias_h[:, :], ident[0:3, 0:1], None, ALU.mult))
            step.link(dve.scalar_tensor_tensor(bias_row[:, :], bias_m[:, :], ident[0:3, 1:2], bias_rest[:, :],
                                               ALU.mult, ALU.add))
            dve.scalar_tensor_tensor(bias3[:, :], bias_l[:, :], ident[0:3, 2:3], bias_row[:, :],
                                     ALU.mult, ALU.add).then_inc(const_ready, 1)

            dve.wait_ge(w2_loaded, 16 * (7 + HG))
            for k in range(KD):
                g1, g2 = ln_col[:, 0, k:k + 1], ln_col[:, 1, k:k + 1]
                dve.tensor_scalar(wqk[:, k, 0:D], wqk[:, k, 0:D], g1, -(HD ** -0.5), ALU.mult, ALU.mult)
                dve.tensor_scalar(wqk[:, k, D:2 * D], wqk[:, k, D:2 * D], g1, None, ALU.mult)
                dve.tensor_scalar(wv_sb[:, k, :], wv_sb[:, k, :], g1, None, ALU.mult)
                step.done(dve.tensor_scalar(w1_sb[:, k, :], w1_sb[:, k, :], g2, None, ALU.mult))
            dve.wait_ge(pool_const, 9 + HD // 2)
            dve.tensor_copy(ident_b[:, :], ident[:, :])
            dve.tensor_copy(hi_row[:, :], hi_i[:, :])
            dve.tensor_copy(lo_row[:, :], lo_i[:, :])
            for b in range(B):
                for n in range(3):
                    dve.tensor_copy(vals[:, b, :, n], pgt[:, n, :, :].rearrange("p g t -> p (g t)"))
            for r in range(ROUNDS):
                dve.tensor_scalar(digits[:, r, :], digit_i[:, :], 32 - DIGIT * (r + 1), None, ALU.logical_shift_left)
            step.link(dve.memset(prefix[:, :, :], 0))

            for b in range(B):
                if b > 0:
                    dve.wait_ge(rec_done, 2 * NG * b)
                step.link(dve.memset(h_sb[1][:, GT - 1:GT], 0.0))
                with dve.Fori(0, LOOPS) as i:
                    turn = i + b * LOOPS
                    step.enter(i, U * (3 * T + 2))

                    def scan(u):
                        j = u % 2
                        dve.wait_ge(a_ready[j], before(turn, u, j) + 1)
                        dve.wait_ge(b_ready[j], before(turn, u, j) + 1)
                        dve.wait_ge(h_ready[1 - j], before(turn, u, 1 - j))
                        dve.wait_ge(rec_done, 2 * (U * turn + u) - (2 if u else 0))
                        dve.tensor_tensor_scan(h_sb[j][:, :], a_sb[j][:, :], b_sb[j][:, :],
                                               h_sb[1 - j][:, GT - 1:GT], ALU.mult, ALU.add
                                               ).then_inc(h_ready[j], 1)

                    def products(u, q):
                        n = 2 * (U * turn + u) + q
                        dve.wait_ge(mixed, n - 1 if u else n - q)
                        dve.wait_ge(g_ready, n + 1)
                        dve.scalar_tensor_tensor(dx_g[q][:, :, :], g_sb[q][:, :, :], 1.0,
                                                 ps[:, 3 + 2 * q:5 + 2 * q, D:2 * D],
                                                 ALU.subtract, ALU.mult).then_inc(dx_g_done, 1)
                        dve.wait_ge(rec_done, n + 1)
                        dve.tensor_tensor(rec_g[q][:, :, :], ps[:, 7, :].rearrange("p (t d) -> p t d", t=2),
                                          g_sb[q][:, :, :], ALU.mult).then_inc(rec_g_done, 1)

                    def statistics(u):
                        j, G = u % 2, U * turn + u
                        dve.wait_ge(s_ready, 2 * (G + 1))
                        dve.wait_ge(pow2_ready, G - 1 if u else G)
                        for t in range(T):
                            last = step.done(dve.bn_stats(stats[j][:, t, :], s_sb[j][:, t, :]))
                        dve.wait_ge(dve_step, last)
                        dve.nop(nofuse=True)
                        for t in range(T):
                            last = step.done(dve.bn_aggr(mv[j][:, t, :], stats[j][:, t, :]))
                        dve.wait_ge(dve_step, last)
                        dve.tensor_scalar(small[j][:, 0, :], mv[j][:, :, 1], LN_EPS, None,
                                          ALU.add).then_inc(ve_ready, 1)

                    def normalise(u):
                        j, G = u % 2, U * turn + u
                        dve.wait_ge(pow_ready, G + 1)
                        step.link(dve.tensor_tensor(small[j][:, 2, :], mv[j][:, :, 1], small[j][:, 1, :], ALU.mult))
                        step.link(dve.tensor_tensor(small[j][:, 3, :], small[j][:, 2, :], small[j][:, 1, :], ALU.mult))
                        dve.tensor_scalar(small[j][:, 4, :], small[j][:, 3, :], LN_EPS / 4, None,
                                          ALU.add).then_inc(v2_ready, 1)
                        dve.wait_ge(x1_stored[b][j], 16 * before(i, u, j))
                        if b > 0:
                            dve.wait_ge(x1_stored[b - 1][j], 16 * NG // 2)
                        for t in range(T):
                            dve.tensor_scalar(x1_sb[j][:, t, :], s_sb[j][:, t, :], mv[j][:, t, 0:1],
                                              small[j][:, 1, t:t + 1], ALU.subtract, ALU.mult).then_inc(x1_ready, 1)

                    def route(u):
                        j, G = u % 2, U * turn + u
                        dve.wait_ge(x1_ready, (G + 1) * T)
                        for t in range(T):
                            last = step.done(dve.tensor_tensor_reduce(junk[:, j, t, :], x1_sb[j][:, t, :],
                                                                      rw_row[:, :], 1.0, 0.0, ALU.mult, ALU.add,
                                                                      logit[j][:, t:t + 1]))
                        dve.wait_ge(ob_stored[b][j], 16 * before(i, u, j))
                        if b > 0:
                            dve.wait_ge(ob_stored[b - 1][j], 16 * NG // 2)
                        dve.wait_ge(pow2_ready, G + 1)
                        for t in range(T):
                            dve.tensor_scalar(ob_sb[j][:, t, :], x1_sb[j][:, t, :], small[j][:, 5, t:t + 1], None,
                                              ALU.mult).then_inc(ob_ready, 1)
                        dve.wait_ge(dve_step, last)
                        dve.tensor_scalar(W[:, b, bass.ds(U * i + u, 1), :].rearrange("p a t -> p (a t)"),
                                          logit[j][:, :], rb_col[:, :], None, ALU.add).then_inc(W_ready, 1)

                    scan(0)
                    products(0, 0)
                    for u in range(U):
                        if u + 1 < U:
                            scan(u + 1)
                        products(u, 1)
                        if u:
                            normalise(u - 1)
                        if u + 1 < U:
                            products(u + 1, 0)
                        if u:
                            route(u - 1)
                        statistics(u)
                    normalise(U - 1)
                    route(U - 1)
                step.leave(LOOPS)

            dve.wait_ge(W_ready, B * NG)

            def floats(dst, key, m):
                step.link(dve.tensor_scalar(m, key, 31, -1, ALU.arith_shift_right, ALU.bitwise_xor))
                step.link(dve.scalar_tensor_tensor(dst, m, SIGN, key, ALU.bitwise_or, ALU.bitwise_xor))

            Wv = W[:, :, :, :].rearrange("p b g t -> p b (g t)")
            for r in range(ROUNDS):
                step.link(dve.tensor_tensor(cand[:, :, :], digits[:, r:r + 1, :].broadcast_to((P, B, CAND)),
                                            prefix[:, :, :].broadcast_to((P, B, CAND)), ALU.bitwise_or))
                floats(cand_f[:, :, :], cand[:, :, :], cand_m[:, :, :])
                for b in range(B):
                    last = step.done(dve.tensor_tensor(
                        geq[:, b, :, :], Wv[:, b:b + 1, :].broadcast_to((P, CAND, NG * T)),
                        cand_f[:, b, :].bitcast(F32).rearrange("p (c o) -> p c o", o=1).broadcast_to((P, CAND, NG * T)),
                        ALU.is_ge))
                dve.wait_ge(dve_step, last)
                with nc.allow_low_precision("counts to 32"):
                    dve.tensor_reduce(cnt[:, :], geq[:, :, :, :].rearrange("p b c n -> p (b c) n"), X,
                                      ALU.add).then_inc(cnt_ready, 1)
                dve.wait_ge(cnt_sum, r + 1)
                step.link(dve.tensor_scalar(enough[:, :, :].rearrange("p b c -> p (b c)"), ps[:, 0, 0:B * CAND],
                                            float(K), None, ALU.is_ge))
                with nc.allow_low_precision("counts to 15"):
                    step.link(dve.tensor_reduce(found[:, :], enough[:, :, :], X, ALU.add))
                step.link(dve.tensor_scalar(found[:, :], found[:, :], 32 - DIGIT * (r + 1), None,
                                            ALU.logical_shift_left))
                step.link(dve.tensor_tensor(prefix[:, :, 0], found[:, :], prefix[:, :, 0], ALU.bitwise_or))
            floats(thr[:, :, :], prefix[:, :, :], cand_m[:, :, 0:1])
            thr_f = thr[:, :, :].bitcast(F32)

            thr_w = thr_f.broadcast_to((P, B, NG * T))
            fl = flags[:, :, :, :, :].rearrange("p k b g t -> p k b (g t)")
            dve.tensor_tensor(fl[:, 0], Wv, thr_w, ALU.is_gt)
            step.link(dve.tensor_tensor(fl[:, 1], Wv, thr_w, ALU.is_equal))
            with nc.allow_low_precision("counts to 4"):
                dve.tensor_reduce(fcnt[:, :, :, :].rearrange("p k b g -> p (k b g)"),
                                  flags[:, :, :, :, :].rearrange("p k b g t -> p (k b g) t"), X,
                                  ALU.add).then_inc(fcnt_ready, 1)
            v = vals[:, :, :, :]
            step.link(dve.tensor_copy(v[:, :, :, 3], Wv))
            step.link(dve.tensor_tensor(w_rest[:, 0], Wv, v[:, :, :, 3], ALU.subtract))
            step.link(dve.tensor_copy(v[:, :, :, 4], w_rest[:, 0]))
            step.link(dve.tensor_tensor(w_rest[:, 1], w_rest[:, 0], v[:, :, :, 4], ALU.subtract))
            step.link(dve.tensor_copy(v[:, :, :, 5], w_rest[:, 1]))
            dve.wait_ge(fcnt_sum, 1)
            step.link(dve.tensor_copy(ftot[:, :, :, :].rearrange("p k b g -> p (k b g)"), ps[:, 2, 0:32]))
            for k in range(2):
                for b in range(B):
                    last = step.done(dve.tensor_tensor_scan(fscan[:, k, b, :], ftot[:, k, b, :], zeros[:, :], 0.0,
                                                            ALU.add, ALU.add))
            dve.wait_ge(dve_step, last)
            last_gt = fscan[:, 0, :, NG - 1:NG]
            step.done(dve.tensor_scalar(room[:, :, :], last_gt, -1.0, float(K - 1), ALU.mult, ALU.add))
            step.link(dve.tensor_tensor(ftot[:, :, :, :], fscan[:, :, :, :], ftot[:, :, :, :], ALU.subtract))
            rk = rank[:, :, :, :, :].rearrange("p k b g t -> p (k b g) t")
            fr = flags[:, :, :, :, :].rearrange("p k b g t -> p (k b g) t")
            step.link(dve.tensor_tensor(rk[:, :, 0], ftot[:, :, :, :].rearrange("p k b g -> p (k b g)"),
                                        ps[:, 1, 0:32], ALU.add))
            for t in range(1, T):
                step.link(dve.tensor_tensor(rk[:, :, t], rk[:, :, t - 1], fr[:, :, t - 1], ALU.add))
            rf = rank[:, :, :, :, :].rearrange("p k b g t -> p k b (g t)")
            room_w = room[:, :, :].broadcast_to((P, B, NG * T))
            step.link(dve.tensor_tensor(sel[:, 0], rf[:, 1], room_w, ALU.is_lt))
            step.link(dve.tensor_tensor(sel[:, 0], sel[:, 0], fl[:, 1], ALU.mult))
            step.link(dve.tensor_tensor(sel[:, 0], sel[:, 0], fl[:, 0], ALU.add))
            step.link(dve.tensor_tensor(sel[:, 1], rf[:, 1], room_w, ALU.min))
            step.link(dve.tensor_tensor(sel[:, 1], sel[:, 1], rf[:, 0], ALU.add))
            step.link(dve.tensor_scalar(sel[:, 2], sel[:, 0], -float(K), float(K), ALU.mult, ALU.add))
            step.link(dve.tensor_tensor(slot_i[:, 0], sel[:, 2], sel[:, 1], ALU.add))
            step.done(dve.tensor_scalar(slot_i[:, 1], slot_i[:, 0], 2, None, ALU.arith_shift_right))
            step.link(dve.tensor_scalar(slot_i[:, 2], slot_i[:, 0], C - 1, None, ALU.bitwise_and))
            step.link(dve.tensor_copy(slot_f[:, :, :, :], slot_i[:, 1:3, :, :]))
            step.link(dve.tensor_tensor(
                at_lo[:, :, :, :].rearrange("p b n c -> p (b n) c"),
                slot_f[:, 1].rearrange("p b (n o) -> p (b n) o", o=1).broadcast_to((P, B * NG * T, C)),
                lo_row[:, :].rearrange("p (o c) -> p o c", o=1).broadcast_to((P, B * NG * T, C)), ALU.is_equal))
            dve.tensor_tensor(
                lo_vals[:, :, :, :, :].rearrange("p b n c v -> p (b n) c v"),
                at_lo[:, :, :, :].rearrange("p b n (c o) -> p (b n) c o", o=1).broadcast_to((P, B * NG * T, C, VALS)),
                vals[:, :, :, :].rearrange("p b (n o) v -> p (b n) o v", o=1).broadcast_to((P, B * NG * T, C, VALS)),
                ALU.mult).then_inc(lo_ready, 1)
            for b in range(B):
                dve.tensor_tensor(
                    at_hi[:, b], slot_f[:, 0, b, :].rearrange("p (n o) -> p n o", o=1).broadcast_to((P, NG * T, P)),
                    hi_row[:, :].rearrange("p (o h) -> p o h", o=1).broadcast_to((P, NG * T, P)),
                    ALU.is_equal).then_inc(at_ready[b], 1)
            dve.wait_ge(picked_done, B)
            step.link(dve.tensor_copy(picked[:, :, :, :].rearrange("p b c v -> p b (c v)"), ps[:, 3:5, 0:C * VALS]))
            pk = picked[:, :, :, :]
            step.link(dve.scalar_tensor_tensor(pick_f[:, 0], pk[:, :, :, 0], float(T), pk[:, :, :, 2],
                                               ALU.mult, ALU.add))
            step.link(dve.scalar_tensor_tensor(pick_f[:, 1], pk[:, :, :, 1], float(GT), pick_f[:, 0],
                                               ALU.mult, ALU.add))
            step.done(dve.tensor_scalar(pick_f[:, 2], pick_f[:, 1], float(MS - 1), None, ALU.min))
            step.link(dve.tensor_tensor(pick_f[:, 3], pk[:, :, :, 3], pk[:, :, :, 4], ALU.add))
            step.link(dve.tensor_tensor(w_sel[:, :, :], pick_f[:, 3], pk[:, :, :, 5], ALU.add))
            for b in range(B):
                dve.tensor_scalar(row_x[:, b, :], pick_f[:, 1, b, :], float(b * S), None, ALU.add).then_inc(rows_ready, 1)
                dve.tensor_scalar(row_m[:, b, :], pick_f[:, 2, b, :], float(b * MS), None, ALU.add).then_inc(rows_ready, 1)
            step.done(dve.tensor_copy(row_t[:, :, :], pick_f[:, 2]))
            step.link(dve.tensor_tensor(not_m[:, :, :], w_sel[:, :, :], thr_f.broadcast_to((P, B, C)), ALU.is_le))

            def mean_square(b, sums, out_):
                for c in range(C):
                    last = step.done(dve.tensor_tensor_reduce(
                        rope_a[:, c // 2, (c % 2) * D:(c % 2 + 1) * D], x_sel[b][:, c, :], x_sel[b][:, c, :], 1.0, 0.0, ALU.mult, ALU.add,
                        ms[b][:, sums, c:c + 1]))
                dve.wait_ge(dve_step, last)
                dve.tensor_scalar(ms[b][:, out_, :], ms[b][:, sums, :], 1.0 / D, RMS_EPS, ALU.mult,
                                  ALU.add).then_inc(ms_ready[b], 1)

            def normalised(b, col, n):
                dve.wait_ge(rms_ready[b], n)
                for c in range(C):
                    dve.tensor_scalar(hn[:, c, :], x_sel[b][:, c, :], ms[b][:, col, c:c + 1], None,
                                      ALU.mult).then_inc(hn_ready[b], 1)

            def angles(b):
                tr = trig[b]
                dve.wait_ge(pos_in_s[b], 16 * C)
                step.link(dve.tensor_copy(pos_f[:, b, :], pos_i[:, b, :]))
                step.link(dve.tensor_tensor(
                    tr[:, 0, :, :], pos_f[:, b, :].rearrange("p (c o) -> p c o", o=1).broadcast_to((P, C, HD // 2)),
                    inv_f[:, :].rearrange("p (o k) -> p o k", o=1).broadcast_to((P, C, HD // 2)), ALU.mult))
                step.link(dve.tensor_scalar(tr[:, 1], tr[:, 0], 1.0 / (2 * np.pi), MAGIC, ALU.mult, ALU.add))
                step.link(dve.tensor_scalar(tr[:, 2], tr[:, 1], MAGIC, None, ALU.subtract))
                step.link(dve.scalar_tensor_tensor(tr[:, 1], tr[:, 2], -PI2_A, tr[:, 0], ALU.mult, ALU.add))
                step.link(dve.scalar_tensor_tensor(tr[:, 0], tr[:, 2], -PI2_B, tr[:, 1], ALU.mult, ALU.add))
                step.link(dve.scalar_tensor_tensor(tr[:, 1], tr[:, 2], -PI2_C, tr[:, 0], ALU.mult, ALU.add))
                dve.tensor_scalar(tr[:, 3], tr[:, 1], PI_MAX, -PI_MAX, ALU.min, ALU.max).then_inc(angle_ready[b], 1)

            def values(b):
                for c in range(C):
                    dve.wait_ge(v_done[b], c + 1)
                    dve.tensor_copy(v_sb[b][:, c, :], ps[:, 6 + c % 2, 0:D]).then_inc(v_ready[b], 1)

            def rope(b):
                tr = trig[b]
                dve.wait_ge(sin_ready[b], 1)
                step.link(dve.tensor_tensor(tr[:, 6], tr[:, 5], tr[:, 5], ALU.mult))
                step.link(dve.tensor_scalar(tr[:, 7], tr[:, 6], -2.0, 1.0, ALU.mult, ALU.add))
                hs = lambda ap: ap.rearrange("p (h z k) -> p h z k", z=2, k=HD // 2)
                for c in range(C):
                    dve.wait_ge(qk_ready[b], c + 1)
                    cos = tr[:, 7, c:c + 1, :].rearrange("p (o z) k -> p o z k", z=1)
                    sin = tr[:, 4, c:c + 1, :]
                    a, r, q = hs(rope_a[:, c % 2, :]), hs(rope_b[:, c % 2, :]), hs(qk[:, c, :])
                    if c >= 2:
                        dve.wait_ge(rope_ready[b], c - 1)
                    dve.tensor_tensor(a, q, cos.broadcast_to((P, 2 * H, 2, HD // 2)), ALU.mult)
                    for z in range(2):
                        last = step.done(dve.tensor_tensor(r[:, :, z], q[:, :, 1 - z],
                                                           sin.broadcast_to((P, 2 * H, HD // 2)), ALU.mult))
                    dve.wait_ge(dve_step, last)
                    dve.tensor_tensor(q[:, :, 0], a[:, :, 0], r[:, :, 0], ALU.subtract)
                    dve.tensor_tensor(q[:, :, 1], a[:, :, 1], r[:, :, 1], ALU.add).then_inc(rope_ready[b], 1)

            def copy_mask(b):
                for c in range(C):
                    dve.wait_ge(nm_done[b], c + 1)
                    dve.tensor_copy(nmask[b][:, c, :], ps[:, c % 2, :]).then_inc(nm_ready[b], 1)


            def split(b):
                with dve.Fori(0, C // 2) as i:
                    step.enter(i, 2 * 2)
                    for e in range(2):
                        done = 2 * i + e + b * C
                        for n in range(4):
                            dve.wait_ge(eT_done[n], 2 * i + b * C)
                        src = qk[:, bass.ds(2 * i + e, 1), :].rearrange("p o (m h k) -> p (o m) h k", m=2, h=H)
                        es = e_sb[e]
                        rest = e_rest[:, e, :].rearrange("p (m h k) -> p m h k", m=2, h=H)
                        if e == 0:
                            dve.wait_ge(rope_ready[b], C)
                        dve.wait_ge(e_ready, 2 * (2 * i + b * C))
                        dve.tensor_copy(es[:, :, :, 0, :], src).then_inc(e_parts, 1)
                        dve.wait_ge(e_parts, 2 * done + 1)
                        step.link(dve.tensor_tensor(rest, src, es[:, :, :, 0, :], ALU.subtract))
                        dve.tensor_copy(es[:, :, :, 3, :], rest).then_inc(e_parts, 1)
                        dve.wait_ge(e_parts, 2 * done + 2)
                        step.done(dve.tensor_tensor(es[:, 0, :, 5, :], rest[:, 0], es[:, 0, :, 3, :], ALU.subtract))
                        dve.tensor_tensor(es[:, 1, :, 4, :], rest[:, 1], es[:, 1, :, 3, :],
                                          ALU.subtract).then_inc(e_ready, 1)
                        for half in range(2):
                            dve.wait_ge(eT_done[2 + half], done + 1)
                            dve.tensor_copy(qkT[1][:, 8 * half:8 * half + 8, bass.ds((2 * i + e) * P, P)],
                                            ps[:, :, :].bitcast(BF16)[0:ER, 2 + half, :].rearrange(
                                                "r (h n) -> r h n", h=8)).then_inc(kT_ready, 1)
                step.leave(C // 2)

            def attention(b):
                with dve.Fori(0, H // HG) as hg:
                    turn = hg + b * (H // HG)

                    def masked(u):
                        c, h = u // HG, u % HG
                        dve.wait_ge(s_done, turn * C * HG + u + 1)
                        dve.wait_ge(pr_ready[(u - 2) % 4], turn * 4 + (u + 2) // 4)
                        dve.nop(nofuse=True)
                        dve.tensor_tensor_reduce(sm[u % 2][:, 0:K - 1], ps[:, u % 2, 0:K - 1], nmask[b][:, c, 0:K - 1],
                                                 1.0, 3.4e38, ALU.add, ALU.min,
                                                 nmax[:, c, h:h + 1]).then_inc(sm_ready[u % 2], 1)

                    def copy_probs(u):
                        c, h = u // HG, u % HG
                        dve.wait_ge(prT_done[u % 4], turn * 4 + u // 4 + 1)
                        dve.wait_ge(pv_done[c % 2], turn * 2 + c // 2)
                        dve.tensor_copy(prT[c % 2][:, h, :, :], ps[:, 2 + u % 2, :].rearrange("p (k n) -> p k n", k=C)
                                        ).then_inc(prT_copied[u % 2], 1)

                    dve.wait_ge(nm_ready[b], C)
                    for u in range(C * HG):
                        masked(u)
                        if u % 2 and u > 2:
                            copy_probs(u - 2)
                    copy_probs(C * HG - 1)
                    for n in range(4):
                        dve.wait_ge(pr_ready[n], turn * 4 + 4)
                    dve.reciprocal(rinv[:, :, :], rsum[:, :, :]).then_inc(rinv_ready, 1)
                    dve.wait_ge(rT_done, turn)
                    dve.wait_ge(rinv_ready, 2 * turn + 1)
                    dve.tensor_copy(rinv_w[:, :, :, :], rinv[:, :, :].rearrange("p c (h o) -> p c h o", o=1)
                                    .broadcast_to((P, C, HG, HP))).then_inc(rinv_ready, 1)
                    dve.wait_ge(rT_done, turn + 1)
                    dve.wait_ge(oT_ready, turn + 1)
                    if b > 0:
                        dve.wait_ge(wo_done[b - 1], C)
                    dve.tensor_tensor(onT[:, bass.ds(hg, 1), :].rearrange("p o n -> p (o n)"), oT[:, :], ps[:, 5, :],
                                      ALU.mult).then_inc(onT_ready, 1)

            def residual(b):
                for c in range(C):
                    dve.wait_ge(wo_done[b], c // 2 * 2 + 2)
                    last = step.done(dve.tensor_tensor(x_sel[b][:, c, :], x_sel[b][:, c, :],
                                                       ps[:, 6 + c // 2, (c % 2) * D:(c % 2 + 1) * D], ALU.add))
                dve.wait_ge(dve_step, last)

            def finish(b):
                for c in range(C):
                    dve.wait_ge(w2_done[b], c // 2 * 2 + 2)
                    last = step.done(dve.tensor_tensor(x_sel[b][:, c, :], x_sel[b][:, c, :],
                                                       ps[:, c // 2, (c % 2) * D:(c % 2 + 1) * D], ALU.add))
                dve.wait_ge(dve_step, last)
                for bb in range(B):
                    dve.wait_ge(ob_stored[bb][b], 16 * NG // 2)
                for c in range(C):
                    last = step.done(dve.scalar_tensor_tensor(keep[b][:, c, :], x_sel[b][:, c, :], w_sel[:, b, c:c + 1],
                                                              keep[b][:, c, :], ALU.mult, ALU.add))
                dve.wait_ge(dve_step, last)
                for c in range(C):
                    last = step.done(dve.bn_stats(stat2[:, c, :], keep[b][:, c, :]))
                dve.wait_ge(dve_step, last)
                for c in range(C):
                    last = step.done(dve.bn_aggr(mv2[:, c, :], stat2[:, c, :]))
                dve.wait_ge(dve_step, last)
                dve.tensor_scalar(ms[b][:, 1, :], mv2[:, :, 1], LN_EPS, None, ALU.add).then_inc(ve2_ready[b], 1)
                dve.wait_ge(pow3_ready[b], 1)
                for c in range(C):
                    dve.tensor_scalar(hn[:, c, :], keep[b][:, c, :], mv2[:, c, 0:1], ms[b][:, 2, c:c + 1],
                                      ALU.subtract, ALU.mult).then_inc(fin_ready[b], 1)

            for b in range(B):
                dve.wait_ge(x_sel_in[b], 16 * C)
                mean_square(b, 0, 1)
                for bb in range(B):
                    dve.wait_ge(ob_stored[bb][b], 16 * NG // 2)
                for c in range(C):
                    last = step.done(dve.scalar_tensor_tensor(keep[b][:, c, :], x_sel[b][:, c, :], not_m[:, b, c:c + 1],
                                                              x_sel[b][:, c, :], ALU.mult, ALU.add))
                if b > 0:
                    dve.wait_ge(hnT_done[b - 1], KD)
                normalised(b, 2, 1)
                values(b)
                angles(b)
                rope(b)
                copy_mask(b)
                if b == 0:
                    split(b)
            for b in range(B):
                if b > 0:
                    split(b)
                attention(b)
                residual(b)
                mean_square(b, 3, 4)
                if b > 0:
                    dve.wait_ge(scattered, 16 * C * b)
                normalised(b, 5, 2)
                finish(b)


_INS = ['L0_attn_x', 'L0_attn_WA', 'L0_attn_WB', 'L0_attn_WC', 'L0_attn_WD', 'L0_attn_bD', 'L0_attn_Wg', 'L0_attn_bg',
        'L0_ffn_attention_mask', 'L0_ffn_position_ids', 'L0_ffn_router_w', 'L0_ffn_router_b', 'L0_ffn_wq', 'L0_ffn_wk',
        'L0_ffn_wv', 'L0_ffn_wo', 'L0_ffn_w1', 'L0_ffn_w2', 'L0_ffn_ln1', 'L0_ffn_ln2']


def kernel(**inputs):
    import concourse.bacc as bacc
    from concourse.bass_utils import run_bass_kernel_spmd

    nc = bacc.Bacc("TRN2", target_bir_lowering=False, num_devices=1)
    arrays, args = {}, []
    for name in _INS:
        a = np.ascontiguousarray(inputs[name])
        arrays[f"in_{name}"] = a
        args.append(nc.dram_tensor(f"in_{name}", a.shape, mybir.dt.from_np(a.dtype), kind="ExternalInput").ap())
    out = nc.dram_tensor("out", (B, S, D), F32, kind="ExternalOutput").ap()
    build(nc, *args, out)
    r = run_bass_kernel_spmd(nc, [arrays], core_ids=[0])
    return r.results[0]["out"]
```

```python
from contextlib import ExitStack

import numpy as np

import concourse.bass as bass
from concourse import mybir

ALU = mybir.AluOpType
ACT = mybir.ActivationFunctionType
F32 = mybir.dt.float32
BF16 = mybir.dt.bfloat16
I32 = mybir.dt.int32
X = mybir.AxisListType.X

P = 128
B, S, D = 2, 4096, 256
N = 16
F = 1024
H, HD = 16, 16
KD = D // P
T = 4
GT = T * P
NG = S // GT
U = 4
LOOPS = NG // U
BROW = 32
K = S // 8
MS = 1024
C = K // P
LN_EPS = 1e-5
RMS_EPS = 1e-6
ROPE_BASE = 10000.0
DIGIT = 4
CAND = 2 ** DIGIT - 1
ROUNDS = 32 // DIGIT
VALS = 6
SLOTS = 6
ER = SLOTS * HD
HG = 4
HP = 32
TURNS = H // HG
UNITS = C * HG
AHEAD = 4
S_BANKS = (0, 1, 6, 7)
LAG = 8
FB = F // P
SIGN = -2 ** 31
MAGIC = 1.5 * 2.0 ** 23
PI2_A = 6.28125
PI2_B = float(np.float32(2 * np.pi - PI2_A).view(np.uint32).__and__(np.uint32(0xFFFFF000)).view(np.float32))
PI2_C = float(2 * np.pi - PI2_A - PI2_B)
PI_MAX = float(np.nextafter(np.float32(np.pi), np.float32(0)))
INV_FREQ = [float(v) for v in np.float32(1.0) / np.power(np.float32(ROPE_BASE), np.arange(0, HD, 2, dtype=np.float32) / np.float32(HD))]


def before(turn, u, j):
    return turn * (U // 2) + (u + 1 - j) // 2


class Steps:

    def __init__(self, eng, sem):
        self.eng, self.sem, self.base, self.k, self.reg, self.per = eng, sem, 0, 0, None, 0

    def value(self):
        at = self.base + self.k
        return at if self.reg is None else self.reg * self.per + at

    def done(self, ins):
        self.k += 1
        ins.then_inc(self.sem, 1)
        return self.value()

    def link(self, ins):
        self.eng.wait_ge(self.sem, self.done(ins))

    def enter(self, reg, per):
        self.base, self.k, self.reg, self.per = self.base + self.k, 0, reg, per

    def leave(self, trips):
        assert self.k == self.per, (self.k, self.per)
        self.base, self.k, self.reg = self.base + trips * self.per, 0, None


def build(nc, x_in, WA, WB, WC, WD, bD, Wg, bg, mask_in, pos_in, router_w, router_b,
          wq, wk, wv, wo, w1, w2, ln1, ln2, out):
    with ExitStack() as ctx:
        def sb(name, shape, dt=F32):
            return ctx.enter_context(nc.sbuf_tensor(name, shape, dt))

        def sem(name):
            return ctx.enter_context(nc.semaphore(name))

        def sems(name, n=2):
            return [sem(f"{name}{i}") for i in range(n)]

        mt_dram = [nc.dram_tensor(f"mt_scratch{b}", (MS, K), F32, kind="Internal").ap() for b in range(B)]
        x1_dram = nc.dram_tensor("x1_scratch", (B * S, D), F32, kind="Internal").ap()

        ps = ctx.enter_context(nc.psum_tensor("ps", [P, 8, 512], F32))

        ident = sb("ident", [P, P])
        nmask = [sb(f"nmask{b}", [P, C, K]) for b in range(B)]
        early = [m[:, :, :].rearrange("p c k -> p (c k)") for m in nmask]
        wraw = early[1][:, 0:4 * D].rearrange("p (m h d) -> p m h d", m=2, h=2)
        wab_raw = early[1][0:N, 4 * D:6 * D].rearrange("p (m d) -> p m d", m=2)
        wc_raw = early[1][:, 6 * D:6 * D + 2 * N].rearrange("p (h n) -> p h n", h=2)
        wgdT = sb("wgdT", [P, KD, 2 * D])
        wabT = sb("wabT", [P, KD, BROW + N])
        wcT = sb("wcT", [N, D])
        bias_row = early[0][0:3, 0:2 * D]
        bias_rest = early[0][0:3, 2 * D:4 * D]
        bias_h, bias_m, bias_l = (early[0][0:3, 4 * D + n * D:5 * D + n * D].bitcast(BF16) for n in range(3))
        bias3 = sb("bias3", [3, 2 * D], BF16)
        ones3 = sb("ones3", [3, P], BF16)
        rw_row = sb("rw_row", [P, D])
        rb_col = sb("rb_col", [P, 1])
        minus_half = sb("minus_half", [P, T])

        arena = sb("arena", [P, (U + 4) * T * D])
        x_sb = [arena[:, u * T * D:(u + 1) * T * D].rearrange("p (t d) -> p t d", t=T) for u in range(U)]
        xT = [arena[:, (U + j) * T * D:(U + j + 1) * T * D].rearrange("p (k n) -> p k n", k=KD) for j in range(2)]
        s_sb = [arena[:, (U + 2 + j) * T * D:(U + 3 + j) * T * D].rearrange("p (t d) -> p t d", t=T) for j in range(2)]
        arena2 = sb("arena2", [P, 9216])
        a_sb, b_sb, h_sb = ([arena2[0:N, 4096 + (2 * n + j) * GT:4096 + (2 * n + j + 1) * GT] for j in range(2)]
                            for n in range(3))
        g_sb, rec_g, dx_g, mix = ([arena2[:, (2 * n + q) * 2 * D:(2 * n + q + 1) * 2 * D].rearrange(
            "p (t d) -> p t d", t=2) for q in range(2)] for n in range(4))
        x1_sb = [sb(f"x1_sb{j}", [P, T, D]) for j in range(2)]
        ob_sb = [sb(f"ob_sb{j}", [P, T, D]) for j in range(2)]
        stats = [sb(f"stats{j}", [P, T, 6]) for j in range(2)]
        mv = [sb(f"mv{j}", [P, T, 2]) for j in range(2)]
        small = [sb(f"small{j}", [P, 8, T]) for j in range(2)]
        junk = arena2[:, 7168:9216].rearrange("p (j t d) -> p j t d", j=2, t=T)
        logit = [sb(f"logit{j}", [P, T]) for j in range(2)]
        W = sb("W", [P, B, NG, T])

        ident_b = sb("ident_b", [P, P], BF16)
        ones_b = sb("ones_b", [P, P], BF16)
        below_b = sb("below_b", [P, P], BF16)
        digit_i = sb("digit_i", [P, CAND], I32)
        digits = sb("digits", [P, ROUNDS, CAND], I32)
        hi_i = sb("hi_i", [P, P], I32)
        hi_row = sb("hi_row", [P, P], BF16)
        lo_i = sb("lo_i", [P, C], I32)
        lo_row = sb("lo_row", [P, C])
        pgt = sb("pgt", [P, 3, NG, T], I32)
        vals = sb("vals", [P, B, NG * T, VALS], BF16)
        prefix = sb("prefix", [P, B, 1], I32)
        cand = sb("cand", [P, B, CAND], I32)
        cand_m = sb("cand_m", [P, B, CAND], I32)
        cand_f = sb("cand_f", [P, B, CAND], I32)
        geq = sb("geq", [P, B, CAND, NG * T], BF16)
        cnt = sb("cnt", [P, B * CAND], BF16)
        enough = sb("enough", [P, B, CAND])
        found = sb("found", [P, B], I32)
        thr = sb("thr", [P, B, 1], I32)
        flags = sb("flags", [P, 2, B, NG, T])
        fcnt = sb("fcnt", [P, 2, B, NG], BF16)
        ftot = sb("ftot", [P, 2, B, NG])
        fscan = sb("fscan", [P, 2, B, NG])
        zeros = sb("zeros", [P, NG])
        rank = sb("rank", [P, 2, B, NG, T])
        room = sb("room", [P, B, 1])
        sel = sb("sel", [P, 4, B, NG * T])
        slot_i = sb("slot_i", [P, 3, B, NG * T], I32)
        slot_f = sb("slot_f", [P, 2, B, NG * T])
        w_rest = sb("w_rest", [P, 2, B, NG * T])
        at_lo = sb("at_lo", [P, B, NG * T, C])
        lo_vals = sb("lo_vals", [P, B, NG * T, C, VALS], BF16)
        picked = sb("picked", [P, B, C, VALS])
        pick_f = sb("pick_f", [P, 4, B, C])
        w_sel = sb("w_sel", [P, B, C])
        not_m = sb("not_m", [P, B, C])
        row_x = sb("row_x", [P, B, C], I32)
        row_m = sb("row_m", [P, B, C], I32)
        row_t = sb("row_t", [P, B, C], I32)

        wqk = sb("wqk", [P, KD, 2 * D])
        wv_sb = sb("wv_sb", [P, KD, D])
        wo_pad = sb("wo_pad", [P, H // HG, D])
        w1_sb = sb("w1_sb", [P, KD, F])
        w2_sb = sb("w2_sb", [P, FB, D])
        ln_col = sb("ln_col", [P, 2, KD])
        inv_f = sb("inv_f", [P, HD // 2])
        x_sel, keep = x1_sb, ob_sb
        pos_i = sb("pos_i", [P, B, C], I32)
        pos_f = sb("pos_f", [P, B, C])
        trig = [sb(f"trig{b}", [P, 8, C, HD // 2]) for b in range(B)]
        big = sb("big", [P, C * MS])
        at_hi = big[:, :].bitcast(BF16).rearrange("p (b n h) -> p b n h", b=B, h=P)
        m_rows = [m[:, 0:C * MS].rearrange("p (c s) -> p c s", c=C) for m in (big, arena)]
        m_k = [big[:, b * C * K:(b + 1) * C * K].rearrange("p (c k) -> p c k", c=C) for b in range(B)]
        prT = [big[:, n * 2048:(n + 1) * 2048].rearrange("p (h c n) -> p h c n", h=HG, c=C) for n in range(2)]
        hidden_sb = big[:, :].rearrange("p (f n) -> p f n", f=FB)
        big2 = sb("big2", [P, MS // P // 2, K])
        ms = [sb(f"ms{b}", [P, 6, C]) for b in range(B)]
        hn = wgdT[:, :, :].rearrange("p k (h d) -> p (k h) d", h=2)
        hnT = sb("hnT", [P, KD, K])
        qk = sb("qk", [P, C, 2 * D])
        onT = sb("onT", [P, H // HG, K])
        rope_a = onT[:, 0:2, :]
        rope_b = arena2[:, 1024:2048].rearrange("p (c n) -> p c n", c=2)
        v_sb = [sb(f"v_sb{b}", [P, C, D]) for b in range(B)]
        e_rest = arena2[:, 4096:5120].rearrange("p (e n) -> p e n", e=2)
        e_sb = [arena2[:, 5120 + e * 1536:6656 + e * 1536].bitcast(BF16).rearrange(
            "p (m h s k) -> p m h s k", m=2, h=H, s=SLOTS) for e in range(2)]
        qkT = [arena[:, 4096 * m:4096 * (m + 1)].bitcast(BF16)[0:ER, 0:H * K].rearrange("r (h n) -> r h n", h=H)
               for m in range(2)]
        v_cur = arena2[:, 8704:9216].rearrange("p (c h w) -> p c h w", c=C, h=HG)
        sm = [arena2[:, n * K:(n + 1) * K] for n in range(4)]
        pr = [arena2[:, 2048 + n * K:2048 + (n + 1) * K] for n in range(4)]
        oT = arena2[:, 8192:8704]
        nmax = sb("nmax", [P, C, HG])
        rinv = sb("rinv", [P, C, HG])
        rsum = sb("rsum", [P, C, HG])
        rinv_w = sb("rinv_w", [P, C, HG, HP])
        stat2 = sb("stat2", [P, C, 6])
        mv2 = sb("mv2", [P, C, 2])

        w_loaded = sem("w_loaded")
        w2_loaded = sem("w2_loaded")
        zeroed = sem("zeroed")
        pool_const = sem("pool_const")
        cnt_ready = sem("cnt_ready")
        cnt_sum = sem("cnt_sum")
        fcnt_ready = sem("fcnt_ready")
        fcnt_sum = sem("fcnt_sum")
        at_ready = sems("at_ready")
        lo_ready = sem("lo_ready")
        picked_done = sem("picked_done")
        rows_ready = sem("rows_ready")
        x_sel_in = sems("x_sel_in")
        pos_in_s = sems("pos_in_s")
        m_rows_in = sems("m_rows_in")
        mT_done = sems("mT_done")
        mT_ready = sems("mT_ready")
        mT_stored = sems("mT_stored")
        m_k_in = sems("m_k_in")
        nm_done = sems("nm_done")
        nm_ready = sems("nm_ready")
        ms_ready = sems("ms_ready")
        rms_ready = sems("rms_ready")
        hn_ready = sems("hn_ready")
        hnT_done = sems("hnT_done")
        hnT_ready = sems("hnT_ready")
        qk_done = sems("qk_done")
        v_done = sems("v_done")
        qk_ready = sems("qk_ready")
        v_ready = sems("v_ready")
        angle_ready = sems("angle_ready")
        sin_ready = sems("sin_ready")
        trig_ready = sems("trig_ready")
        rope_ready = sems("rope_ready")
        e_parts = sem("e_parts")
        e_ready = sem("e_ready")
        eT_done = [sem(f"eT_done{n}") for n in range(4)]
        qT_ready = sem("qT_ready")
        kT_ready = sem("kT_ready")
        v_cur_ready = sem("v_cur_ready")
        s_done = sem("s_done")
        sm_ready = sem("sm_ready")
        pr_ready = sem("pr_ready")
        prT_done = sem("prT_done")
        prT_copied = sems("prT_copied")
        pv_done = sem("pv_done")
        rinv_ready = sem("rinv_ready")
        rT_done = sem("rT_done")
        oT_ready = sem("oT_ready")
        onT_ready = sem("onT_ready")
        wo_done = sems("wo_done")
        h1_done = sems("h1_done")
        gelu_ready = sems("gelu_ready")
        w2_done = sems("w2_done")
        x2_ready = sems("x2_ready")
        ve2_ready = sems("ve2_ready")
        pow3_ready = sems("pow3_ready")
        fin_ready = sems("fin_ready")
        scattered = sem("scattered")
        ident_ready = sem("ident_ready")
        wt_done = sem("wt_done")
        wt_copied = sem("wt_copied")
        const_ready = sem("const_ready")
        x_loaded = sems("x_loaded", U)
        xT_done = sems("xT_done")
        xT_copied = sems("xT_copied")
        ab_done = sem("ab_done")
        a_ready = sems("a_ready")
        b_ready = sems("b_ready")
        h_ready = sems("h_ready")
        gd_done = sem("gd_done")
        rec_done = sem("rec_done")
        g_ready = sem("g_ready")
        rec_g_done = sem("rec_g_done")
        dx_g_done = sem("dx_g_done")
        mixed = sem("mixed")
        s_ready = sem("s_ready")
        ve_ready = sem("ve_ready")
        pow_ready = sem("pow_ready")
        v2_ready = sem("v2_ready")
        pow2_ready = sem("pow2_ready")
        W_ready = sem("W_ready")
        x1_ready = sem("x1_ready")
        ob_ready = sem("ob_ready")
        dve_step = sem("dve_step")
        x1_stored = [sems(f"x1_stored{b}_") for b in range(B)]
        ob_stored = [sems(f"ob_stored{b}_") for b in range(B)]

        x1_rows = x1_dram.rearrange("(n p t) d -> n p (t d)", p=P, t=T)
        out_rows = out.rearrange("b (g p t) d -> (b g) p (t d)", p=P, t=T)
        xin_rows = x_in.rearrange("b (g p t) d -> (b g) p (t d)", p=P, t=T)

        units = [(c, h) for c in range(C) for h in range(HG)]

        def hg_is(hg, n):
            return isinstance(hg, int) and hg == n

        def first(b, hg):
            return b == 0 and hg_is(hg, 0)

        def unit_number(b, hg, u):
            return (hg + b * TURNS) * UNITS + u

        def all_turns(eng, body):
            body(0)
            with eng.Fori(1, TURNS - 1) as hg:
                body(hg)
            body(TURNS - 1)

        def copy_probs(eng, copy, b, hg, u):
            c, h = units[u]
            eng.wait_ge(prT_done, unit_number(b, hg, u) + 1)
            if not first(b, hg) or c >= 2:
                eng.wait_ge(pv_done, (hg + b * TURNS) * C + c - 1)
            copy(prT[c % 2][:, h, :, :], ps[:, 2 + u % 2, :].rearrange("p (k n) -> p k n", k=C)
                 ).then_inc(prT_copied[u % 2], 1)

        block = ctx.enter_context(nc.Block())

        @block.sync
        def _(sp):
            sp.dma_start(wraw[:, 0, :, :], Wg.rearrange("(h e) d -> e h d", e=P)).then_inc(w_loaded, 16)
            sp.dma_start(wraw[:, 1, :, :], WD.rearrange("(h e) d -> e h d", e=P)).then_inc(w_loaded, 16)
            sp.dma_start(wab_raw[:, 0, :], WA).then_inc(w_loaded, 16)
            sp.dma_start(wab_raw[:, 1, :], WB).then_inc(w_loaded, 16)
            sp.dma_start(wc_raw[:, :, :], WC.rearrange("(h e) n -> e h n", e=P)).then_inc(w_loaded, 16)
            for u in range(U):
                sp.dma_start(x_sb[u][:, :, :], xin_rows[u]).then_inc(x_loaded[u], 16)
            bgr, bDr = (v.rearrange("(a d) -> a d", a=1).broadcast_to((3, D)) for v in (bg, bD))
            sp.dma_start(bias_row[:, 0:D], bgr).then_inc(w_loaded, 16)
            sp.dma_start(bias_row[:, D:2 * D], bDr).then_inc(w_loaded, 16)
            sp.dma_start(rw_row[:, :], router_w.rearrange("d a -> a d").broadcast_to((P, D))).then_inc(w_loaded, 16)
            sp.dma_start(rb_col[:, :], router_b.rearrange("(a d) -> a d", a=1).broadcast_to((P, 1))).then_inc(w_loaded, 16)

            sp.dma_start(wqk[:, :, 0:D], wq.rearrange("(k p) n -> p k n", p=P)).then_inc(w2_loaded, 16)
            sp.dma_start(wqk[:, :, D:2 * D], wk.rearrange("(k p) n -> p k n", p=P)).then_inc(w2_loaded, 16)
            sp.dma_start(wv_sb[:, :, :], wv.rearrange("(k p) n -> p k n", p=P)).then_inc(w2_loaded, 16)
            sp.dma_start(w1_sb[:, :, :], w1.rearrange("(k p) f -> p k f", p=P)).then_inc(w2_loaded, 16)
            sp.dma_start(w2_sb[:, :, :], w2.rearrange("(f p) n -> p f n", p=P)).then_inc(w2_loaded, 16)
            with nc.allow_non_contiguous_dma("two short columns"):
                sp.dma_start(ln_col[:, 0, :], ln1.rearrange("(k p) -> p k", p=P)).then_inc(w2_loaded, 16)
                sp.dma_start(ln_col[:, 1, :], ln2.rearrange("(k p) -> p k", p=P)).then_inc(w2_loaded, 16)
            sp.wait_ge(zeroed, 1)
            wo_v = wo.rearrange("(g h e) n -> h e g n", h=HG, e=HD)
            for h in range(HG):
                sp.dma_start(wo_pad[h * HP:h * HP + HD, :, :], wo_v[h]).then_inc(w2_loaded, 16)

            for b in range(B):
                def body(i, more, b=b):
                    turn = i + b * LOOPS
                    for u in range(U):
                        j, G = u % 2, U * turn + u
                        if more:
                            sp.wait_ge(s_ready, (G + 1) * 2)
                            sp.wait_ge(xT_done[1], G + 1)
                            sp.dma_start(x_sb[u][:, :, :], xin_rows[G + U]).then_inc(x_loaded[u], 16)
                        sp.wait_ge(x1_ready, (G + 1) * T)
                        sp.dma_start(x1_rows[G], x1_sb[j][:, :, :]).then_inc(x1_stored[b][j], 16)
                        sp.wait_ge(ob_ready, (G + 1) * T)
                        sp.dma_start(out_rows[G], ob_sb[j][:, :, :]).then_inc(ob_stored[b][j], 16)
                if b < B - 1:
                    with sp.Fori(0, LOOPS) as i:
                        body(i, True)
                else:
                    with sp.Fori(0, LOOPS - 1) as i:
                        body(i, True)
                    body(LOOPS - 1, False)
            for b in range(B):
                for h in range(2):
                    sp.wait_ge(mT_ready[b], (h + 1) * MS // P // 2)
                    sp.dma_start(mt_dram[b].rearrange("(h n p) q -> h p n q", p=P, h=2)[h],
                                 big2[:, :, :]).then_inc(mT_stored[b], 16)
            for b in range(B):
                for j in range(2):
                    sp.wait_ge(ob_stored[b][j], 16 * NG // 2)
            sp.wait_ge(scattered, 16 * B * C)

        @block.gpsimd
        def _(pool):
            pool.memset(ident[:, :], 0.0).then_inc(ident_ready, 1)
            pool.wait_ge(ident_ready, 1)
            pool.affine_select(out=ident[:, :], in_=ident[:, :], compare_op=ALU.not_equal, fill=1.0, base=0,
                               pattern=[[-1, P]], channel_multiplier=1).then_inc(ident_ready, 1)
            pool.memset(minus_half[:, :], -0.5).then_inc(ident_ready, 1)
            pool.memset(ones3[:, :], 1.0).then_inc(ident_ready, 1)
            pool.wait_ge(ident_ready, 3)
            pool.memset(wo_pad[:, :, :], 0.0).then_inc(zeroed, 1)
            pool.memset(zeros[:, :], 0.0).then_inc(pool_const, 1)
            pool.memset(ones_b[:, :], 1.0).then_inc(pool_const, 1)
            pool.wait_ge(pool_const, 2)
            pool.affine_select(out=below_b[:, :], in_=ones_b[:, :], compare_op=ALU.is_gt, fill=0.0, base=0,
                               pattern=[[1, P]], channel_multiplier=-1).then_inc(pool_const, 1)
            pool.iota(digit_i[:, :], [[1, CAND]], base=1, channel_multiplier=0).then_inc(pool_const, 1)
            pool.iota(hi_i[:, :], [[1, P]], base=0, channel_multiplier=0).then_inc(pool_const, 1)
            pool.iota(lo_i[:, :], [[1, C]], base=0, channel_multiplier=0).then_inc(pool_const, 1)
            pool.iota(pgt[:, 0, :, :], [[0, NG], [0, T]], base=0, channel_multiplier=1).then_inc(pool_const, 1)
            pool.iota(pgt[:, 1, :, :], [[1, NG], [0, T]], base=0, channel_multiplier=0).then_inc(pool_const, 1)
            pool.iota(pgt[:, 2, :, :], [[0, NG], [1, T]], base=0, channel_multiplier=0).then_inc(pool_const, 1)
            for k in range(HD // 2):
                pool.memset(inv_f[:, k:k + 1], INV_FREQ[k]).then_inc(pool_const, 1)

            for b in range(B):
                with pool.Fori(0, LOOPS) as i:
                    turn = i + b * LOOPS

                    def combine(u, q):
                        j, G = u % 2, U * turn + u
                        n = 2 * G + q
                        pool.wait_ge(rec_g_done, n + 1)
                        pool.wait_ge(dx_g_done, n + 1)
                        pool.tensor_tensor(mix[q][:, :, :], rec_g[q][:, :, :], dx_g[q][:, :, :],
                                           ALU.subtract).then_inc(mixed, 1)
                        pool.wait_ge(x1_ready, before(turn, u, j) * 2 * T - T * (1 if j and u > 1 else 0))
                        pool.wait_ge(mixed, n + 1)
                        pool.tensor_tensor(s_sb[j][:, 2 * q:2 * q + 2, :], mix[q][:, :, :],
                                           x_sb[u][:, 2 * q:2 * q + 2, :], ALU.add).then_inc(s_ready, 1)

                    def rstd(u):
                        pool.wait_ge(ve_ready, U * turn + u + 1)
                        pool.tensor_tensor(small[u % 2][:, 1, :], small[u % 2][:, 0, :], minus_half[:, :],
                                           ALU.pow).then_inc(pow_ready, 1)

                    def rstd2(u):
                        pool.wait_ge(v2_ready, U * turn + u + 1)
                        pool.tensor_tensor(small[u % 2][:, 5, :], small[u % 2][:, 4, :], minus_half[:, :],
                                           ALU.pow).then_inc(pow2_ready, 1)

                    combine(0, 0)
                    for u in range(U):
                        combine(u, 1)
                        rstd(u)
                        if u + 1 < U:
                            combine(u + 1, 0)
                        rstd2(u)

            def gather(dst, table, index, signal):
                pool.indirect_dma_start(out=dst, out_offset=None, in_=table,
                                        in_offset=bass.IndirectOffsetOnAxis(ap=index, axis=0)).then_inc(signal, 16)

            def rsqrt(dst, src, ready, n, signal):
                pool.wait_ge(ready, n)
                pool.tensor_tensor(dst, src, minus_half[:, 0:C], ALU.pow).then_inc(signal, 1)

            mask_rows = mask_in.rearrange("a o s t -> (a o s) t")
            pos_rows = pos_in.rearrange("a (s o) -> (a s) o", o=1)
            pool.wait_ge(rows_ready, 4)
            for b in range(B):
                for j in range(2):
                    pool.wait_ge(x1_stored[b][j], 16 * NG // 2)
            for b in range(B):
                for c in range(C):
                    gather(x_sel[b][:, c, :], x1_dram, row_x[:, b, c:c + 1], x_sel_in[b])
                for c in range(C):
                    gather(m_rows[b][:, c, :], mask_rows, row_m[:, b, c:c + 1], m_rows_in[b])
                for c in range(C):
                    gather(pos_i[:, b, c:c + 1], pos_rows, row_m[:, b, c:c + 1], pos_in_s[b])
                rsqrt(ms[b][:, 2, :], ms[b][:, 1, :], ms_ready[b], 1, rms_ready[b])
            pool.wait_ge(mT_done[0], MS // P)
            for b in range(B):
                pool.wait_ge(mT_stored[b], 32)
                for c in range(C):
                    gather(m_k[b][:, c, :], mt_dram[b], row_t[:, b, c:c + 1], m_k_in[b])
            for b in range(B):
                if b == 0:
                    pool.memset(v_cur[:, :, :, :], 0.0).then_inc(zeroed, 1)
                    pool.memset(arena2[:, 2048:4096].rearrange("p (n k) -> p n k", n=4)[:, :, K - 1:K],
                                0.0).then_inc(zeroed, 1)
                    pool.wait_ge(zeroed, 3)
                pool.wait_ge(v_ready[b], C)

                def turn_body(hg):
                    turn = hg + b * TURNS
                    if not first(b, hg):
                        pool.wait_ge(pv_done, turn * C)
                    pool.tensor_copy(v_cur[:, :, :, 0:HD], v_sb[b][:, :, bass.ts(hg, HG * HD)].rearrange(
                        "p c (h w) -> p c h w", h=HG)).then_inc(v_cur_ready, 1)

                all_turns(pool, turn_body)
                rsqrt(ms[b][:, 5, :], ms[b][:, 4, :], ms_ready[b], 2, rms_ready[b])
            for b in range(B):
                rsqrt(ms[b][:, 2, :], ms[b][:, 1, :], ve2_ready[b], 1, pow3_ready[b])
                for bb in range(B):
                    for j in range(2):
                        pool.wait_ge(ob_stored[bb][j], 16 * NG // 2)
                for c in range(C):
                    n = P - (c == C - 1)
                    pool.wait_ge(fin_ready[b], c + 1)
                    pool.indirect_dma_start(out=out.rearrange("b s d -> (b s) d"),
                                            out_offset=bass.IndirectOffsetOnAxis(ap=row_x[0:n, b, c:c + 1], axis=0),
                                            in_=x_sel[b][0:n, c, :], in_offset=None).then_inc(scattered, 16)

        @block.tensor
        def _(pe):
            pe.wait_ge(ident_ready, 4)
            pe.wait_ge(w_loaded, 16 * 9)
            for c in range(KD):
                for m in range(2):
                    for h in range(2):
                        pe.transpose(ps[:, c, m * D + h * P:m * D + (h + 1) * P],
                                     wraw[:, m, h, c * P:(c + 1) * P], ident[:, :])
                for m in range(2):
                    pe.transpose(ps[:, 2, c * 64 + m * BROW:c * 64 + m * BROW + N],
                                 wab_raw[:, m, c * P:(c + 1) * P], ident[0:N, 0:N])
            for h in range(2):
                mm = pe.transpose(ps[0:N, 3, h * P:(h + 1) * P], wc_raw[:, h, :], ident[:, :])
            mm.then_inc(wt_done, 1)
            pe.wait_ge(wt_copied, 5)
            pe.wait_ge(const_ready, 1)
            for b in range(B):
                with pe.Fori(0, LOOPS) as i:
                    turn = i + b * LOOPS

                    def transposes(u):
                        j, G = u % 2, U * turn + u
                        pe.wait_ge(x_loaded[u], (turn + 1) * 16)
                        for c in range(KD):
                            if u == 0:
                                pe.wait_ge(xT_copied[1], before(turn, u, 1) * KD)
                            else:
                                pe.wait_ge(xT_copied[1 - j], (before(turn, u, 1 - j) - 1) * KD + c + 1)
                            for t in range(T):
                                mm = pe.transpose(ps[:, c, t * P:(t + 1) * P],
                                                  x_sb[u][:, t, c * P:(c + 1) * P], ident[:, :])
                            mm.then_inc(xT_done[c], 1)

                    def recurrence_inputs(u):
                        j = u % 2
                        pe.wait_ge(xT_copied[j], (before(turn, u, j) + 1) * KD)
                        pe.wait_ge(a_ready[1 - j], before(turn, u, 1 - j))
                        pe.wait_ge(b_ready[1 - j], before(turn, u, 1 - j))
                        for c in range(KD):
                            mm = pe.matmul(ps[0:BROW + N, 2, :], wabT[:, c, :], xT[j][:, c, :],
                                           start=(c == 0), stop=(c == KD - 1))
                        mm.then_inc(ab_done, 1)

                    def gates(u, q):
                        j, n = u % 2, 2 * (U * turn + u) + q
                        pe.wait_ge(dx_g_done, n - 1 if u else n - q)
                        for t in range(2):
                            o = ps[:, 3 + 2 * q + t, :]
                            tt = 2 * q + t
                            pe.matmul(o, ones3[:, :], bias3[:, :], start=True, stop=False)
                            for c in range(KD):
                                mm = pe.matmul(o, xT[j][:, c, tt * P:(tt + 1) * P], wgdT[:, c, :],
                                               start=False, stop=(c == KD - 1))
                        mm.then_inc(gd_done, 1)

                    def recurrence_out(u, q):
                        j, n = u % 2, 2 * (U * turn + u) + q
                        pe.wait_ge(h_ready[j], before(turn, u, j) + 1)
                        pe.wait_ge(rec_g_done, n)
                        for t in range(2):
                            tt = 2 * q + t
                            mm = pe.matmul(ps[:, 7, t * D:(t + 1) * D],
                                           h_sb[j][:, :].rearrange("n (p t) -> n t p", t=T)[:, tt, :],
                                           wcT[:, :], start=True, stop=True)
                        mm.then_inc(rec_done, 1)

                    transposes(0)
                    transposes(1)
                    recurrence_inputs(0)
                    for u in range(U):
                        gates(u, 0)
                        recurrence_out(u, 0)
                        if u + 1 < U:
                            recurrence_inputs(u + 1)
                        gates(u, 1)
                        if u + 2 < U:
                            transposes(u + 2)
                        recurrence_out(u, 1)

            for r in range(ROUNDS):
                pe.wait_ge(cnt_ready, r + 1)
                pe.matmul(ps[:, 0, 0:B * CAND], ones_b[:, :], cnt[:, :], start=True, stop=True).then_inc(cnt_sum, 1)
            pe.wait_ge(fcnt_ready, 1)
            pe.matmul(ps[:, 1, 0:32], below_b[:, :], fcnt[:, :, :, :], start=True, stop=True)
            pe.matmul(ps[:, 2, 0:32], ones_b[:, :], fcnt[:, :, :, :], start=True, stop=True).then_inc(fcnt_sum, 1)
            pe.wait_ge(lo_ready, 1)
            for b in range(B):
                pe.wait_ge(at_ready[b], 1)
                for n in range(NG * T):
                    mm = pe.matmul(ps[:, 3 + b, 0:C * VALS], at_hi[:, b, n, :], lo_vals[:, b, n, :, :],
                                   start=(n == 0), stop=(n == NG * T - 1))
                mm.then_inc(picked_done, 1)

            def turn_mask_rows(b):
                pe.wait_ge(m_rows_in[b], 16 * C)
                for n in range(MS // P):
                    if n >= 2:
                        pe.wait_ge(mT_ready[b], n - 1)
                    elif b > 0:
                        pe.wait_ge(mT_ready[b - 1], MS // P)
                    for c in range(C):
                        mm = pe.transpose(ps[:, n % 2, c * P:(c + 1) * P], m_rows[b][:, c, n * P:(n + 1) * P], ident[:, :])
                    mm.then_inc(mT_done[b], 1)

            def turn_mask_columns(b):
                pe.wait_ge(m_k_in[b], 16 * C)
                pe.wait_ge(qT_ready, C * 2)
                for c in range(C):
                    if c >= 2:
                        pe.wait_ge(nm_ready[b], c - 1)
                    elif b > 0:
                        pe.wait_ge(nm_ready[b - 1], C)
                    for k in range(C):
                        mm = pe.transpose(ps[:, c % 2, k * P:(k + 1) * P], m_k[b][:, k, c * P:(c + 1) * P], ident[:, :])
                    mm.then_inc(nm_done[b], 1)

            def turn_hn(b, first):
                for k in range(KD):
                    for c in range(C):
                        pe.wait_ge(hn_ready[b], first + c + 1)
                        mm = pe.transpose(ps[:, 2 + k, c * P:(c + 1) * P], hn[:, c, k * P:(k + 1) * P], ident[:, :])
                    mm.then_inc(hnT_done[b], 1)

            def project(b):
                pe.wait_ge(hnT_ready[b], KD)
                for c in range(C):
                    if c >= 2:
                        pe.wait_ge(qk_ready[b], c - 1)
                        pe.wait_ge(v_ready[b], c - 1)
                    for k in range(KD):
                        mm = pe.matmul(ps[:, 4 + c % 2, :], hnT[:, k, c * P:(c + 1) * P], wqk[:, k, :],
                                       start=(k == 0), stop=(k == KD - 1))
                    mm.then_inc(qk_done[b], 1)
                    for k in range(KD):
                        mm = pe.matmul(ps[:, 6 + c % 2, 0:D], hnT[:, k, c * P:(c + 1) * P], wv_sb[:, k, :],
                                       start=(k == 0), stop=(k == KD - 1))
                    mm.then_inc(v_done[b], 1)

            psb = ps[:, :, :].bitcast(BF16)

            def turn_split(b):
                with pe.Fori(0, C // 2) as i:
                    for e in range(2):
                        done = 2 * i + e + b * C
                        pe.wait_ge(e_ready, (done + 1) * 2)
                        for m in range(2):
                            for half in range(2):
                                pe.wait_ge((qT_ready, kT_ready)[m], done * 2)
                                for h in range(8):
                                    mm = pe.transpose(psb[0:ER, 2 * m + half, h * P:(h + 1) * P],
                                                      e_sb[e][:, m, 8 * half + h, :, :], ident_b[:, :])
                                mm.then_inc(eT_done[2 * m + half], 1)

            def attention(b):
                pe.wait_ge(nm_ready[B - 1], C)
                pe.wait_ge(v_ready[B - 1], C)
                pe.wait_ge(qT_ready, (b + 1) * C * 2)
                pe.wait_ge(kT_ready, (b + 1) * C * 2)
                if b > 0:
                    pe.wait_ge(x2_ready[b - 1], C)
                pe.wait_ge(zeroed, 3)

                def scores(hg, u):
                    c, h = units[u]
                    n = unit_number(b, hg, u)
                    if not first(b, hg) or u >= AHEAD:
                        pe.wait_ge(sm_ready, n - AHEAD + 1)
                    pe.matmul(ps[:, S_BANKS[u % AHEAD], :], qkT[0][:, bass.ds(hg * HG + h, 1), c * P:(c + 1) * P],
                              qkT[1][:, bass.ds(hg * HG + h, 1), :], start=True, stop=True).then_inc(s_done, 1)

                def turn_probs(hg, u):
                    n = unit_number(b, hg, u)
                    pe.wait_ge(pr_ready, n + 1)
                    if not first(b, hg) or u >= 2:
                        pe.wait_ge(prT_copied[u % 2], (b * TURNS + hg) * (UNITS // 2) + u // 2)
                    for k in range(C):
                        mm = pe.transpose(ps[:, 2 + u % 2, k * P:(k + 1) * P], pr[u % 4][:, k * P:(k + 1) * P],
                                          ident[:, :])
                    mm.then_inc(prT_done, 1)

                def values(hg, c, half):
                    turn = hg + b * TURNS
                    if half == 0:
                        for par in range(2):
                            pe.wait_ge(prT_copied[par], turn * (UNITS // 2) + 2 * (c + 1))
                        if c == 0:
                            pe.wait_ge(v_cur_ready, turn + 1)
                            if not first(b, hg):
                                pe.wait_ge(onT_ready, turn)
                    for k in range(half * C // 2, (half + 1) * C // 2):
                        for h in range(HG):
                            mm = pe.matmul(ps[h * HP:(h + 1) * HP, 4, c * P:(c + 1) * P],
                                           v_cur[:, k, h, :], prT[c % 2][:, h, k, :],
                                           start=(k == 0), stop=(k == C - 1))
                    if half == 1:
                        mm.then_inc(pv_done, 1)
                        pe.wait_ge(rinv_ready, turn * 2 * C + 2 * c + 2)
                        pe.transpose(ps[:, 5, c * P:(c + 1) * P], rinv_w[:, c, :, :], ident[:, :]).then_inc(rT_done, 1)

                def late(hg, u):
                    for c in range(C):
                        for half in range(2):
                            if u == c * HG + LAG + half:
                                values(hg, c, half)

                def turn_body(hg):
                    if hg_is(hg, 0):
                        for u in range(AHEAD):
                            scores(hg, u)
                    for u in range(UNITS):
                        if u + AHEAD < UNITS:
                            scores(hg, u + AHEAD)
                        elif not hg_is(hg, TURNS - 1):
                            scores(hg + 1, u + AHEAD - UNITS)
                        turn_probs(hg, u)
                        late(hg, u)
                        if not hg_is(hg, 0):
                            late(hg - 1, u + UNITS)
                    if hg_is(hg, TURNS - 1):
                        for u in range(UNITS, UNITS + LAG):
                            late(hg, u)

                all_turns(pe, turn_body)

            def project_out(b):
                pe.wait_ge(onT_ready, (b + 1) * TURNS)
                for c in range(C):
                    for g in range(H // HG):
                        mm = pe.matmul(ps[:, 6 + c // 2, (c % 2) * D:(c % 2 + 1) * D], onT[:, g, c * P:(c + 1) * P],
                                       wo_pad[:, g, :], start=(g == 0), stop=(g == H // HG - 1))
                    mm.then_inc(wo_done[b], 1)

            def feed_forward(b):
                pe.wait_ge(hnT_ready[b], 2 * KD)
                for f in range(FB):
                    if f >= 2:
                        pe.wait_ge(gelu_ready[b], f - 1)
                    for k in range(KD):
                        mm = pe.matmul(ps[:, 4 + f % 2, :], w1_sb[:, k, f * P:(f + 1) * P], hnT[:, k, :],
                                       start=(k == 0), stop=(k == KD - 1))
                    mm.then_inc(h1_done[b], 1)
                pe.wait_ge(gelu_ready[b], FB)
                for c in range(C):
                    for f in range(FB):
                        mm = pe.matmul(ps[:, 0 + c // 2, (c % 2) * D:(c % 2 + 1) * D], hidden_sb[:, f, c * P:(c + 1) * P],
                                       w2_sb[:, f, :], start=(f == 0), stop=(f == FB - 1))
                    mm.then_inc(w2_done[b], 1)

            turn_hn(0, 0)
            project(0)
            turn_mask_rows(0)
            turn_mask_rows(1)
            pe.wait_ge(mT_ready[1], MS // P)
            turn_split(0)
            turn_mask_columns(0)
            pe.wait_ge(kT_ready, C * 2)
            turn_hn(1, 0)
            project(1)
            turn_mask_columns(1)
            for b in range(B):
                attention(b)
                project_out(b)
                turn_hn(b, C)
                if b < B - 1:
                    pe.wait_ge(hnT_ready[b], 2 * KD)
                    turn_split(b + 1)
                    pe.wait_ge(qT_ready, (b + 2) * C * 2)
                feed_forward(b)

        @block.scalar
        def _(act):
            act.wait_ge(wt_done, 1)
            for c in range(KD):
                act.copy(wgdT[:, c, :], ps[:, c, :]).then_inc(wt_copied, 1)
            act.copy(wcT[:, :], ps[0:N, 3, 0:D]).then_inc(wt_copied, 1)
            for b in range(B):
                with act.Fori(0, LOOPS) as i:
                    turn = i + b * LOOPS

                    def copy_xT(u):
                        j, G = u % 2, U * turn + u
                        for c in range(KD):
                            act.wait_ge(xT_done[c], G + 1)
                            if c == 0:
                                act.wait_ge(gd_done, 2 * G - 2 if u else 2 * G)
                            act.copy(xT[j][:, c, :], ps[:, c, :]).then_inc(xT_copied[j], 1)

                    def recurrence(u):
                        j = u % 2
                        act.wait_ge(ab_done, U * turn + u + 1)
                        act.wait_ge(h_ready[j], before(turn, u, j))
                        act.activation(a_sb[j][:, :].rearrange("n (p t) -> n t p", t=T),
                                       ps[0:N, 2, :].rearrange("n (t p) -> n t p", t=T),
                                       ACT.Tanh).then_inc(a_ready[j], 1)
                        act.copy(b_sb[j][:, :].rearrange("n (p t) -> n t p", t=T),
                                 ps[BROW:BROW + N, 2, :].rearrange("n (t p) -> n t p", t=T)).then_inc(b_ready[j], 1)

                    def gate(u, q):
                        n = 2 * (U * turn + u) + q
                        act.wait_ge(gd_done, n + 1)
                        act.wait_ge(dx_g_done, n - 1 if u else n - q)
                        act.wait_ge(rec_g_done, n - 1 if u else n - q)
                        act.activation(g_sb[q][:, :, :], ps[:, 3 + 2 * q:5 + 2 * q, 0:D],
                                       ACT.Sigmoid).then_inc(g_ready, 1)

                    copy_xT(0)
                    copy_xT(1)
                    recurrence(0)
                    for u in range(U):
                        gate(u, 0)
                        if u + 1 < U:
                            recurrence(u + 1)
                        gate(u, 1)
                        if u + 2 < U:
                            copy_xT(u + 2)

            def copy_hnT(b, first):
                for k in range(KD):
                    act.wait_ge(hnT_done[b], first + k + 1)
                    act.copy(hnT[:, k, :], ps[:, 2 + k, :]).then_inc(hnT_ready[b], 1)

            def copy_qk(b):
                for c in range(C):
                    act.wait_ge(qk_done[b], c + 1)
                    if b > 0:
                        act.wait_ge(e_ready, 2 * C * b)
                    act.copy(qk[:, c, :], ps[:, 4 + c % 2, :]).then_inc(qk_ready[b], 1)

            def sines(b):
                act.wait_ge(angle_ready[b], 1)
                act.activation(trig[b][:, 4, :, :], trig[b][:, 3, :, :], ACT.Sin)
                act.activation(trig[b][:, 5, :, :], trig[b][:, 3, :, :], ACT.Sin, scale=0.5).then_inc(sin_ready[b], 1)

            def copy_mask_rows(b):
                for n in range(MS // P):
                    act.wait_ge(mT_done[b], n + 1)
                    if n == MS // P // 2:
                        act.wait_ge(mT_stored[b], 16)
                    elif b > 0 and n == 0:
                        act.wait_ge(mT_stored[b - 1], 32)
                    act.mul(big2[:, n % (MS // P // 2), :], ps[:, n % 2, :], -1.0).then_inc(mT_ready[b], 1)

            def split(b):
                with act.Fori(0, C // 2) as i:
                    for e in range(2):
                        done = 2 * i + e + b * C
                        q, k = e_sb[e][:, 0, :, :, :], e_sb[e][:, 1, :, :, :]
                        h2 = e_sb[e][:, :, :, 0:1, :].broadcast_to((P, 2, H, 2, HD))
                        act.wait_ge(e_parts, 2 * done + 1)
                        act.copy(q[:, :, 2:5:2, :], h2[:, 0])
                        act.copy(k[:, :, 1:6:4, :], h2[:, 1])
                        act.wait_ge(e_parts, 2 * done + 2)
                        act.copy(q[:, :, 1, :], q[:, :, 3, :])
                        act.copy(k[:, :, 2, :], k[:, :, 3, :]).then_inc(e_ready, 1)
                        for half in range(2):
                            act.wait_ge(eT_done[half], done + 1)
                            act.copy(qkT[0][:, 8 * half:8 * half + 8, bass.ds((2 * i + e) * P, P)],
                                     ps[:, :, :].bitcast(BF16)[0:ER, half, :].rearrange("r (h n) -> r h n", h=8)
                                     ).then_inc(qT_ready, 1)

            def attention(b):
                def exponentials(hg, u):
                    c, h = units[u]
                    n = unit_number(b, hg, u)
                    act.wait_ge(sm_ready, n + 1)
                    if not first(b, hg) or u >= 4:
                        act.wait_ge(prT_done, n - 3)
                    if h == 0 and not first(b, hg):
                        act.wait_ge(rinv_ready, (hg + b * TURNS) * 2 * C - 2 * C + 2 * c + 1)
                    act.activation(pr[u % 4][:, 0:K - 1], sm[u % 4][:, 0:K - 1], ACT.Exp,
                                   bias=nmax[:, c, h:h + 1], scale=-1.0,
                                   accum_out=rsum[:, c, h:h + 1]).then_inc(pr_ready, 1)

                def copy_heads(hg):
                    turn = hg + b * TURNS
                    act.wait_ge(pv_done, turn * C + C)
                    if not first(b, hg):
                        act.wait_ge(onT_ready, turn)
                    act.copy(oT[:, :], ps[:, 4, :]).then_inc(oT_ready, 1)

                def turn_body(hg):
                    for u in range(UNITS):
                        exponentials(hg, u)
                        if u == 6 and not hg_is(hg, 0):
                            copy_heads(hg - 1)
                        if u % 2 == 0 and u >= 2:
                            copy_probs(act, act.copy, b, hg, u - 2)
                        elif u == 0 and not hg_is(hg, 0):
                            copy_probs(act, act.copy, b, hg - 1, UNITS - 2)
                    if hg_is(hg, TURNS - 1):
                        copy_probs(act, act.copy, b, hg, UNITS - 2)
                        copy_heads(hg)

                all_turns(act, turn_body)

            def hidden(b):
                for f in range(FB):
                    act.wait_ge(h1_done[b], f + 1)
                    if b > 0 and f == 0:
                        act.wait_ge(w2_done[b - 1], C)
                    act.activation(hidden_sb[:, f, :], ps[:, 4 + f % 2, :], ACT.Gelu_apprx_tanh).then_inc(gelu_ready[b], 1)

            copy_hnT(0, 0)
            copy_qk(0)
            sines(0)
            copy_mask_rows(0)
            copy_mask_rows(1)
            split(0)
            copy_hnT(1, 0)
            copy_qk(1)
            sines(1)
            for b in range(B):
                attention(b)
                copy_hnT(b, KD)
                if b < B - 1:
                    split(b + 1)
                hidden(b)

        @block.vector
        def _(dve):
            step = Steps(dve, dve_step)
            step.link(dve.memset(wabT[:, :, :], 0.0))
            dve.wait_ge(wt_done, 1)
            for m in range(2):
                dve.tensor_copy(wabT[:, :, m * BROW:m * BROW + N],
                                ps[:, 2, 0:128].rearrange("p (c w) -> p c w", c=2)[:, :, m * BROW:m * BROW + N]
                                ).then_inc(wt_copied, 1)
            dve.wait_ge(w_loaded, 16 * 9)
            dve.wait_ge(ident_ready, 2)
            step.link(dve.tensor_copy(bias_h[:, :], bias_row[:, :]))
            step.link(dve.tensor_tensor(bias_rest[:, :], bias_row[:, :], bias_h[:, :], ALU.subtract))
            step.link(dve.tensor_copy(bias_m[:, :], bias_rest[:, :]))
            step.link(dve.tensor_tensor(bias_row[:, :], bias_rest[:, :], bias_m[:, :], ALU.subtract))
            step.link(dve.tensor_copy(bias_l[:, :], bias_row[:, :]))
            step.link(dve.tensor_scalar(bias_rest[:, :], bias_h[:, :], ident[0:3, 0:1], None, ALU.mult))
            step.link(dve.scalar_tensor_tensor(bias_row[:, :], bias_m[:, :], ident[0:3, 1:2], bias_rest[:, :],
                                               ALU.mult, ALU.add))
            dve.scalar_tensor_tensor(bias3[:, :], bias_l[:, :], ident[0:3, 2:3], bias_row[:, :],
                                     ALU.mult, ALU.add).then_inc(const_ready, 1)

            dve.wait_ge(w2_loaded, 16 * (7 + HG))
            for k in range(KD):
                g1, g2 = ln_col[:, 0, k:k + 1], ln_col[:, 1, k:k + 1]
                dve.tensor_scalar(wqk[:, k, 0:D], wqk[:, k, 0:D], g1, -(HD ** -0.5), ALU.mult, ALU.mult)
                dve.tensor_scalar(wqk[:, k, D:2 * D], wqk[:, k, D:2 * D], g1, None, ALU.mult)
                dve.tensor_scalar(wv_sb[:, k, :], wv_sb[:, k, :], g1, None, ALU.mult)
                step.done(dve.tensor_scalar(w1_sb[:, k, :], w1_sb[:, k, :], g2, None, ALU.mult))
            dve.wait_ge(pool_const, 9 + HD // 2)
            dve.tensor_copy(ident_b[:, :], ident[:, :])
            dve.tensor_copy(hi_row[:, :], hi_i[:, :])
            dve.tensor_copy(lo_row[:, :], lo_i[:, :])
            for b in range(B):
                for n in range(3):
                    dve.tensor_copy(vals[:, b, :, n], pgt[:, n, :, :].rearrange("p g t -> p (g t)"))
            for r in range(ROUNDS):
                dve.tensor_scalar(digits[:, r, :], digit_i[:, :], 32 - DIGIT * (r + 1), None, ALU.logical_shift_left)
            step.link(dve.memset(prefix[:, :, :], 0))

            for b in range(B):
                if b > 0:
                    dve.wait_ge(rec_done, 2 * NG * b)
                step.link(dve.memset(h_sb[1][:, GT - 1:GT], 0.0))
                with dve.Fori(0, LOOPS) as i:
                    turn = i + b * LOOPS
                    step.enter(i, U * (3 * T + 2))

                    def scan(u):
                        j = u % 2
                        dve.wait_ge(a_ready[j], before(turn, u, j) + 1)
                        dve.wait_ge(b_ready[j], before(turn, u, j) + 1)
                        dve.wait_ge(h_ready[1 - j], before(turn, u, 1 - j))
                        dve.wait_ge(rec_done, 2 * (U * turn + u) - (2 if u else 0))
                        dve.tensor_tensor_scan(h_sb[j][:, :], a_sb[j][:, :], b_sb[j][:, :],
                                               h_sb[1 - j][:, GT - 1:GT], ALU.mult, ALU.add
                                               ).then_inc(h_ready[j], 1)

                    def products(u, q):
                        n = 2 * (U * turn + u) + q
                        dve.wait_ge(mixed, n - 1 if u else n - q)
                        dve.wait_ge(g_ready, n + 1)
                        dve.scalar_tensor_tensor(dx_g[q][:, :, :], g_sb[q][:, :, :], 1.0,
                                                 ps[:, 3 + 2 * q:5 + 2 * q, D:2 * D],
                                                 ALU.subtract, ALU.mult).then_inc(dx_g_done, 1)
                        dve.wait_ge(rec_done, n + 1)
                        dve.tensor_tensor(rec_g[q][:, :, :], ps[:, 7, :].rearrange("p (t d) -> p t d", t=2),
                                          g_sb[q][:, :, :], ALU.mult).then_inc(rec_g_done, 1)

                    def statistics(u):
                        j, G = u % 2, U * turn + u
                        dve.wait_ge(s_ready, 2 * (G + 1))
                        dve.wait_ge(pow2_ready, G - 1 if u else G)
                        for t in range(T):
                            last = step.done(dve.bn_stats(stats[j][:, t, :], s_sb[j][:, t, :]))
                        dve.wait_ge(dve_step, last)
                        dve.nop(nofuse=True)
                        for t in range(T):
                            last = step.done(dve.bn_aggr(mv[j][:, t, :], stats[j][:, t, :]))
                        dve.wait_ge(dve_step, last)
                        dve.tensor_scalar(small[j][:, 0, :], mv[j][:, :, 1], LN_EPS, None,
                                          ALU.add).then_inc(ve_ready, 1)

                    def normalise(u):
                        j, G = u % 2, U * turn + u
                        dve.wait_ge(pow_ready, G + 1)
                        step.link(dve.tensor_tensor(small[j][:, 2, :], mv[j][:, :, 1], small[j][:, 1, :], ALU.mult))
                        step.link(dve.tensor_tensor(small[j][:, 3, :], small[j][:, 2, :], small[j][:, 1, :], ALU.mult))
                        dve.tensor_scalar(small[j][:, 4, :], small[j][:, 3, :], LN_EPS / 4, None,
                                          ALU.add).then_inc(v2_ready, 1)
                        dve.wait_ge(x1_stored[b][j], 16 * before(i, u, j))
                        if b > 0:
                            dve.wait_ge(x1_stored[b - 1][j], 16 * NG // 2)
                        for t in range(T):
                            dve.tensor_scalar(x1_sb[j][:, t, :], s_sb[j][:, t, :], mv[j][:, t, 0:1],
                                              small[j][:, 1, t:t + 1], ALU.subtract, ALU.mult).then_inc(x1_ready, 1)

                    def route(u):
                        j, G = u % 2, U * turn + u
                        dve.wait_ge(x1_ready, (G + 1) * T)
                        for t in range(T):
                            last = step.done(dve.tensor_tensor_reduce(junk[:, j, t, :], x1_sb[j][:, t, :],
                                                                      rw_row[:, :], 1.0, 0.0, ALU.mult, ALU.add,
                                                                      logit[j][:, t:t + 1]))
                        dve.wait_ge(ob_stored[b][j], 16 * before(i, u, j))
                        if b > 0:
                            dve.wait_ge(ob_stored[b - 1][j], 16 * NG // 2)
                        dve.wait_ge(pow2_ready, G + 1)
                        for t in range(T):
                            dve.tensor_scalar(ob_sb[j][:, t, :], x1_sb[j][:, t, :], small[j][:, 5, t:t + 1], None,
                                              ALU.mult).then_inc(ob_ready, 1)
                        dve.wait_ge(dve_step, last)
                        dve.tensor_scalar(W[:, b, bass.ds(U * i + u, 1), :].rearrange("p a t -> p (a t)"),
                                          logit[j][:, :], rb_col[:, :], None, ALU.add).then_inc(W_ready, 1)

                    scan(0)
                    products(0, 0)
                    for u in range(U):
                        if u + 1 < U:
                            scan(u + 1)
                        products(u, 1)
                        if u:
                            normalise(u - 1)
                        if u + 1 < U:
                            products(u + 1, 0)
                        if u:
                            route(u - 1)
                        statistics(u)
                    normalise(U - 1)
                    route(U - 1)
                step.leave(LOOPS)

            dve.wait_ge(W_ready, B * NG)

            def floats(dst, key, m):
                step.link(dve.tensor_scalar(m, key, 31, -1, ALU.arith_shift_right, ALU.bitwise_xor))
                step.link(dve.scalar_tensor_tensor(dst, m, SIGN, key, ALU.bitwise_or, ALU.bitwise_xor))

            Wv = W[:, :, :, :].rearrange("p b g t -> p b (g t)")
            for r in range(ROUNDS):
                step.link(dve.tensor_tensor(cand[:, :, :], digits[:, r:r + 1, :].broadcast_to((P, B, CAND)),
                                            prefix[:, :, :].broadcast_to((P, B, CAND)), ALU.bitwise_or))
                floats(cand_f[:, :, :], cand[:, :, :], cand_m[:, :, :])
                for b in range(B):
                    last = step.done(dve.tensor_tensor(
                        geq[:, b, :, :], Wv[:, b:b + 1, :].broadcast_to((P, CAND, NG * T)),
                        cand_f[:, b, :].bitcast(F32).rearrange("p (c o) -> p c o", o=1).broadcast_to((P, CAND, NG * T)),
                        ALU.is_ge))
                dve.wait_ge(dve_step, last)
                with nc.allow_low_precision("counts to 32"):
                    dve.tensor_reduce(cnt[:, :], geq[:, :, :, :].rearrange("p b c n -> p (b c) n"), X,
                                      ALU.add).then_inc(cnt_ready, 1)
                dve.wait_ge(cnt_sum, r + 1)
                step.link(dve.tensor_scalar(enough[:, :, :].rearrange("p b c -> p (b c)"), ps[:, 0, 0:B * CAND],
                                            float(K), None, ALU.is_ge))
                with nc.allow_low_precision("counts to 15"):
                    step.link(dve.tensor_reduce(found[:, :], enough[:, :, :], X, ALU.add))
                step.link(dve.tensor_scalar(found[:, :], found[:, :], 32 - DIGIT * (r + 1), None,
                                            ALU.logical_shift_left))
                step.link(dve.tensor_tensor(prefix[:, :, 0], found[:, :], prefix[:, :, 0], ALU.bitwise_or))
            floats(thr[:, :, :], prefix[:, :, :], cand_m[:, :, 0:1])
            thr_f = thr[:, :, :].bitcast(F32)

            thr_w = thr_f.broadcast_to((P, B, NG * T))
            fl = flags[:, :, :, :, :].rearrange("p k b g t -> p k b (g t)")
            dve.tensor_tensor(fl[:, 0], Wv, thr_w, ALU.is_gt)
            step.link(dve.tensor_tensor(fl[:, 1], Wv, thr_w, ALU.is_equal))
            with nc.allow_low_precision("counts to 4"):
                dve.tensor_reduce(fcnt[:, :, :, :].rearrange("p k b g -> p (k b g)"),
                                  flags[:, :, :, :, :].rearrange("p k b g t -> p (k b g) t"), X,
                                  ALU.add).then_inc(fcnt_ready, 1)
            v = vals[:, :, :, :]
            step.link(dve.tensor_copy(v[:, :, :, 3], Wv))
            step.link(dve.tensor_tensor(w_rest[:, 0], Wv, v[:, :, :, 3], ALU.subtract))
            step.link(dve.tensor_copy(v[:, :, :, 4], w_rest[:, 0]))
            step.link(dve.tensor_tensor(w_rest[:, 1], w_rest[:, 0], v[:, :, :, 4], ALU.subtract))
            step.link(dve.tensor_copy(v[:, :, :, 5], w_rest[:, 1]))
            dve.wait_ge(fcnt_sum, 1)
            step.link(dve.tensor_copy(ftot[:, :, :, :].rearrange("p k b g -> p (k b g)"), ps[:, 2, 0:32]))
            for k in range(2):
                for b in range(B):
                    last = step.done(dve.tensor_tensor_scan(fscan[:, k, b, :], ftot[:, k, b, :], zeros[:, :], 0.0,
                                                            ALU.add, ALU.add))
            dve.wait_ge(dve_step, last)
            last_gt = fscan[:, 0, :, NG - 1:NG]
            step.done(dve.tensor_scalar(room[:, :, :], last_gt, -1.0, float(K - 1), ALU.mult, ALU.add))
            step.link(dve.tensor_tensor(ftot[:, :, :, :], fscan[:, :, :, :], ftot[:, :, :, :], ALU.subtract))
            rk = rank[:, :, :, :, :].rearrange("p k b g t -> p (k b g) t")
            fr = flags[:, :, :, :, :].rearrange("p k b g t -> p (k b g) t")
            step.link(dve.tensor_tensor(rk[:, :, 0], ftot[:, :, :, :].rearrange("p k b g -> p (k b g)"),
                                        ps[:, 1, 0:32], ALU.add))
            for t in range(1, T):
                step.link(dve.tensor_tensor(rk[:, :, t], rk[:, :, t - 1], fr[:, :, t - 1], ALU.add))
            rf = rank[:, :, :, :, :].rearrange("p k b g t -> p k b (g t)")
            room_w = room[:, :, :].broadcast_to((P, B, NG * T))
            step.link(dve.tensor_tensor(sel[:, 0], rf[:, 1], room_w, ALU.is_lt))
            step.link(dve.tensor_tensor(sel[:, 0], sel[:, 0], fl[:, 1], ALU.mult))
            step.link(dve.tensor_tensor(sel[:, 0], sel[:, 0], fl[:, 0], ALU.add))
            step.link(dve.tensor_tensor(sel[:, 1], rf[:, 1], room_w, ALU.min))
            step.link(dve.tensor_tensor(sel[:, 1], sel[:, 1], rf[:, 0], ALU.add))
            step.link(dve.tensor_scalar(sel[:, 2], sel[:, 0], -float(K), float(K), ALU.mult, ALU.add))
            step.link(dve.tensor_tensor(slot_i[:, 0], sel[:, 2], sel[:, 1], ALU.add))
            step.done(dve.tensor_scalar(slot_i[:, 1], slot_i[:, 0], 2, None, ALU.arith_shift_right))
            step.link(dve.tensor_scalar(slot_i[:, 2], slot_i[:, 0], C - 1, None, ALU.bitwise_and))
            step.link(dve.tensor_copy(slot_f[:, :, :, :], slot_i[:, 1:3, :, :]))
            step.link(dve.tensor_tensor(
                at_lo[:, :, :, :].rearrange("p b n c -> p (b n) c"),
                slot_f[:, 1].rearrange("p b (n o) -> p (b n) o", o=1).broadcast_to((P, B * NG * T, C)),
                lo_row[:, :].rearrange("p (o c) -> p o c", o=1).broadcast_to((P, B * NG * T, C)), ALU.is_equal))
            dve.tensor_tensor(
                lo_vals[:, :, :, :, :].rearrange("p b n c v -> p (b n) c v"),
                at_lo[:, :, :, :].rearrange("p b n (c o) -> p (b n) c o", o=1).broadcast_to((P, B * NG * T, C, VALS)),
                vals[:, :, :, :].rearrange("p b (n o) v -> p (b n) o v", o=1).broadcast_to((P, B * NG * T, C, VALS)),
                ALU.mult).then_inc(lo_ready, 1)
            for b in range(B):
                dve.tensor_tensor(
                    at_hi[:, b], slot_f[:, 0, b, :].rearrange("p (n o) -> p n o", o=1).broadcast_to((P, NG * T, P)),
                    hi_row[:, :].rearrange("p (o h) -> p o h", o=1).broadcast_to((P, NG * T, P)),
                    ALU.is_equal).then_inc(at_ready[b], 1)
            dve.wait_ge(picked_done, B)
            step.link(dve.tensor_copy(picked[:, :, :, :].rearrange("p b c v -> p b (c v)"), ps[:, 3:5, 0:C * VALS]))
            pk = picked[:, :, :, :]
            step.link(dve.scalar_tensor_tensor(pick_f[:, 0], pk[:, :, :, 0], float(T), pk[:, :, :, 2],
                                               ALU.mult, ALU.add))
            step.link(dve.scalar_tensor_tensor(pick_f[:, 1], pk[:, :, :, 1], float(GT), pick_f[:, 0],
                                               ALU.mult, ALU.add))
            step.done(dve.tensor_scalar(pick_f[:, 2], pick_f[:, 1], float(MS - 1), None, ALU.min))
            step.link(dve.tensor_tensor(pick_f[:, 3], pk[:, :, :, 3], pk[:, :, :, 4], ALU.add))
            step.link(dve.tensor_tensor(w_sel[:, :, :], pick_f[:, 3], pk[:, :, :, 5], ALU.add))
            for b in range(B):
                dve.tensor_scalar(row_x[:, b, :], pick_f[:, 1, b, :], float(b * S), None, ALU.add).then_inc(rows_ready, 1)
                dve.tensor_scalar(row_m[:, b, :], pick_f[:, 2, b, :], float(b * MS), None, ALU.add).then_inc(rows_ready, 1)
            step.done(dve.tensor_copy(row_t[:, :, :], pick_f[:, 2]))
            step.link(dve.tensor_tensor(not_m[:, :, :], w_sel[:, :, :], thr_f.broadcast_to((P, B, C)), ALU.is_le))

            def mean_square(b, sums, out_):
                for c in range(C):
                    last = step.done(dve.tensor_tensor_reduce(
                        rope_a[:, c // 2, (c % 2) * D:(c % 2 + 1) * D], x_sel[b][:, c, :], x_sel[b][:, c, :], 1.0, 0.0, ALU.mult, ALU.add,
                        ms[b][:, sums, c:c + 1]))
                dve.wait_ge(dve_step, last)
                dve.tensor_scalar(ms[b][:, out_, :], ms[b][:, sums, :], 1.0 / D, RMS_EPS, ALU.mult,
                                  ALU.add).then_inc(ms_ready[b], 1)

            def normalised(b, col, n):
                dve.wait_ge(rms_ready[b], n)
                for c in range(C):
                    dve.tensor_scalar(hn[:, c, :], x_sel[b][:, c, :], ms[b][:, col, c:c + 1], None,
                                      ALU.mult).then_inc(hn_ready[b], 1)

            def angles(b):
                tr = trig[b]
                dve.wait_ge(pos_in_s[b], 16 * C)
                step.link(dve.tensor_copy(pos_f[:, b, :], pos_i[:, b, :]))
                step.link(dve.tensor_tensor(
                    tr[:, 0, :, :], pos_f[:, b, :].rearrange("p (c o) -> p c o", o=1).broadcast_to((P, C, HD // 2)),
                    inv_f[:, :].rearrange("p (o k) -> p o k", o=1).broadcast_to((P, C, HD // 2)), ALU.mult))
                step.link(dve.tensor_scalar(tr[:, 1], tr[:, 0], 1.0 / (2 * np.pi), MAGIC, ALU.mult, ALU.add))
                step.link(dve.tensor_scalar(tr[:, 2], tr[:, 1], MAGIC, None, ALU.subtract))
                step.link(dve.scalar_tensor_tensor(tr[:, 1], tr[:, 2], -PI2_A, tr[:, 0], ALU.mult, ALU.add))
                step.link(dve.scalar_tensor_tensor(tr[:, 0], tr[:, 2], -PI2_B, tr[:, 1], ALU.mult, ALU.add))
                step.link(dve.scalar_tensor_tensor(tr[:, 1], tr[:, 2], -PI2_C, tr[:, 0], ALU.mult, ALU.add))
                dve.tensor_scalar(tr[:, 3], tr[:, 1], PI_MAX, -PI_MAX, ALU.min, ALU.max).then_inc(angle_ready[b], 1)

            def values(b):
                for c in range(C):
                    dve.wait_ge(v_done[b], c + 1)
                    dve.tensor_copy(v_sb[b][:, c, :], ps[:, 6 + c % 2, 0:D]).then_inc(v_ready[b], 1)

            def rope(b):
                tr = trig[b]
                dve.wait_ge(sin_ready[b], 1)
                step.link(dve.tensor_tensor(tr[:, 6], tr[:, 5], tr[:, 5], ALU.mult))
                step.link(dve.tensor_scalar(tr[:, 7], tr[:, 6], -2.0, 1.0, ALU.mult, ALU.add))
                hs = lambda ap: ap.rearrange("p (h z k) -> p h z k", z=2, k=HD // 2)
                for c in range(C):
                    dve.wait_ge(qk_ready[b], c + 1)
                    cos = tr[:, 7, c:c + 1, :].rearrange("p (o z) k -> p o z k", z=1)
                    sin = tr[:, 4, c:c + 1, :]
                    a, r, q = hs(rope_a[:, c % 2, :]), hs(rope_b[:, c % 2, :]), hs(qk[:, c, :])
                    if c >= 2:
                        dve.wait_ge(rope_ready[b], c - 1)
                    dve.tensor_tensor(a, q, cos.broadcast_to((P, 2 * H, 2, HD // 2)), ALU.mult)
                    for z in range(2):
                        last = step.done(dve.tensor_tensor(r[:, :, z], q[:, :, 1 - z],
                                                           sin.broadcast_to((P, 2 * H, HD // 2)), ALU.mult))
                    dve.wait_ge(dve_step, last)
                    dve.tensor_tensor(q[:, :, 0], a[:, :, 0], r[:, :, 0], ALU.subtract)
                    dve.tensor_tensor(q[:, :, 1], a[:, :, 1], r[:, :, 1], ALU.add).then_inc(rope_ready[b], 1)

            def copy_mask(b):
                for c in range(C):
                    dve.wait_ge(nm_done[b], c + 1)
                    dve.tensor_copy(nmask[b][:, c, :], ps[:, c % 2, :]).then_inc(nm_ready[b], 1)


            def split(b):
                with dve.Fori(0, C // 2) as i:
                    step.enter(i, 2 * 2)
                    for e in range(2):
                        done = 2 * i + e + b * C
                        for n in range(4):
                            dve.wait_ge(eT_done[n], 2 * i + b * C)
                        src = qk[:, bass.ds(2 * i + e, 1), :].rearrange("p o (m h k) -> p (o m) h k", m=2, h=H)
                        es = e_sb[e]
                        rest = e_rest[:, e, :].rearrange("p (m h k) -> p m h k", m=2, h=H)
                        if e == 0:
                            dve.wait_ge(rope_ready[b], C)
                        dve.wait_ge(e_ready, 2 * (2 * i + b * C))
                        dve.tensor_copy(es[:, :, :, 0, :], src).then_inc(e_parts, 1)
                        dve.wait_ge(e_parts, 2 * done + 1)
                        step.link(dve.tensor_tensor(rest, src, es[:, :, :, 0, :], ALU.subtract))
                        dve.tensor_copy(es[:, :, :, 3, :], rest).then_inc(e_parts, 1)
                        dve.wait_ge(e_parts, 2 * done + 2)
                        step.done(dve.tensor_tensor(es[:, 0, :, 5, :], rest[:, 0], es[:, 0, :, 3, :], ALU.subtract))
                        dve.tensor_tensor(es[:, 1, :, 4, :], rest[:, 1], es[:, 1, :, 3, :],
                                          ALU.subtract).then_inc(e_ready, 1)
                        for half in range(2):
                            dve.wait_ge(eT_done[2 + half], done + 1)
                            dve.tensor_copy(qkT[1][:, 8 * half:8 * half + 8, bass.ds((2 * i + e) * P, P)],
                                            ps[:, :, :].bitcast(BF16)[0:ER, 2 + half, :].rearrange(
                                                "r (h n) -> r h n", h=8)).then_inc(kT_ready, 1)
                step.leave(C // 2)

            def attention(b):
                if b > 0:
                    dve.wait_ge(wo_done[b - 1], C)

                def masked(hg, u):
                    c, h = units[u]
                    n = unit_number(b, hg, u)
                    dve.wait_ge(s_done, n + 1)
                    if not first(b, hg) or u >= 4:
                        dve.wait_ge(pr_ready, n - 3)
                    dve.nop(nofuse=True)
                    dve.tensor_tensor_reduce(sm[u % 4][:, 0:K - 1], ps[:, S_BANKS[u % AHEAD], 0:K - 1],
                                             nmask[b][:, c, 0:K - 1], 1.0, 3.4e38, ALU.add, ALU.min,
                                             nmax[:, c, h:h + 1]).then_inc(sm_ready, 1)

                def inverses(hg, c):
                    turn = hg + b * TURNS
                    dve.wait_ge(pr_ready, turn * UNITS + HG * (c + 1))
                    dve.reciprocal(rinv[:, c, :], rsum[:, c, :]).then_inc(rinv_ready, 1)
                    if not first(b, hg):
                        dve.wait_ge(rT_done, turn * C - C + c + 1)
                    dve.wait_ge(rinv_ready, turn * 2 * C + 2 * c + 1)
                    dve.tensor_copy(rinv_w[:, c, :, :], rinv[:, c, :].rearrange("p (h o) -> p h o", o=1)
                                    .broadcast_to((P, HG, HP))).then_inc(rinv_ready, 1)

                def normalise_heads(hg):
                    turn = hg + b * TURNS
                    dve.wait_ge(rT_done, turn * C + C)
                    dve.wait_ge(oT_ready, turn + 1)
                    dve.tensor_tensor(onT[:, bass.ds(hg, 1), :].rearrange("p o n -> p (o n)"), oT[:, :], ps[:, 5, :],
                                      ALU.mult).then_inc(onT_ready, 1)

                def late(hg, u):
                    if (u - 3) % 2 and 0 <= u - 3 < UNITS:
                        copy_probs(dve, dve.tensor_copy, b, hg, u - 3)
                    if (u - 5) % HG == 0 and 0 <= (u - 5) // HG < C:
                        inverses(hg, (u - 5) // HG)
                    if u == UNITS + 7:
                        normalise_heads(hg)

                def turn_body(hg):
                    for u in range(UNITS):
                        masked(hg, u)
                        late(hg, u)
                        if not hg_is(hg, 0):
                            late(hg - 1, u + UNITS)
                    if hg_is(hg, TURNS - 1):
                        for u in range(UNITS, 2 * UNITS):
                            late(hg, u)

                all_turns(dve, turn_body)

            def residual(b):
                for c in range(C):
                    dve.wait_ge(wo_done[b], c // 2 * 2 + 2)
                    last = step.done(dve.tensor_tensor(x_sel[b][:, c, :], x_sel[b][:, c, :],
                                                       ps[:, 6 + c // 2, (c % 2) * D:(c % 2 + 1) * D], ALU.add))
                dve.wait_ge(dve_step, last)

            def second_sum(b):
                for c in range(C):
                    dve.wait_ge(w2_done[b], c // 2 * 2 + 2)
                    dve.tensor_tensor(x_sel[b][:, c, :], x_sel[b][:, c, :],
                                      ps[:, c // 2, (c % 2) * D:(c % 2 + 1) * D], ALU.add).then_inc(x2_ready[b], 1)

            def finish(b):
                dve.wait_ge(x2_ready[b], C)
                for c in range(C):
                    last = step.done(dve.scalar_tensor_tensor(keep[b][:, c, :], x_sel[b][:, c, :], w_sel[:, b, c:c + 1],
                                                              keep[b][:, c, :], ALU.mult, ALU.add))
                dve.wait_ge(dve_step, last)
                for c in range(C):
                    last = step.done(dve.bn_stats(stat2[:, c, :], keep[b][:, c, :]))
                dve.wait_ge(dve_step, last)
                for c in range(C):
                    last = step.done(dve.bn_aggr(mv2[:, c, :], stat2[:, c, :]))
                dve.wait_ge(dve_step, last)
                dve.tensor_scalar(ms[b][:, 1, :], mv2[:, :, 1], LN_EPS, None, ALU.add).then_inc(ve2_ready[b], 1)
                dve.wait_ge(pow3_ready[b], 1)
                for c in range(C):
                    dve.tensor_scalar(x_sel[b][:, c, :], keep[b][:, c, :], mv2[:, c, 0:1], ms[b][:, 2, c:c + 1],
                                      ALU.subtract, ALU.mult).then_inc(fin_ready[b], 1)

            def kept(b):
                for bb in range(B):
                    dve.wait_ge(ob_stored[bb][b], 16 * NG // 2)
                for c in range(C):
                    last = step.done(dve.scalar_tensor_tensor(keep[b][:, c, :], x_sel[b][:, c, :], not_m[:, b, c:c + 1],
                                                              x_sel[b][:, c, :], ALU.mult, ALU.add))

            dve.wait_ge(x_sel_in[0], 16 * C)
            mean_square(0, 0, 1)
            kept(0)
            normalised(0, 2, 1)
            values(0)
            angles(0)
            rope(0)
            dve.wait_ge(rope_ready[0], C)
            dve.wait_ge(x_sel_in[1], 16 * C)
            mean_square(1, 0, 1)
            kept(1)
            split(0)
            dve.wait_ge(hnT_done[0], KD)
            normalised(1, 2, 1)
            copy_mask(0)
            values(1)
            angles(1)
            rope(1)
            copy_mask(1)
            for b in range(B):
                attention(b)
                residual(b)
                mean_square(b, 3, 4)
                normalised(b, 5, 2)
                if b < B - 1:
                    split(b + 1)
                    second_sum(b)
            finish(0)
            second_sum(1)
            finish(1)


_INS = ['L0_attn_x', 'L0_attn_WA', 'L0_attn_WB', 'L0_attn_WC', 'L0_attn_WD', 'L0_attn_bD', 'L0_attn_Wg', 'L0_attn_bg',
        'L0_ffn_attention_mask', 'L0_ffn_position_ids', 'L0_ffn_router_w', 'L0_ffn_router_b', 'L0_ffn_wq', 'L0_ffn_wk',
        'L0_ffn_wv', 'L0_ffn_wo', 'L0_ffn_w1', 'L0_ffn_w2', 'L0_ffn_ln1', 'L0_ffn_ln2']


def kernel(**inputs):
    import concourse.bacc as bacc
    from concourse.bass_utils import run_bass_kernel_spmd

    nc = bacc.Bacc("TRN2", target_bir_lowering=False, num_devices=1)
    arrays, args = {}, []
    for name in _INS:
        a = np.ascontiguousarray(inputs[name])
        arrays[f"in_{name}"] = a
        args.append(nc.dram_tensor(f"in_{name}", a.shape, mybir.dt.from_np(a.dtype), kind="ExternalInput").ap())
    out = nc.dram_tensor("out", (B, S, D), F32, kind="ExternalOutput").ap()
    build(nc, *args, out)
    r = run_bass_kernel_spmd(nc, [arrays], core_ids=[0])
    return r.results[0]["out"]
```

```python
from contextlib import ExitStack

import numpy as np

import concourse.bass as bass
from concourse import mybir

ALU = mybir.AluOpType
ACT = mybir.ActivationFunctionType
F32 = mybir.dt.float32
BF16 = mybir.dt.bfloat16
F32R = mybir.dt.float32r
I32 = mybir.dt.int32
X = mybir.AxisListType.X

P = 128
B, S, D = 2, 4096, 256
N = 16
F = 1024
H, HD = 16, 16
KD = D // P
T = 4
GT = T * P
NG = S // GT
U = 4
LOOPS = B * NG // U
BROW = 64
BIAS_K = 33
HROWS = 3 * N
K = S // 8
MS = 1024
C = K // P
LN_EPS = 1e-5
RMS_EPS = 1e-6
ROPE_BASE = 10000.0
DIGIT = 4
CAND = 2 ** DIGIT - 1
ROUNDS = 32 // DIGIT
VALS = 6
SLOTS = 6
ER = SLOTS * HD
HG = 4
HP = 32
TURNS = H // HG
UNITS = C * HG
M_STORES = MS // P
AHEAD = 4
S_BANKS = (0, 1, 6, 7)
M_BANKS = (4, 6, 5, 7)
O_BANKS = (0, 1, 6, 7)
LAG = 7
PARTS = ((range(C),), (range(2), range(2, 3), range(3, C)))
FB = F // P
SIGN = -2 ** 31
MAGIC = 1.5 * 2.0 ** 23
PI2_A = 6.28125
PI2_B = float(np.float32(2 * np.pi - PI2_A).view(np.uint32).__and__(np.uint32(0xFFFFF000)).view(np.float32))
PI2_C = float(2 * np.pi - PI2_A - PI2_B)
PI_MAX = float(np.nextafter(np.float32(np.pi), np.float32(0)))
INV_FREQ = [float(v) for v in np.float32(1.0) / np.power(np.float32(ROPE_BASE), np.arange(0, HD, 2, dtype=np.float32) / np.float32(HD))]


def before(turn, u, j):
    return turn * (U // 2) + (u + 1 - j) // 2


class Steps:

    def __init__(self, eng, sem):
        self.eng, self.sem, self.base, self.k, self.reg, self.per = eng, sem, 0, 0, None, 0

    def value(self):
        at = self.base + self.k
        return at if self.reg is None else self.reg * self.per + at

    def done(self, ins):
        self.k += 1
        ins.then_inc(self.sem, 1)
        return self.value()

    def link(self, ins):
        self.eng.wait_ge(self.sem, self.done(ins))

    def enter(self, reg, per):
        self.base, self.k, self.reg, self.per = self.base + self.k, 0, reg, per

    def leave(self, trips):
        assert self.k == self.per, (self.k, self.per)
        self.base, self.k, self.reg = self.base + trips * self.per, 0, None


def build(nc, x_in, WA, WB, WC, WD, bD, Wg, bg, mask_in, pos_in, router_w, router_b,
          wq, wk, wv, wo, w1, w2, ln1, ln2, out):
    with ExitStack() as ctx:
        def sb(name, shape, dt=F32):
            return ctx.enter_context(nc.sbuf_tensor(name, shape, dt))

        def under(*tensors):
            with ExitStack() as inner:
                return [inner.enter_context(nc.sbuf_tensor(*t)) for t in tensors]

        def sem(name):
            return ctx.enter_context(nc.semaphore(name))

        def sems(name, n=2):
            return [sem(f"{name}{i}") for i in range(n)]

        mt_dram = [nc.dram_tensor(f"mt_scratch{b}", (MS, K), F32, kind="Internal").ap() for b in range(B)]
        x1_dram = nc.dram_tensor("x1_scratch", (B * S, D), F32, kind="Internal").ap()

        ps = ctx.enter_context(nc.psum_tensor("ps", [P, 8, 512], F32))

        ident = sb("ident", [P, P])
        h_parts = under(*[(f"h_parts{j}", [HROWS, GT], F32R) for j in range(2)])
        nmask = [sb("nmask0", [P, C, K])]
        wgd_lo, = under(("wgd_lo", [P, KD, 2 * D], F32R))
        nmask.append(sb("nmask1", [P, C, K]))
        early = [m[:, :, :].rearrange("p c k -> p (c k)") for m in nmask]
        wraw = early[1][:, 0:4 * D].rearrange("p (m h d) -> p m h d", m=2, h=2)
        wab_raw = early[1][0:N, 4 * D:6 * D].rearrange("p (m d) -> p m d", m=2)
        wc_raw = early[1][:, 6 * D:6 * D + 2 * HROWS].rearrange("p (h n) -> p h n", h=2)
        wgd_hi, = under(("wgd_hi", [P, KD, 2 * D], F32R))
        hn = sb("hn", [P, C, D])
        wab_hi, wab_lo = (sb(f"wab_{n}", [P, KD, 2 * BROW], F32R) for n in ("hi", "lo"))
        wc = sb("wc", [HROWS, D], F32R)
        wc_hi = early[0][0:HROWS, 7 * D:8 * D].bitcast(F32R)
        wc_lo = early[1][0:HROWS, 6 * D + 2 * HROWS:7 * D + 2 * HROWS]
        is_lo = sb("is_lo", [HROWS, 2])
        bias_row = early[0][0:BIAS_K, 0:2 * D]
        ones_k = sb("ones_k", [BIAS_K, P], F32R)
        rw_row = sb("rw_row", [P, D])
        rb_col = sb("rb_col", [P, 1])
        minus_half = sb("minus_half", [P, T])

        x_hi = under(*[(f"x_hi{j}", [P, KD, GT], F32R) for j in range(2)])
        arena = sb("arena", [P, (U + 4) * T * D])
        x_sb = [arena[:, (u + 2) * T * D:(u + 3) * T * D].rearrange("p (t d) -> p t d", t=T) for u in range(U)]
        s_sb = [arena[:, (U + 2 + j) * T * D:(U + 3 + j) * T * D].rearrange("p (t d) -> p t d", t=T) for j in range(2)]
        arena2 = sb("arena2", [P, 9216])
        a_sb, b_sb, h_sb = ([arena2[0:HROWS, 4096 + (2 * n + j) * GT:4096 + (2 * n + j + 1) * GT] for j in range(2)]
                            for n in range(3))
        g_sb, rec_g, dx_g, mix = ([arena2[:, (2 * n + q) * 2 * D:(2 * n + q + 1) * 2 * D].rearrange(
            "p (t d) -> p t d", t=2) for q in range(2)] for n in range(4))
        x1_sb = [sb(f"x1_sb{j}", [P, T, D]) for j in range(2)]
        ob_sb = [sb(f"ob_sb{j}", [P, T, D]) for j in range(2)]
        stats = [sb(f"stats{j}", [P, T, 6]) for j in range(2)]
        mv = [sb(f"mv{j}", [P, T, 2]) for j in range(2)]
        small = [sb(f"small{j}", [P, 8, T]) for j in range(2)]
        junk = arena2[:, 7168:9216].rearrange("p (j t d) -> p j t d", j=2, t=T)
        logit = [sb(f"logit{j}", [P, T]) for j in range(2)]
        zero_state = sb("zero_state", [HROWS, 1])
        next_state = sb("next_state", [HROWS, 1], I32)
        going_on = sb("going_on", [HROWS, LOOPS], I32)
        W = sb("W", [P, B, NG, T])

        ident_b = sb("ident_b", [P, P], BF16)
        ones_b = sb("ones_b", [P, P], BF16)
        below_b = sb("below_b", [P, P], BF16)
        digit_i = sb("digit_i", [P, CAND], I32)
        digits = sb("digits", [P, ROUNDS, CAND], I32)
        hi_i = sb("hi_i", [P, P], I32)
        hi_row = sb("hi_row", [P, P], BF16)
        lo_i = sb("lo_i", [P, C], I32)
        lo_row = sb("lo_row", [P, C])
        pgt = sb("pgt", [P, 3, NG, T], I32)
        vals = sb("vals", [P, B, NG * T, VALS], BF16)
        cand = sb("cand", [P, B, CAND], I32)
        cand_m = sb("cand_m", [P, B, CAND], I32)
        cand_f = sb("cand_f", [P, B, CAND], I32)
        geq = sb("geq", [P, B, CAND, NG * T], BF16)
        cnt = sb("cnt", [P, B * CAND], BF16)
        enough = sb("enough", [P, B, CAND])
        found = sb("found", [P, B, 1], I32)
        thr = sb("thr", [P, B, 1], I32)
        flags = sb("flags", [P, 2, B, NG, T])
        fcnt = sb("fcnt", [P, 2, B, NG], BF16)
        ftot = sb("ftot", [P, 2, B, NG])
        fscan = sb("fscan", [P, 2, B, NG])
        zeros = sb("zeros", [P, NG])
        rank = sb("rank", [P, 2, B, NG, T])
        room = sb("room", [P, B, 1])
        sel = sb("sel", [P, 4, B, NG * T])
        slot_i = sb("slot_i", [P, 3, B, NG * T], I32)
        slot_f = sb("slot_f", [P, 2, B, NG * T])
        w_rest = sb("w_rest", [P, 2, B, NG * T])
        at_lo = sb("at_lo", [P, B, NG * T, C])
        lo_vals = sb("lo_vals", [P, B, NG * T, C, VALS], BF16)
        picked = sb("picked", [P, B, C, VALS])
        pick_f = sb("pick_f", [P, 4, B, C])
        w_sel = sb("w_sel", [P, B, C])
        not_m = sb("not_m", [P, B, C])
        row_x = sb("row_x", [P, B, C], I32)
        row_m = sb("row_m", [P, B, C], I32)
        row_t = sb("row_t", [P, B, C], I32)

        wqk = sb("wqk", [P, KD, 2 * D])
        wv_sb = sb("wv_sb", [P, KD, D])
        wo_pad = sb("wo_pad", [P, H // HG, D])
        w1_sb = sb("w1_sb", [P, KD, F])
        w2_sb = sb("w2_sb", [P, FB, D])
        ln_col = sb("ln_col", [P, 2, KD])
        q_gain = sb("q_gain", [P, KD])
        inv_f = sb("inv_f", [P, HD // 2])
        x_sel, keep = x1_sb, ob_sb
        pos_i = sb("pos_i", [P, B, C], I32)
        pos_f = sb("pos_f", [P, B, C])
        trig = [sb(f"trig{b}", [P, 8, C, HD // 2]) for b in range(B)]
        x_lo = under(*[(f"x_lo{j}", [P, KD, GT], F32R) for j in range(2)])
        big = sb("big", [P, C * MS])
        at_hi = big[:, :].bitcast(BF16).rearrange("p (b n h) -> p b n h", b=B, h=P)
        m_rows = [m[:, 0:C * MS].rearrange("p (c s) -> p c s", c=C) for m in (big, arena)]
        m_k = [arena2[:, 2048:4096].rearrange("p (c k) -> p c k", c=C), nmask[1]]
        prT = [big[:, n * 2048:(n + 1) * 2048].rearrange("p (h c n) -> p h c n", h=HG, c=C) for n in range(2)]
        hidden_sb = big[:, :].rearrange("p (f n) -> p f n", f=FB)
        m_turned = [[early[n // 4][:, n % 4 * K:(n % 4 + 1) * K] for n in range(MS // P)],
                    [big[:, n * K:(n + 1) * K] for n in range(MS // P)]]
        ms = [sb(f"ms{b}", [P, 6, C]) for b in range(B)]
        hnT = sb("hnT", [P, KD, K])
        qk = [sb(f"qk{b}", [P, C, 2 * D]) for b in range(B)]
        bias_parts, = under(("bias_parts", [BIAS_K, 2 * D], F32R))
        onT = sb("onT", [P, H // HG, K])
        rope_a, rope_b = (arena2[:, n * 1024:(n + 1) * 1024].rearrange("p (c n) -> p c n", c=2) for n in range(2))
        v_sb = [sb(f"v_sb{b}", [P, C, D]) for b in range(B)]
        e_rest = arena2[:, 4096:5120].rearrange("p (e n) -> p e n", e=2)
        e_sb = [arena2[:, 5120 + e * 1536:6656 + e * 1536].bitcast(BF16).rearrange(
            "p (m h s k) -> p m h s k", m=2, h=H, s=SLOTS) for e in range(2)]
        qkT = [arena[:, 4096 * m:4096 * (m + 1)].bitcast(BF16)[0:ER, 0:H * K].rearrange("r (h n) -> r h n", h=H)
               for m in range(2)]
        v_cur = arena2[:, 8704:9216].rearrange("p (c h w) -> p c h w", c=C, h=HG)
        sm = [arena2[:, n * K:(n + 1) * K] for n in range(4)]
        pr = [arena2[:, 2048 + n * K:2048 + (n + 1) * K] for n in range(4)]
        oT = arena2[:, 8192:8704]
        nmax = sb("nmax", [P, C, HG])
        rinv = sb("rinv", [P, C, HG])
        rsum = sb("rsum", [P, C, HG])
        rinv_w = arena2[:, 4096:4608].rearrange("p (c h w) -> p c h w", c=C, h=HG)
        stat2 = sb("stat2", [P, C, 6])
        mv2 = sb("mv2", [P, C, 2])

        w_loaded = sem("w_loaded")
        w2_loaded = sem("w2_loaded")
        bias_zeroed = sem("bias_zeroed")
        router_loaded = sem("router_loaded")
        gain_ready = sem("gain_ready")
        w_ready = sem("w_ready")
        zeroed = sem("zeroed")
        pool_const = sem("pool_const")
        cnt_ready = sem("cnt_ready")
        cnt_sum = sem("cnt_sum")
        fcnt_ready = sem("fcnt_ready")
        fcnt_sum = sem("fcnt_sum")
        at_ready = sems("at_ready")
        lo_ready = sem("lo_ready")
        picked_done = sem("picked_done")
        rows_ready = sem("rows_ready")
        x_sel_in = sems("x_sel_in")
        pos_in_s = sems("pos_in_s")
        m_rows_in = sems("m_rows_in")
        mT_done = sems("mT_done")
        mT_ready = sems("mT_ready")
        mT_stored = sems("mT_stored")
        m_k_in = sems("m_k_in")
        nm_done = sems("nm_done")
        nm_ready = sems("nm_ready")
        ms_ready = sems("ms_ready")
        rms_ready = sems("rms_ready")
        hn_ready = sems("hn_ready")
        hnT_done = sems("hnT_done")
        hnT_ready = sems("hnT_ready")
        qk_done = sems("qk_done")
        v_done = sems("v_done")
        qk_ready = sems("qk_ready")
        v_ready = sems("v_ready")
        angle_ready = sems("angle_ready")
        sin_ready = sems("sin_ready")
        rope_ready = sems("rope_ready")
        e_parts = sem("e_parts")
        e_ready = sems("e_ready")
        eT_done = [sem(f"eT_done{n}") for n in range(4)]
        qT_ready = sem("qT_ready")
        kT_ready = sem("kT_ready")
        v_cur_ready = sem("v_cur_ready")
        s_done = sem("s_done")
        sm_ready = sem("sm_ready")
        pr_ready = sem("pr_ready")
        prT_done = sem("prT_done")
        prT_copied = sems("prT_copied")
        pv_done = sem("pv_done")
        rinv_ready = sem("rinv_ready")
        rT_done = sem("rT_done")
        oT_ready = sem("oT_ready")
        onT_ready = sem("onT_ready")
        wo_done = sems("wo_done")
        h1_done = sems("h1_done")
        gelu_ready = sems("gelu_ready")
        w2_done = sems("w2_done")
        x2_ready = sems("x2_ready")
        ve2_ready = sems("ve2_ready")
        pow3_ready = sems("pow3_ready")
        fin_ready = sems("fin_ready")
        scattered = sem("scattered")
        ident_ready = sem("ident_ready")
        wt_done = sem("wt_done")
        wt_copied = sem("wt_copied")
        split_ready = sem("split_ready")
        x_lo_ready = sems("x_lo_ready")
        h_hi_ready = sems("h_hi_ready")
        h_lo_ready = sems("h_lo_ready")
        const_ready = sem("const_ready")
        x_loaded = sems("x_loaded", U)
        xT_done = sems("xT_done")
        xT_copied = sems("xT_copied")
        ab_done = sem("ab_done")
        a_ready = sems("a_ready")
        b_ready = sems("b_ready")
        h_ready = sems("h_ready")
        gd_done = sem("gd_done")
        rec_done = sem("rec_done")
        g_ready = sem("g_ready")
        rec_g_done = sems("rec_g_done")
        dx_g_done = sems("dx_g_done")
        mixed = sems("mixed")
        s_ready = sem("s_ready")
        ve_ready = sem("ve_ready")
        shift_ready = sem("shift_ready")
        pow_ready = sem("pow_ready")
        v2_ready = sem("v2_ready")
        pow2_ready = sems("pow2_ready")
        W_ready = sem("W_ready")
        x1_ready = sems("x1_ready")
        ob_ready = sems("ob_ready")
        dve_step = sem("dve_step")
        x1_stored = sems("x1_stored")
        ob_stored = sems("ob_stored")

        x1_rows = x1_dram.rearrange("(n p t) d -> n p (t d)", p=P, t=T)
        out_rows = out.rearrange("b (g p t) d -> (b g) p (t d)", p=P, t=T)
        xin_rows = x_in.rearrange("b (g p t) d -> (b g) p (t d)", p=P, t=T)

        units = [(c, h) for c in range(C) for h in range(HG)]

        def hg_is(hg, n):
            return isinstance(hg, int) and hg == n

        def first(b, hg):
            return b == 0 and hg_is(hg, 0)

        def unit_number(b, hg, u):
            return (hg + b * TURNS) * UNITS + u

        def second_out(b, c):
            return ps[:, O_BANKS[c], 0:D] if b == B - 1 else ps[:, 6 + c // 2, (c % 2) * D:(c % 2 + 1) * D]

        def all_turns(eng, body):
            body(0)
            with eng.Fori(1, TURNS - 1) as hg:
                body(hg)
            body(TURNS - 1)

        def all_groups(eng, body):
            with eng.Fori(0, LOOPS - 1) as i:
                body(i, True)
            body(LOOPS - 1, False)

        def copy_probs(eng, copy, b, hg, u):
            c, h = units[u]
            eng.wait_ge(prT_done, unit_number(b, hg, u) + 1)
            if not first(b, hg) or c >= 2:
                eng.wait_ge(pv_done, (hg + b * TURNS) * C + c - 1)
            copy(prT[c % 2][:, h, :, :], ps[:, 2 + u % 2, :].rearrange("p (k n) -> p k n", k=C)
                 ).then_inc(prT_copied[u % 2], 1)

        block = ctx.enter_context(nc.Block())

        @block.sync
        def _(sp):
            sp.dma_start(wraw[:, 0, :, :], Wg.rearrange("(h e) d -> e h d", e=P)).then_inc(w_loaded, 16)
            sp.dma_start(wraw[:, 1, :, :], WD.rearrange("(h e) d -> e h d", e=P)).then_inc(w_loaded, 16)
            sp.dma_start(wab_raw[:, 0, :], WA).then_inc(w_loaded, 16)
            sp.dma_start(wab_raw[:, 1, :], WB).then_inc(w_loaded, 16)
            for r in range(3):
                sp.dma_start(wc_raw[:, :, r * N:(r + 1) * N], WC.rearrange("(h e) n -> e h n", e=P)).then_inc(w_loaded, 16)
            sp.wait_ge(bias_zeroed, 1)
            for row in (0, BIAS_K - 1):
                for n, v in enumerate((bg, bD)):
                    sp.dma_start(bias_row[row:row + 1, n * D:(n + 1) * D],
                                 v.rearrange("(a d) -> a d", a=1)).then_inc(w_loaded, 16)
            for u in range(U):
                sp.dma_start(x_sb[u][:, :, :], xin_rows[u]).then_inc(x_loaded[u], 16)
            sp.dma_start(rw_row[:, :], router_w.rearrange("d a -> a d").broadcast_to((P, D))).then_inc(router_loaded, 16)
            sp.dma_start(rb_col[:, :], router_b.rearrange("(a d) -> a d", a=1).broadcast_to((P, 1))).then_inc(router_loaded, 16)

            sp.dma_start(wqk[:, :, 0:D], wq.rearrange("(k p) n -> p k n", p=P)).then_inc(w2_loaded, 16)
            sp.dma_start(wqk[:, :, D:2 * D], wk.rearrange("(k p) n -> p k n", p=P)).then_inc(w2_loaded, 16)
            sp.dma_start(wv_sb[:, :, :], wv.rearrange("(k p) n -> p k n", p=P)).then_inc(w2_loaded, 16)
            sp.dma_start(w1_sb[:, :, :], w1.rearrange("(k p) f -> p k f", p=P)).then_inc(w2_loaded, 16)
            sp.dma_start(w2_sb[:, :, :], w2.rearrange("(f p) n -> p f n", p=P)).then_inc(w2_loaded, 16)
            with nc.allow_non_contiguous_dma("two short columns"):
                sp.dma_start(ln_col[:, 0, :], ln1.rearrange("(k p) -> p k", p=P)).then_inc(w2_loaded, 16)
                sp.dma_start(ln_col[:, 1, :], ln2.rearrange("(k p) -> p k", p=P)).then_inc(w2_loaded, 16)
            sp.wait_ge(zeroed, 1)
            wo_v = wo.rearrange("(g h e) n -> h e g n", h=HG, e=HD)
            for h in range(HG):
                sp.dma_start(wo_pad[h * HP:h * HP + HD, :, :], wo_v[h]).then_inc(w2_loaded, 16)

            def body(turn, more):
                for u in range(U):
                    j, G = u % 2, U * turn + u
                    if more:
                        sp.wait_ge(s_ready, (G + 1) * 2)
                        sp.wait_ge(xT_done[1], G + 1)
                        sp.dma_start(x_sb[u][:, :, :], xin_rows[G + U]).then_inc(x_loaded[u], 16)
                    sp.wait_ge(x1_ready[j], (before(turn, u, j) + 1) * T)
                    sp.dma_start(x1_rows[G], x1_sb[j][:, :, :]).then_inc(x1_stored[j], 16)
                    sp.wait_ge(ob_ready[j], (before(turn, u, j) + 1) * T)
                    sp.dma_start(out_rows[G], ob_sb[j][:, :, :]).then_inc(ob_stored[j], 16)

            all_groups(sp, body)
            for b in range(B):
                for n in range(MS // P):
                    sp.wait_ge(mT_ready[b], n + 1)
                    sp.dma_start(mt_dram[b][n * P:(n + 1) * P, :], m_turned[b][n]).then_inc(mT_stored[b], 16)
            for j in range(2):
                sp.wait_ge(ob_stored[j], 16 * B * NG // 2)
            sp.wait_ge(scattered, 16 * B * C)

        @block.gpsimd
        def _(pool):
            pool.memset(bias_row[:, :], 0.0).then_inc(bias_zeroed, 1)
            pool.memset(ident[:, :], 0.0).then_inc(ident_ready, 1)
            pool.wait_ge(ident_ready, 1)
            pool.affine_select(out=ident[:, :], in_=ident[:, :], compare_op=ALU.not_equal, fill=1.0, base=0,
                               pattern=[[-1, P]], channel_multiplier=1).then_inc(ident_ready, 1)
            pool.memset(minus_half[:, :], -0.5).then_inc(ident_ready, 1)
            pool.wait_ge(ident_ready, 2)
            pool.memset(wo_pad[:, :, :], 0.0).then_inc(zeroed, 1)
            pool.memset(zeros[:, :], 0.0).then_inc(pool_const, 1)
            pool.memset(ones_b[:, :], 1.0).then_inc(pool_const, 1)
            pool.wait_ge(pool_const, 2)
            pool.affine_select(out=below_b[:, :], in_=ones_b[:, :], compare_op=ALU.is_gt, fill=0.0, base=0,
                               pattern=[[1, P]], channel_multiplier=-1).then_inc(pool_const, 1)
            pool.iota(digit_i[:, :], [[1, CAND]], base=1, channel_multiplier=0).then_inc(pool_const, 1)
            pool.iota(hi_i[:, :], [[1, P]], base=0, channel_multiplier=0).then_inc(pool_const, 1)
            pool.iota(lo_i[:, :], [[1, C]], base=0, channel_multiplier=0).then_inc(pool_const, 1)
            pool.iota(pgt[:, 0, :, :], [[0, NG], [0, T]], base=0, channel_multiplier=1).then_inc(pool_const, 1)
            pool.iota(pgt[:, 1, :, :], [[1, NG], [0, T]], base=0, channel_multiplier=0).then_inc(pool_const, 1)
            pool.iota(pgt[:, 2, :, :], [[0, NG], [1, T]], base=0, channel_multiplier=0).then_inc(pool_const, 1)
            for k in range(HD // 2):
                pool.memset(inv_f[:, k:k + 1], INV_FREQ[k]).then_inc(pool_const, 1)

            def combine(turn, u, q):
                j, G = u % 2, U * turn + u
                pool.wait_ge(rec_g_done[q], G + 1)
                pool.wait_ge(dx_g_done[q], G + 1)
                pool.tensor_tensor(mix[q][:, :, :], rec_g[q][:, :, :], dx_g[q][:, :, :],
                                   ALU.subtract).then_inc(mixed[q], 1)
                pool.wait_ge(x1_ready[j], before(turn, u, j) * T)
                pool.wait_ge(mixed[q], G + 1)
                pool.tensor_tensor(s_sb[j][:, 2 * q:2 * q + 2, :], mix[q][:, :, :],
                                   x_sb[u % U][:, 2 * q:2 * q + 2, :], ALU.add).then_inc(s_ready, 1)

            def groups(turn, more):
                def rstd(u):
                    pool.wait_ge(ve_ready, U * turn + u + 1)
                    pool.tensor_tensor(small[u % 2][:, 1, :], small[u % 2][:, 0, :], minus_half[:, :],
                                       ALU.pow).then_inc(pow_ready, 1)

                def rstd2(u):
                    j = u % 2
                    pool.wait_ge(v2_ready, U * turn + u + 1)
                    pool.wait_ge(ob_ready[j], before(turn, u, j) * T)
                    pool.tensor_tensor(small[u % 2][:, 5, :], small[u % 2][:, 4, :], minus_half[:, :],
                                       ALU.pow).then_inc(pow2_ready[j], 1)

                for u in range(U):
                    rstd(u)
                    if u + 1 < U or more:
                        combine(turn, u + 1, 0)
                    rstd2(u)
                    if u + 1 < U or more:
                        combine(turn, u + 1, 1)

            combine(0, 0, 0)
            combine(0, 0, 1)
            all_groups(pool, groups)

            def gather(dst, table, index, signal):
                pool.indirect_dma_start(out=dst, out_offset=None, in_=table,
                                        in_offset=bass.IndirectOffsetOnAxis(ap=index, axis=0)).then_inc(signal, 16)

            def rsqrt(dst, src, ready, n, signal):
                pool.wait_ge(ready, n)
                pool.tensor_tensor(dst, src, minus_half[:, 0:C], ALU.pow).then_inc(signal, 1)

            mask_rows = mask_in.rearrange("a o s t -> (a o s) t")
            pos_rows = pos_in.rearrange("a (s o) -> (a s) o", o=1)
            pool.wait_ge(rows_ready, 3)
            for j in range(2):
                pool.wait_ge(x1_stored[j], 16 * B * NG // 2)
            for j in range(2):
                pool.wait_ge(ob_ready[j], B * NG // 2 * T)
            def gather_x(b):
                for c in range(C):
                    gather(x_sel[b][:, c, :], x1_dram, row_x[:, b, c:c + 1], x_sel_in[b])

            def gather_positions(b):
                for c in range(C):
                    gather(pos_i[:, b, c:c + 1], pos_rows, row_m[:, b, c:c + 1], pos_in_s[b])

            def gather_mask_rows(b):
                for c in range(C):
                    gather(m_rows[b][:, c, :], mask_rows, row_m[:, b, c:c + 1], m_rows_in[b])

            gather_x(0)
            gather_positions(0)
            rsqrt(ms[0][:, 2, :], ms[0][:, 1, :], ms_ready[0], 1, rms_ready[0])
            pool.wait_ge(rows_ready, 6)
            gather_x(1)
            gather_mask_rows(0)
            rsqrt(ms[1][:, 2, :], ms[1][:, 1, :], ms_ready[1], 1, rms_ready[1])
            gather_mask_rows(1)
            gather_positions(1)
            for b in range(B):
                pool.wait_ge(mT_stored[b], 16 * M_STORES)
                for c in range(C):
                    gather(m_k[b][:, c, :], mt_dram[b], row_t[:, b, c:c + 1], m_k_in[b])
            for b in range(B):
                if b == 0:
                    pool.memset(v_cur[:, :, :, :], 0.0).then_inc(zeroed, 1)
                    pool.wait_ge(nm_done[0], C)
                    pool.memset(arena2[:, 2048:4096].rearrange("p (n k) -> p n k", n=4)[:, :, K - 1:K],
                                0.0).then_inc(zeroed, 1)
                    pool.wait_ge(zeroed, 3)
                pool.wait_ge(v_ready[b], C)

                def turn_body(hg):
                    turn = hg + b * TURNS
                    if not first(b, hg):
                        pool.wait_ge(pv_done, turn * C)
                    pool.tensor_copy(v_cur[:, :, :, 0:HD], v_sb[b][:, :, bass.ts(hg, HG * HD)].rearrange(
                        "p c (h w) -> p c h w", h=HG)).then_inc(v_cur_ready, 1)

                all_turns(pool, turn_body)
                rsqrt(ms[b][:, 5, :], ms[b][:, 4, :], ms_ready[b], 2, rms_ready[b])
            for j in range(2):
                pool.wait_ge(ob_stored[j], 16 * B * NG // 2)
            for b in range(B):
                for part, cs in enumerate(PARTS[b]):
                    pool.wait_ge(ve2_ready[b], part + 1)
                    pool.tensor_tensor(ms[b][:, 2, cs[0]:cs[-1] + 1], ms[b][:, 1, cs[0]:cs[-1] + 1],
                                       minus_half[:, 0:len(cs)], ALU.pow).then_inc(pow3_ready[b], 1)
                    for c in cs:
                        n = P - (c == C - 1)
                        pool.wait_ge(fin_ready[b], c + 1)
                        pool.indirect_dma_start(out=out.rearrange("b s d -> (b s) d"),
                                                out_offset=bass.IndirectOffsetOnAxis(ap=row_x[0:n, b, c:c + 1], axis=0),
                                                in_=x_sel[b][0:n, c, :], in_offset=None).then_inc(scattered, 16)

        @block.tensor
        def _(pe):
            pe.wait_ge(ident_ready, 2)
            pe.wait_ge(w_loaded, 16 * 11)
            for c in range(KD):
                for m in range(2):
                    for h in range(2):
                        pe.transpose(ps[:, c, m * D + h * P:m * D + (h + 1) * P],
                                     wraw[:, m, h, c * P:(c + 1) * P], ident[:, :])
                for m in range(2):
                    pe.transpose(ps[:, 2, (c * 2 + m) * N:(c * 2 + m + 1) * N],
                                 wab_raw[:, m, c * P:(c + 1) * P], ident[0:N, 0:N])
            for h in range(2):
                mm = pe.transpose(ps[0:HROWS, 3, h * P:(h + 1) * P], wc_raw[:, h, :], ident[:, :])
            mm.then_inc(wt_done, 1)
            pe.wait_ge(split_ready, KD)
            def transposes(turn, u):
                j, G = u % 2, U * turn + u
                pe.wait_ge(x_loaded[u % U], (turn + 1 + u // U) * 16)
                for c in range(KD):
                    if u:
                        pe.wait_ge(x_lo_ready[1 - j], (before(turn, u, 1 - j) - 1) * KD + c + 1)
                    for t in range(T):
                        mm = pe.transpose(ps[:, c, t * P:(t + 1) * P],
                                          x_sb[u % U][:, t, c * P:(c + 1) * P], ident[:, :])
                    mm.then_inc(xT_done[c], 1)

            def recurrence_inputs(turn, u):
                j = u % 2
                pe.wait_ge(x_lo_ready[j], (before(turn, u, j) + 1) * KD)
                pe.wait_ge(a_ready[1 - j], before(turn, u, 1 - j))
                pe.wait_ge(b_ready[1 - j], before(turn, u, 1 - j))
                for c in range(KD):
                    pe.matmul(ps[:, 2, :], wab_hi[:, c, :], x_hi[j][:, c, :], start=(c == 0), stop=False)
                    pe.matmul(ps[:, 2, :], wab_hi[:, c, :], x_lo[j][:, c, :], start=False, stop=False)
                    mm = pe.matmul(ps[:, 2, :], wab_lo[:, c, :], x_hi[j][:, c, :], start=False, stop=(c == KD - 1))
                mm.then_inc(ab_done, 1)

            def gates(turn, u, q):
                j = u % 2
                pe.wait_ge(dx_g_done[q], U * turn + u)
                for t in range(2):
                    o = ps[:, 3 + 2 * q + t, :]
                    tt = 2 * q + t
                    pe.matmul(o, ones_k[:, :], bias_parts[:, :], start=True, stop=False)
                    for c in range(KD):
                        hi, lo = (x[j][:, c, tt * P:(tt + 1) * P] for x in (x_hi, x_lo))
                        pe.matmul(o, hi, wgd_hi[:, c, :], start=False, stop=False)
                        pe.matmul(o, hi, wgd_lo[:, c, :], start=False, stop=False)
                        mm = pe.matmul(o, lo, wgd_hi[:, c, :], start=False, stop=(c == KD - 1))
                mm.then_inc(gd_done, 1)

            def recurrence_out(turn, u, q):
                j = u % 2
                pe.wait_ge(h_lo_ready[j], before(turn, u, j) + 1)
                pe.wait_ge(rec_g_done[1 - q], U * turn + u + q)
                for t in range(2):
                    tt = 2 * q + t
                    mm = pe.matmul(ps[:, 7, t * D:(t + 1) * D],
                                   h_parts[j][:, :].rearrange("n (p t) -> n t p", t=T)[:, tt, :],
                                   wc[:, :], start=True, stop=True)
                mm.then_inc(rec_done, 1)

            def groups(turn, more):
                for u in range(U):
                    gates(turn, u, 0)
                    recurrence_out(turn, u, 0)
                    if u + 1 < U or more:
                        recurrence_inputs(turn, u + 1)
                    gates(turn, u, 1)
                    if u + 2 < U or more:
                        transposes(turn, u + 2)
                    recurrence_out(turn, u, 1)

            transposes(0, 0)
            transposes(0, 1)
            pe.wait_ge(split_ready, 2 * KD)
            recurrence_inputs(0, 0)
            pe.wait_ge(split_ready, 2 * KD + 1)
            pe.wait_ge(const_ready, 1)
            all_groups(pe, groups)

            for r in range(ROUNDS):
                pe.wait_ge(cnt_ready, r + 1)
                pe.matmul(ps[:, 0, 0:B * CAND], ones_b[:, :], cnt[:, :], start=True, stop=True).then_inc(cnt_sum, 1)
            pe.wait_ge(fcnt_ready, 1)
            pe.matmul(ps[:, 1, 0:32], below_b[:, :], fcnt[:, :, :, :], start=True, stop=True)
            pe.matmul(ps[:, 2, 0:32], ones_b[:, :], fcnt[:, :, :, :], start=True, stop=True).then_inc(fcnt_sum, 1)
            for b in range(B):
                pe.wait_ge(lo_ready, b + 1)
                pe.wait_ge(at_ready[b], 1)
                for n in range(NG * T):
                    mm = pe.matmul(ps[:, 3 + b, 0:C * VALS], at_hi[:, b, n, :], lo_vals[:, b, n, :, :],
                                   start=(n == 0), stop=(n == NG * T - 1))
                mm.then_inc(picked_done, 1)

            def turn_mask_rows(b):
                pe.wait_ge(m_rows_in[b], 16 * C)
                for n in range(MS // P):
                    if n >= 2:
                        pe.wait_ge(mT_ready[b], n - 1)
                    elif b > 0:
                        pe.wait_ge(mT_ready[b - 1], MS // P)
                    for c in range(C):
                        mm = pe.transpose(ps[:, n % 2, c * P:(c + 1) * P], m_rows[b][:, c, n * P:(n + 1) * P], ident[:, :])
                    mm.then_inc(mT_done[b], 1)

            def turn_mask_columns():
                pe.wait_ge(m_k_in[0], 16 * C)
                for c in range(C):
                    pe.wait_ge(qk_ready[1], 3 + c // 2)
                    pe.wait_ge(v_ready[1], 3 + c // 2)
                    for k in range(C):
                        mm = pe.transpose(ps[:, M_BANKS[c], k * P:(k + 1) * P], m_k[0][:, k, c * P:(c + 1) * P], ident[:, :])
                    mm.then_inc(nm_done[0], 1)

            def turn_second_mask_columns():
                pe.wait_ge(m_k_in[1], 16 * C)
                for c in range(C):
                    for k in range(C):
                        mm = pe.transpose(ps[:, 2 + c, k * P:(k + 1) * P], m_k[1][:, k, c * P:(c + 1) * P], ident[:, :])
                    mm.then_inc(nm_done[1], 1)

            def turn_hn(b, first):
                for k in range(KD):
                    for c in range(C):
                        pe.wait_ge(hn_ready[b], first + c + 1)
                        mm = pe.transpose(ps[:, 2 + k, c * P:(c + 1) * P], hn[:, c, k * P:(k + 1) * P], ident[:, :])
                    mm.then_inc(hnT_done[b], 1)

            def project(b, chunks):
                pe.wait_ge(hnT_ready[b], KD)
                pe.wait_ge(w_ready, KD)
                for c in chunks:
                    if c >= 2:
                        pe.wait_ge(qk_ready[b], c - 1)
                        pe.wait_ge(v_ready[b], c - 1)
                    elif b > 0:
                        pe.wait_ge(qk_ready[b - 1], C)
                        pe.wait_ge(v_ready[b - 1], C)
                    for k in range(KD):
                        mm = pe.matmul(ps[:, 4 + c % 2, :], hnT[:, k, c * P:(c + 1) * P], wqk[:, k, :],
                                       start=(k == 0), stop=(k == KD - 1))
                    mm.then_inc(qk_done[b], 1)
                    for k in range(KD):
                        mm = pe.matmul(ps[:, 6 + c % 2, 0:D], hnT[:, k, c * P:(c + 1) * P], wv_sb[:, k, :],
                                       start=(k == 0), stop=(k == KD - 1))
                    mm.then_inc(v_done[b], 1)

            psb = ps[:, :, :].bitcast(BF16)

            def turn_split(b, c):
                done = c + b * C
                for n in range(2):
                    pe.wait_ge(e_ready[n], done + 1)
                for m in range(2):
                    for half in range(2):
                        pe.wait_ge((qT_ready, kT_ready)[m], done * 2)
                        for h in range(8):
                            mm = pe.transpose(psb[0:ER, 2 * m + half, h * P:(h + 1) * P],
                                              e_sb[c % 2][:, m, 8 * half + h, :, :], ident_b[:, :])
                        mm.then_inc(eT_done[2 * m + half], 1)

            def project_out(b, c, groups):
                for g in groups:
                    mm = pe.matmul(ps[:, O_BANKS[c], 0:D], onT[:, g, c * P:(c + 1) * P],
                                   wo_pad[:, g, :], start=(g == 0), stop=(g == TURNS - 1))
                    if g == TURNS - 1:
                        mm.then_inc(wo_done[b], 1)

            def attention(b):
                pe.wait_ge(qT_ready, (b + 1) * C * 2)
                pe.wait_ge(kT_ready, (b + 1) * C * 2)

                def scores(hg, u):
                    c, h = units[u]
                    n = unit_number(b, hg, u)
                    if not first(b, hg) or u >= AHEAD:
                        pe.wait_ge(sm_ready, n - AHEAD + 1)
                    if hg_is(hg, 0) and S_BANKS[u % AHEAD] >= 6:
                        if b > 0:
                            pe.wait_ge(x2_ready[b - 1], C)
                        else:
                            pe.wait_ge(nm_ready[0], C)
                    pe.matmul(ps[:, S_BANKS[u % AHEAD], :], qkT[0][:, bass.ds(hg * HG + h, 1), c * P:(c + 1) * P],
                              qkT[1][:, bass.ds(hg * HG + h, 1), :], start=True, stop=True).then_inc(s_done, 1)

                def turn_probs(hg, u):
                    n = unit_number(b, hg, u)
                    pe.wait_ge(pr_ready, n + 1)
                    if first(b, hg) and u == 0:
                        pe.wait_ge(zeroed, 3)
                    if not first(b, hg) or u >= 2:
                        pe.wait_ge(prT_copied[u % 2], (b * TURNS + hg) * (UNITS // 2) + u // 2)
                    for k in range(C):
                        mm = pe.transpose(ps[:, 2 + u % 2, k * P:(k + 1) * P], pr[u % 4][:, k * P:(k + 1) * P],
                                          ident[:, :])
                    mm.then_inc(prT_done, 1)

                def values(hg, c, half):
                    turn = hg + b * TURNS
                    if half == 0:
                        for par in range(2):
                            pe.wait_ge(prT_copied[par], turn * (UNITS // 2) + 2 * (c + 1))
                        if c == 0:
                            pe.wait_ge(v_cur_ready, turn + 1)
                            if not first(b, hg):
                                pe.wait_ge(oT_ready, turn)
                    for k in range(half * C // 2, (half + 1) * C // 2):
                        for h in range(HG):
                            mm = pe.matmul(ps[h * HP:(h + 1) * HP, 4, c * P:(c + 1) * P],
                                           v_cur[:, k, h, :], prT[c % 2][:, h, k, :],
                                           start=(k == 0), stop=(k == C - 1))
                    if half == 1:
                        mm.then_inc(pv_done, 1)

                def sums(hg, c):
                    turn = hg + b * TURNS
                    pe.wait_ge(rinv_ready, turn * 2 * C + 2 * c + 2)
                    if c == 0 and not first(b, hg):
                        pe.wait_ge(onT_ready, turn)
                    pe.transpose(ps[:, 5, c * P:(c + 1) * P], rinv_w[:, c, :, :], ident[:, :]).then_inc(rT_done, 1)

                def late(hg, u):
                    for c in range(C):
                        for half in range(2):
                            if u == c * HG + LAG + half:
                                values(hg, c, half)
                        if u == c * HG + LAG + 2:
                            sums(hg, c)

                def turn_body(hg):
                    if hg_is(hg, 0):
                        for u in range(AHEAD):
                            scores(hg, u)
                    for u in range(UNITS):
                        if u + AHEAD < UNITS:
                            scores(hg, u + AHEAD)
                        elif not hg_is(hg, TURNS - 1):
                            scores(hg + 1, u + AHEAD - UNITS)
                        turn_probs(hg, u)
                        late(hg, u)
                        if not hg_is(hg, 0):
                            late(hg - 1, u + UNITS)
                        if hg_is(hg, TURNS - 1) and u >= UNITS - AHEAD:
                            pe.wait_ge(sm_ready, unit_number(b, hg, u) + 1)
                            pe.wait_ge(onT_ready, b * TURNS + TURNS - 1)
                            project_out(b, u - (UNITS - AHEAD), range(TURNS - 1))
                    if hg_is(hg, TURNS - 1):
                        for u in range(UNITS, UNITS + LAG):
                            late(hg, u)

                all_turns(pe, turn_body)

            def hidden(b):
                for f in range(FB):
                    if f >= 2:
                        pe.wait_ge(gelu_ready[b], f - 1)
                    for k in range(KD):
                        pe.wait_ge(hnT_ready[b], KD + k + 1)
                        mm = pe.matmul(ps[:, 4 + f % 2, :], w1_sb[:, k, f * P:(f + 1) * P], hnT[:, k, :],
                                       start=(k == 0), stop=(k == KD - 1))
                    mm.then_inc(h1_done[b], 1)

            def second_product(b, c):
                for f in range(FB):
                    pe.wait_ge(gelu_ready[b], f + 1)
                    mm = pe.matmul(second_out(b, c), hidden_sb[:, f, c * P:(c + 1) * P],
                                   w2_sb[:, f, :], start=(f == 0), stop=(f == FB - 1))
                mm.then_inc(w2_done[b], 1)

            turn_hn(0, 0)
            project(0, range(C))
            turn_mask_rows(0)
            turn_mask_rows(1)
            turn_hn(1, 0)
            pe.wait_ge(mT_ready[1], MS // P)
            pe.wait_ge(hnT_ready[1], KD)
            for c in range(C):
                turn_split(0, c)
                project(1, range(c, c + 1))
            turn_mask_columns()
            for b in range(B):
                attention(b)
                pe.wait_ge(onT_ready, (b + 1) * TURNS)
                for c in range(C):
                    project_out(b, c, range(TURNS - 1, TURNS))
                if b == 0:
                    turn_second_mask_columns()
                    pe.wait_ge(nm_ready[1], 2)
                turn_hn(b, C)
                pe.wait_ge(nm_ready[1], C)
                hidden(b)
                for c in range(C):
                    if b < B - 1 and c == C - 1:
                        turn_split(b + 1, c)
                    second_product(b, c)
                    if b < B - 1 and c < C - 1:
                        turn_split(b + 1, c)

        @block.scalar
        def _(act):
            act.wait_ge(wt_done, 1)
            for c in range(KD):
                act.copy(wgd_hi[:, c, :], ps[:, c, :]).then_inc(wt_copied, 1)
            act.copy(wc_hi[:, :], ps[0:HROWS, 3, 0:D]).then_inc(wt_copied, 1)
            def copy_xT(turn, u):
                j, G = u % 2, U * turn + u
                for c in range(KD):
                    act.wait_ge(xT_done[c], G + 1)
                    if c == 0 and u >= 2:
                        act.wait_ge(gd_done, 2 * G - 2)
                    act.copy(x_hi[j][:, c, :], ps[:, c, :]).then_inc(xT_copied[j], 1)

            def recurrence(turn, u):
                j = u % 2
                act.wait_ge(ab_done, U * turn + u + 1)
                act.wait_ge(h_ready[j], before(turn, u, j))
                act.activation(a_sb[j][:, :].rearrange("n (p t) -> n t p", t=T),
                               ps[0:HROWS, 2, :].rearrange("n (t p) -> n t p", t=T),
                               ACT.Tanh).then_inc(a_ready[j], 1)
                act.copy(b_sb[j][:, :].rearrange("n (p t) -> n t p", t=T),
                         ps[BROW:BROW + HROWS, 2, :].rearrange("n (t p) -> n t p", t=T)).then_inc(b_ready[j], 1)

            def gate(turn, u, q):
                n = 2 * (U * turn + u) + q
                act.wait_ge(gd_done, n + 1)
                act.wait_ge(dx_g_done[q], U * turn + u)
                act.wait_ge(rec_g_done[q], U * turn + u)
                act.activation(g_sb[q][:, :, :], ps[:, 3 + 2 * q:5 + 2 * q, 0:D],
                               ACT.Sigmoid).then_inc(g_ready, 1)

            def round_h(turn, u):
                j = u % 2
                act.wait_ge(h_ready[j], before(turn, u, j) + 1)
                if u >= 2:
                    act.wait_ge(rec_done, 2 * (U * turn + u) - 2)
                act.copy(h_parts[j][:, :], h_sb[j][:, :]).then_inc(h_hi_ready[j], 1)

            def first_norm(turn, u):
                j, G = u % 2, U * turn + u
                act.wait_ge(shift_ready, G + 1)
                act.wait_ge(x1_stored[j], 16 * before(turn, u, j))
                for t in range(T):
                    act.activation(x1_sb[j][:, t, :], s_sb[j][:, t, :], ACT.Identity, bias=small[j][:, 6, t:t + 1],
                                   scale=small[j][:, 1, t:t + 1]).then_inc(x1_ready[j], 1)

            def second_norm(turn, u):
                j = u % 2
                act.wait_ge(pow2_ready[j], before(turn, u, j) + 1)
                act.wait_ge(x1_ready[j], (before(turn, u, j) + 1) * T)
                act.wait_ge(ob_stored[j], 16 * before(turn, u, j))
                for t in range(T):
                    act.mul(ob_sb[j][:, t, :], x1_sb[j][:, t, :], small[j][:, 5, t:t + 1]).then_inc(ob_ready[j], 1)

            def groups(turn, more):
                for u in range(U):
                    if u + 1 < U or more:
                        gate(turn, u + 1, 0)
                    if u + 2 < U or more:
                        recurrence(turn, u + 2)
                    if u + 1 < U or more:
                        gate(turn, u + 1, 1)
                    if u + 2 < U or more:
                        round_h(turn, u + 2)
                    if u + 3 < U or more:
                        copy_xT(turn, u + 3)
                    first_norm(turn, u)
                    second_norm(turn, u)

            copy_xT(0, 0)
            copy_xT(0, 1)
            act.wait_ge(const_ready, 1)
            for u in range(2):
                recurrence(0, u)
                round_h(0, u)
                gate(0, 0, u)
            copy_xT(0, 2)
            all_groups(act, groups)

            act.wait_ge(w2_loaded, 16 * (7 + HG))
            act.mul(q_gain[:, :], ln_col[:, 0, :], -(HD ** -0.5)).then_inc(gain_ready, 1)
            act.wait_ge(gain_ready, 1)
            for k in range(KD):
                g1, g2 = ln_col[:, 0, k:k + 1], ln_col[:, 1, k:k + 1]
                act.mul(wqk[:, k, 0:D], wqk[:, k, 0:D], q_gain[:, k:k + 1])
                act.mul(wqk[:, k, D:2 * D], wqk[:, k, D:2 * D], g1)
                act.mul(wv_sb[:, k, :], wv_sb[:, k, :], g1)
                act.mul(w1_sb[:, k, :], w1_sb[:, k, :], g2).then_inc(w_ready, 1)

            def copy_hnT(b, first):
                for k in range(KD):
                    act.wait_ge(hnT_done[b], first + k + 1)
                    act.copy(hnT[:, k, :], ps[:, 2 + k, :]).then_inc(hnT_ready[b], 1)

            def copy_qk(b, c):
                act.wait_ge(qk_done[b], c + 1)
                act.copy(qk[b][:, c, :], ps[:, 4 + c % 2, :]).then_inc(qk_ready[b], 1)

            def sines(b):
                act.wait_ge(angle_ready[b], 1)
                act.activation(trig[b][:, 4, :, :], trig[b][:, 3, :, :], ACT.Sin)
                act.activation(trig[b][:, 5, :, :], trig[b][:, 3, :, :], ACT.Sin, scale=0.5).then_inc(sin_ready[b], 1)

            def copy_mask_rows(b):
                for n in range(MS // P):
                    act.wait_ge(mT_done[b], n + 1)
                    act.mul(m_turned[b][n], ps[:, n % 2, :], -1.0).then_inc(mT_ready[b], 1)

            def split(b, beside=None):
                def copy_turned(c):
                    for half in range(2):
                        act.wait_ge(eT_done[half], c + b * C + 1)
                        act.copy(qkT[0][:, 8 * half:8 * half + 8, c * P:(c + 1) * P],
                                 ps[:, :, :].bitcast(BF16)[0:ER, half, :].rearrange("r (h n) -> r h n", h=8)
                                 ).then_inc(qT_ready, 1)

                for c in range(C):
                    done = c + b * C
                    q, k = e_sb[c % 2][:, 0, :, :, :], e_sb[c % 2][:, 1, :, :, :]
                    h2 = e_sb[c % 2][:, :, :, 0:1, :].broadcast_to((P, 2, H, 2, HD))
                    act.wait_ge(e_parts, 2 * done + 1)
                    act.copy(q[:, :, 2:5:2, :], h2[:, 0])
                    act.copy(k[:, :, 1:6:4, :], h2[:, 1])
                    act.wait_ge(e_parts, 2 * done + 2)
                    act.copy(q[:, :, 1, :], q[:, :, 3, :])
                    act.copy(k[:, :, 2, :], k[:, :, 3, :]).then_inc(e_ready[1], 1)
                    if c:
                        copy_turned(c - 1)
                        if b == 0:
                            beside(c - 1)
                copy_turned(C - 1)
                if b == 0:
                    beside(C - 1)

            def attention(b):
                def exponentials(hg, u):
                    c, h = units[u]
                    n = unit_number(b, hg, u)
                    act.wait_ge(sm_ready, n + 1)
                    if not first(b, hg) or u >= 4:
                        act.wait_ge(prT_done, n - 3)
                    if h == 0 and not first(b, hg):
                        act.wait_ge(rinv_ready, (hg + b * TURNS) * 2 * C - 2 * C + 2 * c + 1)
                    act.activation(pr[u % 4][:, 0:K - 1], sm[u % 4][:, 0:K - 1], ACT.Exp,
                                   bias=nmax[:, c, h:h + 1], scale=-1.0,
                                   accum_out=rsum[:, c, h:h + 1]).then_inc(pr_ready, 1)

                def copy_heads(hg):
                    turn = hg + b * TURNS
                    act.wait_ge(pv_done, turn * C + C)
                    if not first(b, hg):
                        act.wait_ge(onT_ready, turn)
                    act.copy(oT[:, :], ps[:, 4, :]).then_inc(oT_ready, 1)

                def turn_body(hg):
                    for u in range(UNITS):
                        exponentials(hg, u)
                        if u == 7 and not hg_is(hg, 0):
                            copy_heads(hg - 1)
                        if u % 2 == 0 and u >= 2:
                            copy_probs(act, act.copy, b, hg, u - 2)
                        elif u == 0 and not hg_is(hg, 0):
                            copy_probs(act, act.copy, b, hg - 1, UNITS - 2)
                    if hg_is(hg, TURNS - 1):
                        copy_probs(act, act.copy, b, hg, UNITS - 2)
                        copy_heads(hg)

                all_turns(act, turn_body)

            def hidden(b):
                for f in range(FB):
                    act.wait_ge(h1_done[b], f + 1)
                    if b > 0 and f == 0:
                        act.wait_ge(w2_done[b - 1], C)
                    act.activation(hidden_sb[:, f, :], ps[:, 4 + f % 2, :], ACT.Gelu_apprx_tanh).then_inc(gelu_ready[b], 1)

            copy_hnT(0, 0)
            sines(0)
            for c in range(C):
                copy_qk(0, c)
            copy_mask_rows(0)
            copy_mask_rows(1)
            copy_hnT(1, 0)
            split(0, lambda c: copy_qk(1, c))
            for b in range(B):
                attention(b)
                if b == 0:
                    sines(1)
                    act.wait_ge(nm_done[1], C)
                    for c in range(C):
                        act.copy(nmask[1][:, c, :], ps[:, 2 + c, :]).then_inc(nm_ready[1], 1)
                copy_hnT(b, KD)
                hidden(b)
                if b < B - 1:
                    split(b + 1)

        @block.vector
        def _(dve):
            step = Steps(dve, dve_step)
            dve.wait_ge(pool_const, 9 + HD // 2)
            dve.wait_ge(ident_ready, 2)
            dve.tensor_copy(ident_b[:, :], ident[:, :])
            dve.tensor_copy(hi_row[:, :], hi_i[:, :])
            dve.tensor_copy(lo_row[:, :], lo_i[:, :])
            for b in range(B):
                for n in range(3):
                    dve.tensor_copy(vals[:, b, :, n], pgt[:, n, :, :].rearrange("p g t -> p (g t)"))
            for r in range(ROUNDS):
                dve.tensor_scalar(digits[:, r, :], digit_i[:, :], 32 - DIGIT * (r + 1), None, ALU.logical_shift_left)
            step.link(dve.memset(zero_state[:, :], 0.0))
            step.link(dve.memset(going_on[:, :], -1))
            step.link(dve.memset(going_on[:, NG // U - 1:LOOPS:NG // U], 0))

            dve.wait_ge(wt_done, 1)
            dve.wait_ge(wt_copied, KD + 1)
            for c in range(KD):
                dve.tensor_tensor(wgd_lo[:, c, :], ps[:, c, :], wgd_hi[:, c, :].bitcast(F32),
                                  ALU.subtract).then_inc(split_ready, 1)
            raw = ps[:, 2, 0:4 * N].rearrange("p (c m o n) -> p c m o n", c=KD, m=2, o=1).broadcast_to(
                (P, KD, 2, BROW // N, N))
            wab4 = [w[:, :, :].rearrange("p c (m r n) -> p c m r n", m=2, r=BROW // N) for w in (wab_hi, wab_lo)]
            for c in range(KD):
                step.link(dve.tensor_copy(wab4[0][:, c], raw[:, c]))
                dve.tensor_tensor(wab4[1][:, c], raw[:, c], wab4[0][:, c].bitcast(F32),
                                  ALU.subtract).then_inc(split_ready, 1)
            def scan(turn, u):
                j = u % 2
                dve.wait_ge(a_ready[j], before(turn, u, j) + 1)
                dve.wait_ge(b_ready[j], before(turn, u, j) + 1)
                if u:
                    dve.wait_ge(h_ready[1 - j], before(turn, u, 1 - j))
                if u >= 2:
                    dve.wait_ge(rec_done, 2 * (U * turn + u) - 2)
                state = h_sb[1 - j][:, GT - 1:GT]
                if u == 0:
                    state = zero_state[:, :]
                elif u == U:
                    step.link(dve.tensor_tensor(next_state[:, :], state.bitcast(I32),
                                                going_on[:, bass.ds(turn, 1)], ALU.bitwise_and))
                    state = next_state[:, :].bitcast(F32)
                dve.tensor_tensor_scan(h_sb[j][:, :], a_sb[j][:, :], b_sb[j][:, :],
                                       state, ALU.mult, ALU.add
                                       ).then_inc(h_ready[j], 1)

            def products(turn, u, q):
                n = 2 * (U * turn + u) + q
                dve.wait_ge(mixed[q], U * turn + u)
                dve.wait_ge(g_ready, n + 1)
                dve.scalar_tensor_tensor(dx_g[q][:, :, :], g_sb[q][:, :, :], 1.0,
                                         ps[:, 3 + 2 * q:5 + 2 * q, D:2 * D],
                                         ALU.subtract, ALU.mult).then_inc(dx_g_done[q], 1)
                dve.wait_ge(rec_done, n + 1)
                dve.tensor_tensor(rec_g[q][:, :, :], ps[:, 7, :].rearrange("p (t d) -> p t d", t=2),
                                  g_sb[q][:, :, :], ALU.mult).then_inc(rec_g_done[q], 1)

            def statistics(turn, u):
                j, G = u % 2, U * turn + u
                dve.wait_ge(s_ready, 2 * (G + 1))
                dve.wait_ge(pow2_ready[j], before(turn, u, j))
                for t in range(T):
                    last = step.done(dve.bn_stats(stats[j][:, t, :], s_sb[j][:, t, :]))
                dve.wait_ge(dve_step, last)
                dve.nop(nofuse=True)
                for t in range(T):
                    last = step.done(dve.bn_aggr(mv[j][:, t, :], stats[j][:, t, :]))
                dve.wait_ge(dve_step, last)
                dve.tensor_scalar(small[j][:, 0, :], mv[j][:, :, 1], LN_EPS, None,
                                  ALU.add).then_inc(ve_ready, 1)

            def normalise(turn, u):
                j, G = u % 2, U * turn + u
                dve.wait_ge(pow_ready, G + 1)
                step.link(dve.tensor_tensor(small[j][:, 2, :], mv[j][:, :, 1], small[j][:, 1, :], ALU.mult))
                step.link(dve.tensor_tensor(small[j][:, 3, :], small[j][:, 2, :], small[j][:, 1, :], ALU.mult))
                dve.tensor_scalar(small[j][:, 4, :], small[j][:, 3, :], LN_EPS / 4, None,
                                  ALU.add).then_inc(v2_ready, 1)
                dve.scalar_tensor_tensor(small[j][:, 6, :], mv[j][:, :, 0], -1.0, small[j][:, 1, :],
                                         ALU.mult, ALU.mult).then_inc(shift_ready, 1)

            def route(turn, u):
                j, G = u % 2, U * turn + u
                dve.wait_ge(x1_ready[j], (before(turn, u, j) + 1) * T)
                for t in range(T):
                    last = step.done(dve.tensor_tensor_reduce(junk[:, j, t, :], x1_sb[j][:, t, :],
                                                              rw_row[:, :], 1.0, 0.0, ALU.mult, ALU.add,
                                                              logit[j][:, t:t + 1]))
                dve.wait_ge(dve_step, last)
                dve.tensor_scalar(W[:, :, :, :].rearrange("p b g t -> p (b g) t")[:, bass.ds(U * turn + u, 1), :].rearrange("p a t -> p (a t)"),
                                  logit[j][:, :], rb_col[:, :], None, ALU.add).then_inc(W_ready, 1)

            def rest_of_x(turn, u):
                j, G = u % 2, U * turn + u
                for c in range(KD):
                    dve.wait_ge(xT_copied[j], before(turn, u, j) * KD + c + 1)
                    if c == 0 and u >= 2:
                        dve.wait_ge(gd_done, 2 * G - 2)
                    dve.tensor_tensor(x_lo[j][:, c, :], ps[:, c, :], x_hi[j][:, c, :].bitcast(F32),
                                      ALU.subtract).then_inc(x_lo_ready[j], 1)

            def rest_of_h(turn, u):
                j = u % 2
                lo = h_parts[j][2 * N:3 * N, :]
                dve.wait_ge(h_hi_ready[j], before(turn, u, j) + 1)
                dve.tensor_tensor(lo, h_sb[j][2 * N:3 * N, :], lo.bitcast(F32), ALU.subtract).then_inc(h_lo_ready[j], 1)

            def groups(turn, more):
                if more:
                    step.enter(turn, U * (3 * T + 2) + 1)
                for u in range(U):
                    statistics(turn, u)
                    if u + 2 < U or more:
                        scan(turn, u + 2)
                    normalise(turn, u)
                    if u + 2 < U or more:
                        rest_of_h(turn, u + 2)
                    if u + 1 < U or more:
                        products(turn, u + 1, 1)
                    if u + 3 < U or more:
                        rest_of_x(turn, u + 3)
                    route(turn, u)
                    if u + 2 < U or more:
                        products(turn, u + 2, 0)
                if more:
                    step.leave(LOOPS - 1)

            dve.wait_ge(router_loaded, 32)
            rest_of_x(0, 0)
            dve.wait_ge(ident_ready, 2)
            step.link(dve.tensor_reduce(is_lo[:, 0:1], ident[0:HROWS, N:2 * N], X, ALU.add))
            step.done(dve.tensor_scalar(is_lo[:, 1:2], is_lo[:, 0:1], -1.0, 1.0, ALU.mult, ALU.add))
            step.link(dve.tensor_tensor(wc_lo[:, :], ps[0:HROWS, 3, 0:D], wc_hi[:, :].bitcast(F32), ALU.subtract))
            step.link(dve.tensor_scalar(wc_lo[:, :], wc_lo[:, :], is_lo[:, 0:1], None, ALU.mult))
            dve.scalar_tensor_tensor(wc[:, :], wc_hi[:, :].bitcast(F32), is_lo[:, 1:2], wc_lo[:, :],
                                     ALU.mult, ALU.add).then_inc(split_ready, 1)
            lo = bias_parts[BIAS_K - 1:BIAS_K, :]
            step.link(dve.tensor_copy(bias_parts[:, :], bias_row[:, :]))
            dve.tensor_tensor(lo, bias_row[BIAS_K - 1:BIAS_K, :], lo.bitcast(F32), ALU.subtract)
            dve.tensor_scalar(ones_k[:, :], ident[0:BIAS_K, :], 0.0, 1.0, ALU.mult, ALU.add).then_inc(const_ready, 1)
            rest_of_x(0, 1)
            for u in range(2):
                scan(0, u)
                rest_of_h(0, u)
                products(0, 0, u)
            rest_of_x(0, 2)
            products(0, 1, 0)
            all_groups(dve, groups)

            dve.wait_ge(W_ready, B * NG)

            def floats(dst, key, m):
                step.link(dve.tensor_scalar(m, key, 31, -1, ALU.arith_shift_right, ALU.bitwise_xor))
                step.link(dve.scalar_tensor_tensor(dst, m, SIGN, key, ALU.bitwise_or, ALU.bitwise_xor))

            Wv = W[:, :, :, :].rearrange("p b g t -> p b (g t)")
            digit_floats = digits[:, 0:1, :]
            floats(cand_m[:, 0:1, :], digit_floats, cand_f[:, 0:1, :])
            step.link(dve.tensor_copy(cand[:, :, :], cand_m[:, 0:1, :].broadcast_to((P, B, CAND))))
            for r in range(ROUNDS):
                if r:
                    step.link(dve.tensor_tensor(cand[:, :, :], digits[:, r:r + 1, :].broadcast_to((P, B, CAND)),
                                                thr[:, :, :].broadcast_to((P, B, CAND)), ALU.bitwise_xor))
                step.link(dve.tensor_tensor(
                    geq[:, :, :, :], W[:, :, :, :].rearrange("p b (o g) t -> p b o (g t)", o=1).broadcast_to(
                        (P, B, CAND, NG * T)),
                    cand[:, :, :].bitcast(F32).rearrange("p b (c o) -> p b c o", o=1).broadcast_to(
                        (P, B, CAND, NG * T)), ALU.is_ge))
                with nc.allow_low_precision("counts to 32"):
                    dve.tensor_reduce(cnt[:, :], geq[:, :, :, :].rearrange("p b c n -> p (b c) n"), X,
                                      ALU.add).then_inc(cnt_ready, 1)
                dve.wait_ge(cnt_sum, r + 1)
                step.link(dve.tensor_scalar(enough[:, :, :].rearrange("p b c -> p (b c)"), ps[:, 0, 0:B * CAND],
                                            float(K), None, ALU.is_ge))
                with nc.allow_low_precision("counts to 15"):
                    step.link(dve.tensor_reduce(found[:, :, 0], enough[:, :, :], X, ALU.add))
                shift = 32 - DIGIT * (r + 1)
                if r == 0:
                    step.link(dve.tensor_scalar(found[:, :, :], found[:, :, :], shift, None, ALU.logical_shift_left))
                    floats(thr[:, :, :], found[:, :, :], cand_m[:, :, 0:1])
                else:
                    step.link(dve.scalar_tensor_tensor(thr[:, :, :], found[:, :, :], shift, thr[:, :, :],
                                                       ALU.logical_shift_left, ALU.bitwise_xor))
            thr_f = thr[:, :, :].bitcast(F32)

            thr_w = thr_f.broadcast_to((P, B, NG * T))
            fl = flags[:, :, :, :, :].rearrange("p k b g t -> p k b (g t)")
            dve.tensor_tensor(fl[:, 0], Wv, thr_w, ALU.is_gt)
            step.link(dve.tensor_tensor(fl[:, 1], Wv, thr_w, ALU.is_equal))
            with nc.allow_low_precision("counts to 4"):
                dve.tensor_reduce(fcnt[:, :, :, :].rearrange("p k b g -> p (k b g)"),
                                  flags[:, :, :, :, :].rearrange("p k b g t -> p (k b g) t"), X,
                                  ALU.add).then_inc(fcnt_ready, 1)
            v = vals[:, :, :, :]
            step.link(dve.tensor_copy(v[:, :, :, 3], Wv))
            step.link(dve.tensor_tensor(w_rest[:, 0], Wv, v[:, :, :, 3], ALU.subtract))
            step.link(dve.tensor_copy(v[:, :, :, 4], w_rest[:, 0]))
            step.link(dve.tensor_tensor(w_rest[:, 1], w_rest[:, 0], v[:, :, :, 4], ALU.subtract))
            step.link(dve.tensor_copy(v[:, :, :, 5], w_rest[:, 1]))
            dve.wait_ge(fcnt_sum, 1)
            step.link(dve.tensor_copy(ftot[:, :, :, :].rearrange("p k b g -> p (k b g)"), ps[:, 2, 0:32]))
            for k in range(2):
                for b in range(B):
                    last = step.done(dve.tensor_tensor_scan(fscan[:, k, b, :], ftot[:, k, b, :], zeros[:, :], 0.0,
                                                            ALU.add, ALU.add))
            dve.wait_ge(dve_step, last)
            last_gt = fscan[:, 0, :, NG - 1:NG]
            step.done(dve.tensor_scalar(room[:, :, :], last_gt, -1.0, float(K - 1), ALU.mult, ALU.add))
            step.link(dve.tensor_tensor(ftot[:, :, :, :], fscan[:, :, :, :], ftot[:, :, :, :], ALU.subtract))
            rk = rank[:, :, :, :, :].rearrange("p k b g t -> p (k b g) t")
            fr = flags[:, :, :, :, :].rearrange("p k b g t -> p (k b g) t")
            step.link(dve.tensor_tensor(rk[:, :, 0], ftot[:, :, :, :].rearrange("p k b g -> p (k b g)"),
                                        ps[:, 1, 0:32], ALU.add))
            for t in range(1, T):
                step.link(dve.tensor_tensor(rk[:, :, t], rk[:, :, t - 1], fr[:, :, t - 1], ALU.add))
            rf = rank[:, :, :, :, :].rearrange("p k b g t -> p k b (g t)")
            room_w = room[:, :, :].broadcast_to((P, B, NG * T))
            step.link(dve.tensor_tensor(sel[:, 0], rf[:, 1], room_w, ALU.is_lt))
            step.link(dve.tensor_tensor(sel[:, 0], sel[:, 0], fl[:, 1], ALU.mult))
            step.link(dve.tensor_tensor(sel[:, 0], sel[:, 0], fl[:, 0], ALU.add))
            step.link(dve.tensor_tensor(sel[:, 1], rf[:, 1], room_w, ALU.min))
            step.link(dve.tensor_tensor(sel[:, 1], sel[:, 1], rf[:, 0], ALU.add))
            step.link(dve.tensor_scalar(sel[:, 2], sel[:, 0], -float(K), float(K), ALU.mult, ALU.add))
            step.link(dve.tensor_tensor(slot_i[:, 0], sel[:, 2], sel[:, 1], ALU.add))
            step.done(dve.tensor_scalar(slot_i[:, 1], slot_i[:, 0], 2, None, ALU.arith_shift_right))
            step.link(dve.tensor_scalar(slot_i[:, 2], slot_i[:, 0], C - 1, None, ALU.bitwise_and))
            step.link(dve.tensor_copy(slot_f[:, :, :, :], slot_i[:, 1:3, :, :]))
            step.link(dve.tensor_tensor(
                at_lo[:, :, :, :].rearrange("p b n c -> p (b n) c"),
                slot_f[:, 1].rearrange("p b (n o) -> p (b n) o", o=1).broadcast_to((P, B * NG * T, C)),
                lo_row[:, :].rearrange("p (o c) -> p o c", o=1).broadcast_to((P, B * NG * T, C)), ALU.is_equal))
            for b in range(B):
                dve.tensor_tensor(
                    lo_vals[:, b],
                    at_lo[:, b].rearrange("p n (c o) -> p n c o", o=1).broadcast_to((P, NG * T, C, VALS)),
                    vals[:, b].rearrange("p (n o) v -> p n o v", o=1).broadcast_to((P, NG * T, C, VALS)),
                    ALU.mult).then_inc(lo_ready, 1)
                dve.tensor_tensor(
                    at_hi[:, b], slot_f[:, 0, b, :].rearrange("p (n o) -> p n o", o=1).broadcast_to((P, NG * T, P)),
                    hi_row[:, :].rearrange("p (o h) -> p o h", o=1).broadcast_to((P, NG * T, P)),
                    ALU.is_equal).then_inc(at_ready[b], 1)
                dve.wait_ge(picked_done, b + 1)
                step.link(dve.tensor_copy(picked[:, b].rearrange("p c v -> p (c v)"), ps[:, 3 + b, 0:C * VALS]))
                pk = picked[:, b]
                step.link(dve.scalar_tensor_tensor(pick_f[:, 0, b], pk[:, :, 0], float(T), pk[:, :, 2],
                                                   ALU.mult, ALU.add))
                step.link(dve.scalar_tensor_tensor(pick_f[:, 1, b], pk[:, :, 1], float(GT), pick_f[:, 0, b],
                                                   ALU.mult, ALU.add))
                dve.tensor_scalar(row_x[:, b, :], pick_f[:, 1, b], float(b * S), None, ALU.add).then_inc(rows_ready, 1)
                step.link(dve.tensor_scalar(pick_f[:, 2, b], pick_f[:, 1, b], float(MS - 1), None, ALU.min))
                dve.tensor_scalar(row_m[:, b, :], pick_f[:, 2, b], float(b * MS), None, ALU.add).then_inc(rows_ready, 1)
                dve.tensor_copy(row_t[:, b, :], pick_f[:, 2, b]).then_inc(rows_ready, 1)
                step.link(dve.tensor_tensor(pick_f[:, 3, b], pk[:, :, 3], pk[:, :, 4], ALU.add))
                step.link(dve.tensor_tensor(w_sel[:, b, :], pick_f[:, 3, b], pk[:, :, 5], ALU.add))
            step.link(dve.tensor_tensor(not_m[:, :, :], w_sel[:, :, :], thr_f.broadcast_to((P, B, C)), ALU.is_le))

            def mean_square(b, sums, out_):
                for c in range(C):
                    last = step.done(dve.tensor_tensor_reduce(
                        rope_a[:, c // 2, (c % 2) * D:(c % 2 + 1) * D], x_sel[b][:, c, :], x_sel[b][:, c, :], 1.0, 0.0, ALU.mult, ALU.add,
                        ms[b][:, sums, c:c + 1]))
                dve.wait_ge(dve_step, last)
                dve.tensor_scalar(ms[b][:, out_, :], ms[b][:, sums, :], 1.0 / D, RMS_EPS, ALU.mult,
                                  ALU.add).then_inc(ms_ready[b], 1)

            def normalised(b, col, n):
                dve.wait_ge(rms_ready[b], n)
                for c in range(C):
                    dve.tensor_scalar(hn[:, c, :], x_sel[b][:, c, :], ms[b][:, col, c:c + 1], None,
                                      ALU.mult).then_inc(hn_ready[b], 1)

            def angles(b):
                tr = trig[b]
                dve.wait_ge(pos_in_s[b], 16 * C)
                step.link(dve.tensor_copy(pos_f[:, b, :], pos_i[:, b, :]))
                step.link(dve.tensor_tensor(
                    tr[:, 0, :, :], pos_f[:, b, :].rearrange("p (c o) -> p c o", o=1).broadcast_to((P, C, HD // 2)),
                    inv_f[:, :].rearrange("p (o k) -> p o k", o=1).broadcast_to((P, C, HD // 2)), ALU.mult))
                step.link(dve.tensor_scalar(tr[:, 1], tr[:, 0], 1.0 / (2 * np.pi), MAGIC, ALU.mult, ALU.add))
                step.link(dve.tensor_scalar(tr[:, 2], tr[:, 1], MAGIC, None, ALU.subtract))
                step.link(dve.scalar_tensor_tensor(tr[:, 1], tr[:, 2], -PI2_A, tr[:, 0], ALU.mult, ALU.add))
                step.link(dve.scalar_tensor_tensor(tr[:, 0], tr[:, 2], -PI2_B, tr[:, 1], ALU.mult, ALU.add))
                step.link(dve.scalar_tensor_tensor(tr[:, 1], tr[:, 2], -PI2_C, tr[:, 0], ALU.mult, ALU.add))
                dve.tensor_scalar(tr[:, 3], tr[:, 1], PI_MAX, -PI_MAX, ALU.min, ALU.max).then_inc(angle_ready[b], 1)

            def value(b, c):
                dve.wait_ge(v_done[b], c + 1)
                dve.tensor_copy(v_sb[b][:, c, :], ps[:, 6 + c % 2, 0:D]).then_inc(v_ready[b], 1)

            def cosines(b):
                tr = trig[b]
                dve.wait_ge(sin_ready[b], 1)
                step.link(dve.tensor_tensor(tr[:, 6], tr[:, 5], tr[:, 5], ALU.mult))
                step.link(dve.tensor_scalar(tr[:, 7], tr[:, 6], -2.0, 1.0, ALU.mult, ALU.add))

            def rope(b, c):
                tr = trig[b]
                hs = lambda ap: ap.rearrange("p (h z k) -> p h z k", z=2, k=HD // 2)
                dve.wait_ge(qk_ready[b], c + 1)
                cos = tr[:, 7, c:c + 1, :].rearrange("p (o z) k -> p o z k", z=1)
                sin = tr[:, 4, c:c + 1, :]
                a, r, q = hs(rope_a[:, c % 2, :]), hs(rope_b[:, c % 2, :]), hs(qk[b][:, c, :])
                if c >= 2:
                    dve.wait_ge(rope_ready[b], c - 1)
                dve.tensor_tensor(a, q, cos.broadcast_to((P, 2 * H, 2, HD // 2)), ALU.mult)
                for z in range(2):
                    last = step.done(dve.tensor_tensor(r[:, :, z], q[:, :, 1 - z],
                                                       sin.broadcast_to((P, 2 * H, HD // 2)), ALU.mult))
                dve.wait_ge(dve_step, last)
                dve.tensor_tensor(q[:, :, 0], a[:, :, 0], r[:, :, 0], ALU.subtract)
                dve.tensor_tensor(q[:, :, 1], a[:, :, 1], r[:, :, 1], ALU.add).then_inc(rope_ready[b], 1)

            def copy_mask():
                for c in range(C):
                    dve.wait_ge(nm_done[0], c + 1)
                    dve.tensor_copy(nmask[0][:, c, :], ps[:, M_BANKS[c], :]).then_inc(nm_ready[0], 1)

            def split(b, beside=None):
                def copy_turned(c):
                    for half in range(2):
                        dve.wait_ge(eT_done[2 + half], c + b * C + 1)
                        dve.tensor_copy(qkT[1][:, 8 * half:8 * half + 8, c * P:(c + 1) * P],
                                        ps[:, :, :].bitcast(BF16)[0:ER, 2 + half, :].rearrange(
                                            "r (h n) -> r h n", h=8)).then_inc(kT_ready, 1)

                dve.wait_ge(rope_ready[b], C)
                for c in range(C):
                    done = c + b * C
                    for n in range(4):
                        if done >= 2:
                            dve.wait_ge(eT_done[n], done - 1)
                    src = qk[b][:, c:c + 1, :].rearrange("p o (m h k) -> p (o m) h k", m=2, h=H)
                    es = e_sb[c % 2]
                    rest = e_rest[:, c % 2, :].rearrange("p (m h k) -> p m h k", m=2, h=H)
                    dve.tensor_copy(es[:, :, :, 0, :], src).then_inc(e_parts, 1)
                    dve.wait_ge(e_parts, 2 * done + 1)
                    step.link(dve.tensor_tensor(rest, src, es[:, :, :, 0, :], ALU.subtract))
                    dve.tensor_copy(es[:, :, :, 3, :], rest).then_inc(e_parts, 1)
                    dve.wait_ge(e_parts, 2 * done + 2)
                    step.done(dve.tensor_tensor(es[:, 0, :, 5, :], rest[:, 0], es[:, 0, :, 3, :], ALU.subtract))
                    dve.tensor_tensor(es[:, 1, :, 4, :], rest[:, 1], es[:, 1, :, 3, :],
                                      ALU.subtract).then_inc(e_ready[0], 1)
                    if b == 0 and c == 1:
                        angles(1)
                    if c:
                        copy_turned(c - 1)
                        if b == 0:
                            beside(c - 1)
                copy_turned(C - 1)
                if b == 0:
                    beside(C - 1)

            def attention(b):
                if b > 0:
                    dve.wait_ge(wo_done[b - 1], C)

                dve.wait_ge(nm_ready[b], C)

                def masked(hg, u):
                    c, h = units[u]
                    n = unit_number(b, hg, u)
                    dve.wait_ge(s_done, n + 1)
                    if not first(b, hg) or u >= 4:
                        dve.wait_ge(pr_ready, n - 3)
                    dve.nop(nofuse=True)
                    dve.tensor_tensor_reduce(sm[u % 4][:, 0:K - 1], ps[:, S_BANKS[u % AHEAD], 0:K - 1],
                                             nmask[b][:, c, 0:K - 1], 1.0, 3.4e38, ALU.add, ALU.min,
                                             nmax[:, c, h:h + 1]).then_inc(sm_ready, 1)

                def inverses(hg, c):
                    turn = hg + b * TURNS
                    dve.wait_ge(pr_ready, turn * UNITS + HG * (c + 1))
                    dve.reciprocal(rinv[:, c, :], rsum[:, c, :]).then_inc(rinv_ready, 1)
                    if not first(b, hg):
                        dve.wait_ge(rT_done, turn * C - C + c + 1)
                    dve.wait_ge(rinv_ready, turn * 2 * C + 2 * c + 1)
                    dve.tensor_copy(rinv_w[:, c, :, :], rinv[:, c, :].rearrange("p (h o) -> p h o", o=1)
                                    .broadcast_to((P, HG, HP))).then_inc(rinv_ready, 1)

                def normalise_heads(hg):
                    turn = hg + b * TURNS
                    dve.wait_ge(rT_done, turn * C + C)
                    dve.wait_ge(oT_ready, turn + 1)
                    dve.tensor_tensor(onT[:, bass.ds(hg, 1), :].rearrange("p o n -> p (o n)"), oT[:, :], ps[:, 5, :],
                                      ALU.mult).then_inc(onT_ready, 1)

                def late(hg, u):
                    if (u - 3) % 2 and 0 <= u - 3 < UNITS:
                        copy_probs(dve, dve.tensor_copy, b, hg, u - 3)
                    if (u - 5) % HG == 0 and 0 <= (u - 5) // HG < C:
                        inverses(hg, (u - 5) // HG)
                    if u == UNITS + 9:
                        normalise_heads(hg)

                def turn_body(hg):
                    for u in range(UNITS):
                        masked(hg, u)
                        late(hg, u)
                        if not hg_is(hg, 0):
                            late(hg - 1, u + UNITS)
                    if hg_is(hg, TURNS - 1):
                        for u in range(UNITS, 2 * UNITS):
                            late(hg, u)

                all_turns(dve, turn_body)

            def residual(b):
                for c in range(C):
                    dve.wait_ge(wo_done[b], c + 1)
                    last = step.done(dve.tensor_tensor(x_sel[b][:, c, :], x_sel[b][:, c, :],
                                                       ps[:, O_BANKS[c], 0:D], ALU.add))
                dve.wait_ge(dve_step, last)

            def add_second(b, cs):
                for c in cs:
                    dve.wait_ge(w2_done[b], c + 1 if b == B - 1 else c // 2 * 2 + 2)
                    dve.tensor_tensor(x_sel[b][:, c, :], x_sel[b][:, c, :], second_out(b, c),
                                      ALU.add).then_inc(x2_ready[b], 1)

            def finish(b, part, cs):
                dve.wait_ge(x2_ready[b], cs[-1] + 1)
                for c in cs:
                    last = step.done(dve.scalar_tensor_tensor(keep[b][:, c, :], x_sel[b][:, c, :], w_sel[:, b, c:c + 1],
                                                              keep[b][:, c, :], ALU.mult, ALU.add))
                dve.wait_ge(dve_step, last)
                for c in cs:
                    last = step.done(dve.bn_stats(stat2[:, c, :], keep[b][:, c, :]))
                dve.wait_ge(dve_step, last)
                for c in cs:
                    last = step.done(dve.bn_aggr(mv2[:, c, :], stat2[:, c, :]))
                dve.wait_ge(dve_step, last)
                dve.tensor_scalar(ms[b][:, 1, cs[0]:cs[-1] + 1], mv2[:, cs[0]:cs[-1] + 1, 1], LN_EPS, None,
                                  ALU.add).then_inc(ve2_ready[b], 1)
                dve.wait_ge(pow3_ready[b], part + 1)
                for c in cs:
                    dve.tensor_scalar(x_sel[b][:, c, :], keep[b][:, c, :], mv2[:, c, 0:1], ms[b][:, 2, c:c + 1],
                                      ALU.subtract, ALU.mult).then_inc(fin_ready[b], 1)

            def kept(b):
                dve.wait_ge(ob_stored[b], 16 * B * NG // 2)
                for c in range(C):
                    last = step.done(dve.scalar_tensor_tensor(keep[b][:, c, :], x_sel[b][:, c, :], not_m[:, b, c:c + 1],
                                                              x_sel[b][:, c, :], ALU.mult, ALU.add))

            dve.wait_ge(x_sel_in[0], 16 * C)
            mean_square(0, 0, 1)
            normalised(0, 2, 1)
            angles(0)
            dve.wait_ge(x_sel_in[1], 16 * C)
            mean_square(1, 0, 1)
            dve.wait_ge(hnT_done[0], KD)
            normalised(1, 2, 1)
            dve.wait_ge(ms_ready[1], 1)
            cosines(0)
            for c in range(C):
                value(0, c)
                rope(0, c)
            for b in range(B):
                kept(b)
            split(0, lambda c: value(1, c))
            copy_mask()
            for b in range(B):
                attention(b)
                residual(b)
                mean_square(b, 3, 4)
                normalised(b, 5, 2)
                if b < B - 1:
                    cosines(b + 1)
                    for c in range(C):
                        rope(b + 1, c)
                    split(b + 1)
                    add_second(b, range(C))
            for part, cs in enumerate(PARTS[0]):
                finish(0, part, cs)
            for part, cs in enumerate(PARTS[1]):
                add_second(1, cs)
                finish(1, part, cs)


_INS = ['L0_attn_x', 'L0_attn_WA', 'L0_attn_WB', 'L0_attn_WC', 'L0_attn_WD', 'L0_attn_bD', 'L0_attn_Wg', 'L0_attn_bg',
        'L0_ffn_attention_mask', 'L0_ffn_position_ids', 'L0_ffn_router_w', 'L0_ffn_router_b', 'L0_ffn_wq', 'L0_ffn_wk',
        'L0_ffn_wv', 'L0_ffn_wo', 'L0_ffn_w1', 'L0_ffn_w2', 'L0_ffn_ln1', 'L0_ffn_ln2']


def kernel(**inputs):
    import concourse.bacc as bacc
    from concourse.bass_utils import run_bass_kernel_spmd

    nc = bacc.Bacc("TRN2", target_bir_lowering=False, num_devices=1)
    arrays, args = {}, []
    for name in _INS:
        a = np.ascontiguousarray(inputs[name])
        arrays[f"in_{name}"] = a
        args.append(nc.dram_tensor(f"in_{name}", a.shape, mybir.dt.from_np(a.dtype), kind="ExternalInput").ap())
    out = nc.dram_tensor("out", (B, S, D), F32, kind="ExternalOutput").ap()
    build(nc, *args, out)
    r = run_bass_kernel_spmd(nc, [arrays], core_ids=[0])
    return r.results[0]["out"]
```
